# Optimizing a Trainium2 kernel written in Bass

```python
import numpy as np
import jax
import jax.numpy as jnp

def _softmax(x, axis=-1):
    return jax.nn.softmax(x, axis=axis)

def _gelu(x):
    return jax.nn.gelu(x, approximate=True)

def _silu(x):
    return jax.nn.silu(x)

def _sigmoid(x):
    return jax.nn.sigmoid(x)

def _layernorm(x, axis=-1, eps=1e-05):
    m = jnp.mean(x, axis=axis, keepdims=True)
    v = jnp.var(x, axis=axis, keepdims=True)
    return (x - m) / jnp.sqrt(v + eps)

def _scatter_add(tgt, idx, src, axis=0):
    return tgt.at[idx].add(src)

def _segment_sum(src, seg, n):
    return jax.ops.segment_sum(src, seg, n)
kernel_name = 'mk_decoder_postln_d1_seqx_r4_b73005'

def setup_inputs(seed: int=0):
    np.random.seed(seed)
    _w = jnp.asarray

    def _rec_inputs():
        import jax
        import jax.numpy as jnp
        _rk = jax.random.key(seed)
        x = 7.22e-05 + 1 * jax.random.normal(jax.random.fold_in(_rk, 1), (8, 256, 256), jnp.float32)
        _lenS = 256 - jax.random.randint(jax.random.fold_in(_rk, 7), (8,), 0, max(1, 256 // 4) + 1, jnp.int32)
        _lenS2 = 77 - jax.random.randint(jax.random.fold_in(_rk, 8), (8,), 0, max(1, 77 // 4) + 1, jnp.int32)
        _ctx_1024P = jax.random.normal(jax.random.fold_in(_rk, 11), (8, 16, 256), jnp.float32)
        _ctx_1024c = jax.random.dirichlet(jax.random.fold_in(_rk, 511), 0.3 * jnp.ones((16,), jnp.float32), (8, 77))
        _ctx_1024t = jnp.einsum('bsk,bkd->bsd', _ctx_1024c, _ctx_1024P)
        _ctx_1024t = _ctx_1024t * jax.lax.rsqrt(jnp.mean(jnp.square(_ctx_1024t)) + 1e-12) * 0.953939
        ctx_1024 = 4.13588e-05 + 0.999923 * (_ctx_1024t + 0.3 * jax.random.normal(jax.random.fold_in(_rk, 611), (8, 77, 256), jnp.float32))
        _validS = jnp.arange(256)[None, :] < _lenS[:, None]
        _validS2 = jnp.arange(77)[None, :] < _lenS2[:, None]
        _causal = jnp.tril(jnp.ones((256, 256), dtype=bool))
        mask_1x1xSxS2_if1 = jnp.where(jnp.ones((1, 1, 256, 77), dtype=bool), 1, 0).astype(jnp.int32)
        return (x, ctx_1024, mask_1x1xSxS2_if1)
    x, ctx_1024, mask_1x1xSxS2_if1 = _rec_inputs()

    def _L0_attn_setup():
        import jax, jax.numpy as jnp
        import numpy as np
        HEADS = 4
        GATE_NORM = 16.0
        EPS = 1e-08

        def rmsnorm(x, w):
            return x * jax.lax.rsqrt(jnp.mean(jnp.square(x), axis=-1, keepdims=True) + EPS) * w

        def act_quant(x):
            scale = 127.0 / jnp.clip(jnp.max(jnp.abs(x), axis=-1, keepdims=True), 1e-05)
            return jnp.clip(jnp.round(x * scale), -128.0, 127.0) / scale

        def weight_quant(w):
            scale = 1.0 / jnp.clip(jnp.mean(jnp.abs(w)), 1e-05)
            return jnp.clip(jnp.round(w * scale), -1.0, 1.0) / scale

        def bitlinear(x, norm_w, w, b=None):
            xn = rmsnorm(x, norm_w)
            xq = xn + jax.lax.stop_gradient(act_quant(xn) - xn)
            wq = w + jax.lax.stop_gradient(weight_quant(w) - w)
            y = xq @ wq.T
            return y if b is None else y + b

        def split_heads(x):
            B, L, HD = x.shape
            return x.reshape(B, L, HEADS, HD // HEADS).transpose(0, 2, 1, 3)

        def gla_scan(q, k, v, gk):
            B, H, L, Dk = q.shape
            Dv = v.shape[-1]
            q = q * Dk ** (-0.5)

            def step(S, inp):
                qt, kt, vt, gt = inp
                S = jnp.exp(gt)[..., None] * S + kt[..., None] * vt[..., None, :]
                o = jnp.einsum('bhk,bhkv->bhv', qt, S)
                return (S, o)
            S0 = jnp.zeros((B, H, Dk, Dv), dtype=q.dtype)
            xs = tuple((t.transpose(2, 0, 1, 3) for t in (q, k, v, gk)))
            _, o = jax.lax.scan(step, S0, xs)
            return o.transpose(1, 2, 0, 3)
        key = jax.random.key(seed)
        ks = jax.random.split(key, 12)
        D, Dk, Dv, R = (256, 256, 512, 16)
        B, L = (2, 512)
        s = 0.02
        return {'hidden_states': jax.random.normal(ks[0], (B, L, D), jnp.float32), 'wq': jax.random.normal(ks[1], (Dk, D), jnp.float32) * s, 'nq': jnp.ones((D,), jnp.float32), 'wk': jax.random.normal(ks[2], (Dk, D), jnp.float32) * s, 'nk': jnp.ones((D,), jnp.float32), 'wv': jax.random.normal(ks[3], (Dv, D), jnp.float32) * s, 'nv': jnp.ones((D,), jnp.float32), 'wg': jax.random.normal(ks[4], (Dv, D), jnp.float32) * s, 'ng': jnp.ones((D,), jnp.float32), 'wgk1': jax.random.normal(ks[5], (R, D), jnp.float32) * s, 'ngk1': jnp.ones((D,), jnp.float32), 'wgk2': jax.random.normal(ks[6], (Dk, R), jnp.float32) * s, 'bgk2': jnp.zeros((Dk,), jnp.float32), 'ngk2': jnp.ones((R,), jnp.float32), 'wo': jax.random.normal(ks[7], (D, Dv), jnp.float32) * s, 'no': jnp.ones((Dv,), jnp.float32)}
    _L0_attn_all = _L0_attn_setup()
    _L0_attn_in = {k: v for k, v in _L0_attn_all.items() if k in ('wq', 'nq', 'wk', 'nk', 'wv', 'nv', 'wg', 'ng', 'wgk1', 'ngk1', 'wgk2', 'bgk2', 'ngk2', 'wo', 'no')}
    del _L0_attn_all

    def _L0_xattn_setup():
        import jax, jax.numpy as jnp
        import numpy as np
        D_MODEL = 256
        N_HEADS = 16
        D_K = D_MODEL // N_HEADS
        B, S = (4, 512)
        key = jax.random.key(seed)
        ks = jax.random.split(key, 12)
        sc = 1.0 / np.sqrt(D_MODEL)
        inp = {'query': jax.random.normal(ks[0], (B, S, D_MODEL), jnp.float32), 'key': jax.random.normal(ks[1], (B, S, D_MODEL), jnp.float32), 'value': jax.random.normal(ks[2], (B, S, D_MODEL), jnp.float32), 'mask': jnp.ones((1, 1, S, S), jnp.int32), 'W_q': jax.random.normal(ks[3], (D_MODEL, D_MODEL), jnp.float32) * sc, 'b_q': jnp.zeros((D_MODEL,), jnp.float32), 'W_k': jax.random.normal(ks[4], (D_MODEL, D_MODEL), jnp.float32) * sc, 'b_k': jnp.zeros((D_MODEL,), jnp.float32), 'W_v': jax.random.normal(ks[5], (D_MODEL, D_MODEL), jnp.float32) * sc, 'b_v': jnp.zeros((D_MODEL,), jnp.float32), 'W_o': jax.random.normal(ks[6], (D_MODEL, D_MODEL), jnp.float32) * sc, 'b_o': jnp.zeros((D_MODEL,), jnp.float32)}
        return inp
    _L0_xattn_all = _L0_xattn_setup()
    _L0_xattn_in = {k: v for k, v in _L0_xattn_all.items() if k in ('W_q', 'b_q', 'W_k', 'b_k', 'W_v', 'b_v', 'W_o', 'b_o')}
    del _L0_xattn_all

    def _L0_ffn_setup():
        import jax, jax.numpy as jnp
        import numpy as np
        DIM = 256
        INTER = 512
        E = 8
        TOPK = 2
        ROUTE_SCALE = 1.0

        def _mlp(x, w1, w2, w3):
            h = jax.nn.silu(x @ w1.T) * (x @ w3.T)
            return h @ w2.T
        key = jax.random.key(seed)
        ks = jax.random.split(key, 10)
        s_in = 0.02
        return {'x': jax.random.normal(ks[0], (4, 512, DIM), dtype=jnp.float32), 'gate_w': jax.random.normal(ks[1], (E, DIM), dtype=jnp.float32) * s_in, 'gate_bias': jax.random.normal(ks[2], (E,), dtype=jnp.float32) * 0.01, 'w1': jax.random.normal(ks[3], (E, INTER, DIM), dtype=jnp.float32) * s_in, 'w2': jax.random.normal(ks[4], (E, DIM, INTER), dtype=jnp.float32) * s_in, 'w3': jax.random.normal(ks[5], (E, INTER, DIM), dtype=jnp.float32) * s_in, 'sw1': jax.random.normal(ks[6], (INTER, DIM), dtype=jnp.float32) * s_in, 'sw2': jax.random.normal(ks[7], (DIM, INTER), dtype=jnp.float32) * s_in, 'sw3': jax.random.normal(ks[8], (INTER, DIM), dtype=jnp.float32) * s_in}
    _L0_ffn_all = _L0_ffn_setup()
    _L0_ffn_in = {k: v for k, v in _L0_ffn_all.items() if k in ('gate_w', 'gate_bias', 'w1', 'w2', 'w3', 'sw1', 'sw2', 'sw3')}
    del _L0_ffn_all
    return {'x': x, 'ctx_1024': ctx_1024, 'mask_1x1xSxS2_if1': mask_1x1xSxS2_if1, 'L0_attn_wq': _L0_attn_in['wq'], 'L0_attn_nq': _L0_attn_in['nq'], 'L0_attn_wk': _L0_attn_in['wk'], 'L0_attn_nk': _L0_attn_in['nk'], 'L0_attn_wv': _L0_attn_in['wv'], 'L0_attn_nv': _L0_attn_in['nv'], 'L0_attn_wg': _L0_attn_in['wg'], 'L0_attn_ng': _L0_attn_in['ng'], 'L0_attn_wgk1': _L0_attn_in['wgk1'], 'L0_attn_ngk1': _L0_attn_in['ngk1'], 'L0_attn_wgk2': _L0_attn_in['wgk2'], 'L0_attn_bgk2': _L0_attn_in['bgk2'], 'L0_attn_ngk2': _L0_attn_in['ngk2'], 'L0_attn_wo': _L0_attn_in['wo'], 'L0_attn_no': _L0_attn_in['no'], 'L0_xattn_W_q': _L0_xattn_in['W_q'], 'L0_xattn_b_q': _L0_xattn_in['b_q'], 'L0_xattn_W_k': _L0_xattn_in['W_k'], 'L0_xattn_b_k': _L0_xattn_in['b_k'], 'L0_xattn_W_v': _L0_xattn_in['W_v'], 'L0_xattn_b_v': _L0_xattn_in['b_v'], 'L0_xattn_W_o': _L0_xattn_in['W_o'], 'L0_xattn_b_o': _L0_xattn_in['b_o'], 'L0_ffn_gate_w': _L0_ffn_in['gate_w'], 'L0_ffn_gate_bias': _L0_ffn_in['gate_bias'], 'L0_ffn_w1': _L0_ffn_in['w1'], 'L0_ffn_w2': _L0_ffn_in['w2'], 'L0_ffn_w3': _L0_ffn_in['w3'], 'L0_ffn_sw1': _L0_ffn_in['sw1'], 'L0_ffn_sw2': _L0_ffn_in['sw2'], 'L0_ffn_sw3': _L0_ffn_in['sw3']}

def reference(x, ctx_1024, mask_1x1xSxS2_if1, L0_attn_wq, L0_attn_nq, L0_attn_wk, L0_attn_nk, L0_attn_wv, L0_attn_nv, L0_attn_wg, L0_attn_ng, L0_attn_wgk1, L0_attn_ngk1, L0_attn_wgk2, L0_attn_bgk2, L0_attn_ngk2, L0_attn_wo, L0_attn_no, L0_xattn_W_q, L0_xattn_b_q, L0_xattn_W_k, L0_xattn_b_k, L0_xattn_W_v, L0_xattn_b_v, L0_xattn_W_o, L0_xattn_b_o, L0_ffn_gate_w, L0_ffn_gate_bias, L0_ffn_w1, L0_ffn_w2, L0_ffn_w3, L0_ffn_sw1, L0_ffn_sw2, L0_ffn_sw3):
    import jax
    import jax.numpy as jnp

    def _L0_attn_ref(hidden_states, wq, nq, wk, nk, wv, nv, wg, ng, wgk1, ngk1, wgk2, bgk2, ngk2, wo, no):
        import jax, jax.numpy as jnp
        import numpy as np
        HEADS = 4
        GATE_NORM = 16.0
        EPS = 1e-08

        def rmsnorm(x, w):
            return x * jax.lax.rsqrt(jnp.mean(jnp.square(x), axis=-1, keepdims=True) + EPS) * w

        def act_quant(x):
            scale = 127.0 / jnp.clip(jnp.max(jnp.abs(x), axis=-1, keepdims=True), 1e-05)
            return jnp.clip(jnp.round(x * scale), -128.0, 127.0) / scale

        def weight_quant(w):
            scale = 1.0 / jnp.clip(jnp.mean(jnp.abs(w)), 1e-05)
            return jnp.clip(jnp.round(w * scale), -1.0, 1.0) / scale

        def bitlinear(x, norm_w, w, b=None):
            xn = rmsnorm(x, norm_w)
            xq = xn + jax.lax.stop_gradient(act_quant(xn) - xn)
            wq = w + jax.lax.stop_gradient(weight_quant(w) - w)
            y = xq @ wq.T
            return y if b is None else y + b

        def split_heads(x):
            B, L, HD = x.shape
            return x.reshape(B, L, HEADS, HD // HEADS).transpose(0, 2, 1, 3)

        def gla_scan(q, k, v, gk):
            B, H, L, Dk = q.shape
            Dv = v.shape[-1]
            q = q * Dk ** (-0.5)

            def step(S, inp):
                qt, kt, vt, gt = inp
                S = jnp.exp(gt)[..., None] * S + kt[..., None] * vt[..., None, :]
                o = jnp.einsum('bhk,bhkv->bhv', qt, S)
                return (S, o)
            S0 = jnp.zeros((B, H, Dk, Dv), dtype=q.dtype)
            xs = tuple((t.transpose(2, 0, 1, 3) for t in (q, k, v, gk)))
            _, o = jax.lax.scan(step, S0, xs)
            return o.transpose(1, 2, 0, 3)
        x = hidden_states
        q = split_heads(bitlinear(x, nq, wq))
        k = split_heads(bitlinear(x, nk, wk))
        v = split_heads(bitlinear(x, nv, wv))
        gk = bitlinear(bitlinear(x, ngk1, wgk1), ngk2, wgk2, bgk2)
        gk = split_heads(jax.nn.log_sigmoid(gk) / GATE_NORM)
        o = gla_scan(q, k, v, gk)
        B, H, L, Dvh = o.shape
        o = o.transpose(0, 2, 1, 3).reshape(B, L, H * Dvh)
        g = bitlinear(x, ng, wg)
        o = o * jax.nn.silu(g)
        return bitlinear(o, no, wo)

    def _L0_xattn_ref(query, key, value, mask, W_q, b_q, W_k, b_k, W_v, b_v, W_o, b_o):
        import jax, jax.numpy as jnp
        import numpy as np
        D_MODEL = 256
        N_HEADS = 16
        D_K = D_MODEL // N_HEADS
        B, S = (4, 512)
        b = query.shape[0]

        def proj(x, W, bias):
            y = jnp.einsum('bsd,ed->bse', x, W) + bias
            return y.reshape(b, -1, N_HEADS, D_K).transpose(0, 2, 1, 3)
        Q = proj(query, W_q, b_q)
        K = proj(key, W_k, b_k)
        V = proj(value, W_v, b_v)
        scores = jnp.einsum('bhqd,bhkd->bhqk', Q, K) / np.sqrt(D_K)
        scores = jnp.where(mask == 0, jnp.float32(-1000000000.0), scores)
        attn = jax.nn.softmax(scores, axis=-1)
        ctx = jnp.einsum('bhqk,bhkd->bhqd', attn, V)
        ctx = ctx.transpose(0, 2, 1, 3).reshape(b, -1, D_MODEL)
        return jnp.einsum('bsd,ed->bse', ctx, W_o) + b_o

    def _L0_ffn_ref(x, gate_w, gate_bias, w1, w2, w3, sw1, sw2, sw3):
        import jax, jax.numpy as jnp
        import numpy as np
        DIM = 256
        INTER = 512
        E = 8
        TOPK = 2
        ROUTE_SCALE = 1.0

        def _mlp(x, w1, w2, w3):
            h = jax.nn.silu(x @ w1.T) * (x @ w3.T)
            return h @ w2.T
        shape = x.shape
        xt = x.reshape(-1, DIM)
        T = xt.shape[0]
        logits = xt @ gate_w.T
        scores = jax.nn.softmax(logits.astype(jnp.float32), axis=-1)
        original_scores = scores
        biased = scores + gate_bias
        _, indices = jax.lax.top_k(biased, TOPK)
        weights = jnp.take_along_axis(original_scores, indices, axis=1)
        weights = (weights * ROUTE_SCALE).astype(x.dtype)
        combine = (jax.nn.one_hot(indices, E, dtype=weights.dtype) * weights[..., None]).sum(axis=1)
        y = jnp.zeros_like(xt)
        for e in range(E):
            y = y + _mlp(xt, w1[e], w2[e], w3[e]) * combine[:, e:e + 1]
        z = _mlp(xt, sw1, sw2, sw3)
        return (y + z).reshape(shape)
    x = _layernorm(x + _L0_attn_ref(x, L0_attn_wq, L0_attn_nq, L0_attn_wk, L0_attn_nk, L0_attn_wv, L0_attn_nv, L0_attn_wg, L0_attn_ng, L0_attn_wgk1, L0_attn_ngk1, L0_attn_wgk2, L0_attn_bgk2, L0_attn_ngk2, L0_attn_wo, L0_attn_no), axis=-1)
    x = _layernorm(x + _L0_xattn_ref(x, ctx_1024, ctx_1024, mask_1x1xSxS2_if1, L0_xattn_W_q, L0_xattn_b_q, L0_xattn_W_k, L0_xattn_b_k, L0_xattn_W_v, L0_xattn_b_v, L0_xattn_W_o, L0_xattn_b_o), axis=-1)
    x = _layernorm(x + _L0_ffn_ref(x, L0_ffn_gate_w, L0_ffn_gate_bias, L0_ffn_w1, L0_ffn_w2, L0_ffn_w3, L0_ffn_sw1, L0_ffn_sw2, L0_ffn_sw3), axis=-1)
    return x

_drawn_inputs = setup_inputs


def setup_inputs(seed=0):
    import zlib

    import numpy as np

    out = dict(_drawn_inputs(seed))
    spreads = {'L0_attn_nq': (1.0, 0.2),
     'L0_attn_nk': (1.0, 0.2),
     'L0_attn_nv': (1.0, 0.2),
     'L0_attn_ng': (1.0, 0.2),
     'L0_attn_ngk1': (1.0, 0.6),
     'L0_attn_bgk2': (0.0, 0.583),
     'L0_attn_ngk2': (1.0, 0.6),
     'L0_attn_no': (1.0, 0.2),
     'L0_xattn_b_q': (0.0, 0.373),
     'L0_xattn_b_k': (0.0, 2.0),
     'L0_xattn_b_v': (0.0, 0.1),
     'L0_xattn_b_o': (0.0, 0.1)}
    factors = {'L0_attn_wgk1': 8.0,
     'L0_attn_wgk2': 8.0,
     'L0_ffn_gate_w': 8.0,
     'L0_ffn_gate_bias': 8.0,
     'L0_ffn_w1': 8.0,
     'L0_ffn_w2': 8.0,
     'L0_ffn_w3': 8.0,
     'L0_ffn_sw1': 8.0,
     'L0_ffn_sw2': 8.0,
     'L0_ffn_sw3': 8.0}
    for name, (base, spread) in spreads.items():
        noise = np.random.default_rng([zlib.crc32(name.encode()), seed]).standard_normal(out[name].shape)
        drawn = base * np.exp(spread * noise) if base else spread * noise
        out[name] = jnp.asarray(drawn.astype(out[name].dtype))
    for name, factor in factors.items():
        out[name] = (out[name] * factor).astype(out[name].dtype)
    return out
```

```python
from contextlib import ExitStack

import numpy as np

import concourse.bass as bass
from concourse import mybir

F32 = mybir.dt.float32
BF16 = mybir.dt.bfloat16
I32 = mybir.dt.int32
ALU = mybir.AluOpType
ACT = mybir.ActivationFunctionType
AX = mybir.AxisListType

P = 128
ROUND = 12582912.0
LEVELS = [1, 2, 4, 8, 16, 32, 64]


class Lane:

    def __init__(self, sem):
        self.sem, self.count, self.queue, self.met = sem, 0, [], {}

    def wait(self, *marks):
        for m in marks:
            if m is None:
                continue
            sem, value = m
            if value > self.met.get(sem.num, 0):
                self.met[sem.num] = value
                self.queue.append(lambda e, sem=sem, value=value: e.wait_ge(sem, value))

    def do(self, make, after=(), signal=True):
        self.wait(*after)
        if not signal:
            self.queue.append(make)
            return None
        self.count += 1
        self.queue.append(lambda e: make(e).then_inc(self.sem, 1))
        return (self.sem, self.count)

    def dma(self, make, sem, after=()):
        self.wait(*after)
        self.queue.append(lambda e: make(e).then_inc(sem, 16))

    def last(self):
        return (self.sem, self.count) if self.count else None


class Ring:

    def __init__(self, bufs):
        self.bufs, self.marks, self.released = bufs, [()] * len(bufs), -1

    def buf(self, i):
        return self.bufs[i % len(self.bufs)]

    def free(self, i):
        assert i < len(self.bufs) or self.released >= i - len(self.bufs), "taken before its readers are known"
        return self.marks[i % len(self.bufs)]

    def release(self, i, *marks):
        self.marks[i % len(self.bufs)], self.released = marks, i


def decoder_layer(nc, t, out):
    B, L, D = t["x"].shape
    NT = L // P
    TILES = B * NT
    DC = D // P
    DV = t["wvT"].shape[1]
    VC = DV // P
    R = t["wgk1T"].shape[1]
    HEADS = 4
    DK = D // HEADS
    DVH = DV // HEADS
    S2 = t["ctxT"].shape[1] // B
    XH = 16
    XD = D // XH
    HB = XH // 4
    E, F = t["w1T"].shape[0], t["w1T"].shape[2]
    FC = F // P
    NORMS = 5
    JQ, JK, JV, JR, JG = range(NORMS)
    assert DK == 64 and NT == 2 and DC == 2 and HB * S2 <= 512

    with ExitStack() as ctx:
        def sb(name, shape, dt=F32):
            return ctx.enter_context(nc.sbuf_tensor(name, shape, dt))

        wide = sb("wide", [P, 19968])
        late = sb("late", [P, 4512])
        place = {"attention": [wide, 0], "experts": [wide, 0], "prepare": [late, 0], "masks": [wide, wide.shape[1] - 6 * P], "cross": [late, 0]}

        def carve(phase, shape, dt=F32):
            words = int(np.prod(shape[1:])) * (2 if dt == BF16 else 4) // 4
            area, a = place[phase]
            place[phase][1] += words
            assert a + words <= area.shape[1], (phase, a + words)
            v = area[0:shape[0], a:a + words]
            v = v.bitcast(dt) if dt != F32 else v
            names = "abcd"[:len(shape) - 1]
            if len(shape) > 2:
                v = v.rearrange(f"p ({' '.join(names)}) -> p {' '.join(names)}", **dict(zip(names, shape[1:])))
            return v

        def sem(name):
            return ctx.enter_context(nc.semaphore(name))

        pe, act, dve, pool, sp = (Lane(sem(f"{n}_done")) for n in ("pe", "act", "dve", "pool", "sp"))
        loads = {}

        def load(dst, src, name, lane=None):
            if name not in loads:
                loads[name] = [sem(f"ld_{name}"), 0]
            loads[name][1] += 16
            (lane or sp).dma(lambda e: e.dma_start(dst, src), loads[name][0])

        def loaded(name):
            return tuple(loads[name])

        def bcast(ap, n):
            a = ap.unsqueeze(1)
            return a.to_broadcast([a.shape[0], n] + list(a.shape[2:]))

        banks = [ctx.enter_context(nc.psum_tensor(f"bank{i}", [P, 512], F32)) for i in range(8)]
        work = Ring(banks[4:8])
        work_n = [0]

        def take():
            i = work_n[0]
            work_n[0] += 1
            return i, work.buf(i), work.free(i)

        x = sb("x", [P, TILES, D])
        ident = sb("ident", [P, P])
        ident_bf = sb("ident_bf", [P, P], BF16)
        ones = sb("ones", [P, P])
        level_mask = sb("level_mask", [P, 6, P], mybir.dt.int8)
        level_mask_raw = carve("masks", [P, 6, P], I32)
        norm_w = sb("norm_w", [P, NORMS, D])
        no_w = sb("no_w", [P, DV])
        ngk2_w = sb("ngk2_w", [P, R])
        bgk2 = sb("bgk2", [P, DC])
        w_raw = carve("prepare", [P, DC * (2 * D + R + 2 * DV) + VC * D])
        w_int = sb("w_int", [P, DC * (2 * D + R + 2 * DV) + VC * D], BF16)
        wgk2_raw = sb("wgk2_raw", [R, D])
        wgk2_int = sb("wgk2_int", [R, D])
        inv_count = sb("inv_count", [P, 7])
        unit = sb("unit", [P, 7])
        w_sums = sb("w_sums", [P, 7])
        w_mean = sb("w_mean", [P, 7])
        w_scale = sb("w_scale", [P, 7])
        w_unit = sb("w_unit", [P, 7])

        load(ident[:], t["ident"], "const")
        load(inv_count[:], t["inv_count"].partition_broadcast(P), "const")
        load(unit[:], t["unit"].partition_broadcast(P), "const")
        col, at = {}, 0
        for name, chunks, width in (("wqT", DC, D), ("wkT", DC, D), ("wvT", DC, DV), ("wgk1T", DC, R), ("wgT", DC, DV), ("woT", VC, D)):
            col[name] = (at, chunks, width)
            load(w_raw[:, at:at + chunks * width].rearrange("p (c n) -> p c n", c=chunks),
                 t[name].rearrange("(c p) n -> p c n", p=P), "w_bit", act)
            at += chunks * width
        load(wgk2_raw[:], t["wgk2T"], "w_bit", act)
        load(norm_w[:], t["norm_w"].partition_broadcast(P), "norm")
        for b in range(B):
            load(x[:, b * NT:(b + 1) * NT, :], t["x"][b].rearrange("(i p) d -> p i d", p=P), f"x{b}")
            if b == 0:
                load(level_mask_raw, t["level_mask"], "masks")
                load(no_w[:], t["no_w"].partition_broadcast(P), "attn")
                load(ngk2_w[:], t["ngk2"].partition_broadcast(P), "attn")
                load(bgk2[:], t["bgk2"], "attn")

        xw_T = {n: sb(n, [P, DC, D]) for n in ("xWqT", "xWkT", "xWvT", "xWoT")}
        ctxT = sb("ctxT", [P, DC, B * S2])
        xbq = sb("xbq", [P, DC])
        xbk = sb("xbk", [P, DC])
        xbv = sb("xbv", [P, D])
        xbo = sb("xbo", [P, D])
        head_mask = sb("head_mask", [P, XH // DC])
        mask_raw = sb("mask_raw", [P, NT, S2], I32)
        keep = sb("keep", [P, NT, S2])
        drop = sb("drop", [P, NT, S2])
        for n in xw_T:
            load(xw_T[n][:], t[n].rearrange("(c p) n -> p c n", p=P), "cross")
        load(ctxT[:], t["ctxT"].rearrange("(c p) n -> p c n", p=P), "cross")
        load(xbq[:], t["xbq"], "cross")
        load(xbk[:], t["xbk"], "cross")
        load(xbv[:], t["xbv"].partition_broadcast(P), "cross")
        load(xbo[:], t["xbo"].partition_broadcast(P), "cross")
        load(head_mask[:], t["head_mask"], "cross")
        load(mask_raw[:], t["mask"].rearrange("a c (i p) k -> p (a c i) k", p=P), "cross")

        ones_ok = dve.do(lambda e: e.memset(ones[:], 1.0))
        dve.do(lambda e: e.memset(w_sums[:], 0.0))
        sums_zero = dve.last()
        mask_ok = dve.do(lambda e: e.tensor_copy(level_mask[:], level_mask_raw), after=[loaded("masks")])
        ident_ok = act.do(lambda e: e.activation(ident_bf[:], ident[:], ACT.Copy), after=[loaded("const")])
        order = ["wqT", "wkT", "wvT", "wgk1T", "wgT", "woT"]

        def raw(name, buf):
            a, c, w = col[name]
            return buf[:, a:a + c * w]

        for j, n in enumerate(order):
            dve.do(lambda e, j=j, n=n: e.tensor_reduce(w_sums[:, j:j + 1], raw(n, w_raw), AX.X, ALU.add,
                                                       apply_absolute_value=True),
                   after=[loaded("w_bit"), sums_zero])
        sums = dve.do(lambda e: e.tensor_reduce(w_sums[0:R, 6:7], wgk2_raw[:], AX.X, ALU.add, apply_absolute_value=True))
        i, bank, free = take()
        total = pe.do(lambda e, bank=bank: e.matmul(bank[:, 0:7], ones[:], w_sums[:], start=True, stop=True),
                      after=[*free, sums, ones_ok])
        m = dve.do(lambda e, bank=bank: e.tensor_tensor(w_mean[:], bank[:, 0:7], inv_count[:], ALU.mult), after=[total, loaded("const")])
        work.release(i, m)
        m = dve.do(lambda e: e.tensor_scalar(w_mean[:], w_mean[:], 1e-5, None, ALU.max), after=[m])
        dve.do(lambda e: e.reciprocal(w_scale[:], w_mean[:]), after=[m])
        w_unit_ok = m = dve.do(lambda e: e.tensor_tensor(w_unit[:], w_mean[:], unit[:], ALU.mult))
        for j, n in enumerate(order + ["wgk2"]):
            src = wgk2_raw[:] if n == "wgk2" else raw(n, w_raw)
            tmp = wgk2_raw[:] if n == "wgk2" else raw(n, w_raw)
            dst = wgk2_int[:] if n == "wgk2" else raw(n, w_int)
            rows = R if n == "wgk2" else P
            s = w_scale[0:rows, j:j + 1]
            m1 = dve.do(lambda e, a=(tmp, src, s): e.tensor_scalar(a[0], a[1], a[2], 1.0, ALU.mult, ALU.min), after=[m])
            m1 = dve.do(lambda e, a=tmp: e.tensor_scalar(a, a, -1.0, ROUND, ALU.max, ALU.add), after=[m1])
            w_int_ok = dve.do(lambda e, a=(dst, tmp): e.tensor_scalar(a[0], a[1], ROUND, None, ALU.subtract), after=[m1])

        def w_chunk(name, c, a, b):
            at, _, w = col[name]
            return w_int[:, at + c * w + a:at + c * w + b]

        def rsqrt(v, tmp, out, ready):
            m = act.do(lambda e: e.activation(tmp, v, ACT.Ln), after=[ready])
            m = act.do(lambda e: e.activation(out, tmp, ACT.Exp, scale=-0.5), after=[m])
            m = dve.do(lambda e: e.tensor_tensor(tmp, out, out, ALU.mult), after=[m])
            m = dve.do(lambda e: e.tensor_tensor(tmp, tmp, v, ALU.mult), after=[m])
            m = dve.do(lambda e: e.tensor_scalar(tmp, tmp, -0.5, 1.5, ALU.mult, ALU.add), after=[m])
            return dve.do(lambda e: e.tensor_tensor(out, out, tmp, ALU.mult), after=[m])

        def ring(name, shape, n=2, dt=F32, phase=None):
            if phase:
                return Ring([carve(phase, shape, dt) for _ in range(n)])
            return Ring([sb(f"{name}{i}", shape, dt) for i in range(n)])

        xn_r = ring("xn", [P, NORMS, NT * D], phase="attention")
        st_r = ring("st", [P, 64], 3)
        xi_r = ring("xi", [P, NORMS, NT * D], 1, BF16, phase="attention")
        xT_r = ring("xT", [P, NORMS, DC, L], 1, BF16, phase="attention")
        sq_r = ring("sq", [P, D], 2, BF16)
        q_r = ring("q", [P, DC, L])
        k_r = ring("k", [P, DC, L])
        gk_r = ring("gk", [P, DC, L])
        v_r = ring("v", [P, NT, DV], 3, phase="attention")
        sg_r = ring("sg", [P, NT, DV], 3, phase="attention")
        ge_r = ring("ge", [P, DV], 2, phase="attention")
        z_r = ring("z", [P, NT, R])
        zw_r = ring("zw", [P, NT, R])
        zT_r = ring("zT", [R, L])
        S = {}

        def A1(b):
            xb = x[:, b * NT:(b + 1) * NT, :].rearrange("p i d -> p (i d)")
            xn, st, xi, xT = xn_r.buf(b), st_r.buf(b), xi_r.buf(b), xT_r.buf(b)
            wv = norm_w[:].unsqueeze(2).to_broadcast([P, NORMS, NT, D])
            m_xn = pool.do(lambda e: e.tensor_tensor(xn[:].rearrange("p j (i d) -> p j i d", i=NT), bcast(x[:, b * NT:(b + 1) * NT, :], NORMS), wv, ALU.mult),
                           after=[loaded(f"x{b}"), loaded("norm"), *xn_r.free(b)])
            for i in range(NT):
                n = b * NT + i
                act.wait(*sq_r.free(n), *st_r.free(b))
                m = act.do(lambda e, i=i, n=n: e.activation(sq_r.buf(n)[:], x[:, n, :], ACT.Square, accum_out=st[:, i:i + 1]),
                           after=[loaded(f"x{b}")])
                sq_r.release(n, m)
            m = dve.do(lambda e: e.tensor_scalar(st[:, 0:2], st[:, 0:2], 1.0 / D, 1e-8, ALU.mult, ALU.add), after=[m])
            rms = rsqrt(st[:, 0:2], st[:, 4:6], st[:, 2:4], m)
            c = st[:, 10:20]
            cv = c.rearrange("p (j i) -> p j i", i=NT)
            m = dve.do(lambda e: e.tensor_reduce(c, xn[:].rearrange("p j (i d) -> p (j i) d", i=NT), AX.X, ALU.max,
                                                 apply_absolute_value=True), after=[m_xn])
            rb = bcast(st[:, 2:4], NORMS)
            m = dve.do(lambda e: e.tensor_tensor(cv, cv, rb, ALU.mult), after=[m, rms])
            m = dve.do(lambda e: e.tensor_scalar(c, c, 1e-5, None, ALU.max), after=[m])
            s = st[:, 20:30]
            sv = s.rearrange("p (j i) -> p j i", i=NT)
            m = dve.do(lambda e: e.reciprocal(s, c), after=[m])
            m = dve.do(lambda e: e.tensor_tensor(sv, sv, rb, ALU.mult), after=[m])
            m = dve.do(lambda e: e.tensor_scalar(s, s, 127.0, None, ALU.mult), after=[m])
            u = st[:, 30:40]
            m2 = dve.do(lambda e: e.tensor_tensor(u.rearrange("p (j i) -> p j i", i=NT), cv,
                                                  w_unit[:, 0:NORMS].unsqueeze(2).to_broadcast([P, NORMS, NT]), ALU.mult), after=[w_unit_ok])
            m2 = dve.do(lambda e: e.tensor_tensor(st[:, 40:42], st[:, 30 + 2 * JK:32 + 2 * JK], st[:, 30 + 2 * JV:32 + 2 * JV], ALU.mult), after=[m2])
            scales = dve.do(lambda e: e.tensor_scalar(st[:, 42:44], st[:, 30 + 2 * JG:32 + 2 * JG], -1.0, None, ALU.mult))
            for j in range(NORMS):
                for i in range(NT):
                    a = xn[:, j, i * D:(i + 1) * D]
                    m = dve.do(lambda e, a=a, k=20 + 2 * j + i: e.tensor_scalar(a, a, st[:, k:k + 1], ROUND, ALU.mult, ALU.add), after=[m] if i + j == 0 else [])
            m_xi = dve.do(lambda e: e.tensor_scalar(xi[:], xn[:], ROUND, None, ALU.subtract), after=[m, *xi_r.free(b)])
            xn_r.release(b, m_xi)
            copied = []
            for j in range(NORMS):
                if j % 2 == 0:
                    n, bank, free = take()
                    tb = bank[:].bitcast(BF16)
                    pe.wait(m_xi, ident_ok, *free)
                o = (j % 2) * DC * L
                for c_ in range(DC):
                    for i in range(NT):
                        m = pe.do(lambda e, j=j, c_=c_, i=i, tb=tb, o=o: e.transpose(
                            tb[:, o + c_ * L + i * P:o + c_ * L + (i + 1) * P], xi[:, j, i * D + c_ * P:i * D + (c_ + 1) * P], ident_bf[:]),
                            signal=(j % 2 == 1 or j == NORMS - 1) and c_ == DC - 1 and i == NT - 1)
                if j % 2 == 1 or j == NORMS - 1:
                    j0 = j - j % 2
                    k = j - j0 + 1
                    src = tb[:, 0:k * DC * L].rearrange("p (j c l) -> p j c l", j=k, c=DC)
                    mc = act.do(lambda e, src=src, j0=j0, k=k: e.activation(xT[:, j0:j0 + k], src, ACT.Copy), after=[m, *xT_r.free(b)])
                    work.release(n, mc)
                    copied.append(mc)
            xi_r.release(b, m)
            v, sg, z, zw, zT = (r.buf(b) for r in (v_r, sg_r, z_r, zw_r, zT_r))
            n, bank, free = take()
            for i in range(NT):
                for c_ in range(DC):
                    m = pe.do(lambda e, i=i, c_=c_, bank=bank: e.matmul(bank[:, i * R:(i + 1) * R], xT[:, JR, c_, i * P:(i + 1) * P],
                                                                        w_chunk("wgk1T", c_, 0, R), start=c_ == 0, stop=c_ == DC - 1),
                              after=[*free, copied[1], w_int_ok], signal=i == NT - 1 and c_ == DC - 1)
            for i in range(NT):
                mz = dve.do(lambda e, i=i, bank=bank: e.tensor_scalar(z[:, i, :], bank[:, i * R:(i + 1) * R], st[:, 30 + 2 * JR + i:31 + 2 * JR + i], None, ALU.mult),
                            after=[m, scales, *z_r.free(b)])
            work.release(n, mz)
            def project(name, j, m_in):
                n, bank, free = take()
                for e_ in range(DC):
                    for c_ in range(DC):
                        m = pe.do(lambda e, e_=e_, c_=c_, bank=bank: e.matmul(bank[:, e_ * L:(e_ + 1) * L], w_chunk(name, c_, e_ * P, (e_ + 1) * P),
                                                                              xT[:, j, c_, :], start=c_ == 0, stop=c_ == DC - 1),
                                  after=[*free, m_in], signal=e_ == DC - 1 and c_ == DC - 1)
                return n, bank[:].rearrange("p (c l) -> p c l", c=DC), m
            n, qps, m = project("wqT", JQ, copied[0])
            mq = act.do(lambda e: e.activation(q_r.buf(b)[:], qps, ACT.Copy), after=[m, *q_r.free(b)])
            work.release(n, mq)
            n, kps, m = project("wkT", JK, copied[0])
            mk = act.do(lambda e: e.activation(k_r.buf(b)[:], kps, ACT.Copy), after=[m, *k_r.free(b)])
            work.release(n, mk)
            ms, rr, tt, cc, uu = (st[:, 44 + 2 * k:46 + 2 * k] for k in range(5))
            m = dve.do(lambda e: e.tensor_tensor(zw[:], z[:], z[:], ALU.mult), after=[mz, *zw_r.free(b)])
            m = dve.do(lambda e: e.tensor_reduce(ms, zw[:], AX.X, ALU.add), after=[m])
            m = dve.do(lambda e: e.tensor_scalar(ms, ms, 1.0 / R, 1e-8, ALU.mult, ALU.add), after=[m])
            mr = rsqrt(ms, tt, rr, m)
            m = dve.do(lambda e: e.tensor_tensor(zw[:], z[:], bcast(ngk2_w[:], NT), ALU.mult), after=[loaded("attn")])
            m = dve.do(lambda e: e.tensor_reduce(cc, zw[:], AX.X, ALU.max, apply_absolute_value=True), after=[m])
            m = dve.do(lambda e: e.tensor_tensor(cc, cc, rr, ALU.mult), after=[m, mr])
            m = dve.do(lambda e: e.tensor_scalar(cc, cc, 1e-5, None, ALU.max), after=[m])
            m = dve.do(lambda e: e.reciprocal(tt, cc), after=[m])
            m = dve.do(lambda e: e.tensor_tensor(tt, tt, rr, ALU.mult), after=[m])
            m = dve.do(lambda e: e.tensor_scalar(tt, tt, 127.0, None, ALU.mult), after=[m])
            m = dve.do(lambda e: e.tensor_scalar(uu, cc, w_unit[:, 6:7], None, ALU.mult), after=[m])
            for i in range(NT):
                m = dve.do(lambda e, i=i: e.tensor_scalar(zw[:, i, :], zw[:, i, :], tt[:, i:i + 1], ROUND, ALU.mult, ALU.add), after=[m])
            for i in range(NT):
                m = dve.do(lambda e, i=i: e.tensor_scalar(zw[:, i, :], zw[:, i, :], ROUND, uu[:, i:i + 1], ALU.subtract, ALU.mult), after=[m])
            m_zw = m
            for i in range(NT):
                n, bank, free = take()
                for c_ in range(DC):
                    m = pe.do(lambda e, i=i, c_=c_, bank=bank: e.matmul(bank[:], xT[:, JV, c_, i * P:(i + 1) * P], w_chunk("wvT", c_, 0, DV), start=c_ == 0, stop=c_ == DC - 1),
                              after=[*free, copied[1]], signal=c_ == DC - 1)
                mv = act.do(lambda e, i=i, bank=bank: e.activation(v[:, i, :], bank[:], ACT.Copy, scale=st[:, 40 + i:41 + i]), after=[m, scales, *v_r.free(b)])
                work.release(n, mv)
            for i in range(NT):
                n, bank, free = take()
                for c_ in range(DC):
                    m = pe.do(lambda e, i=i, c_=c_, bank=bank: e.matmul(bank[:], xT[:, JG, c_, i * P:(i + 1) * P], w_chunk("wgT", c_, 0, DV), start=c_ == 0, stop=c_ == DC - 1),
                              after=[*free, copied[2]], signal=c_ == DC - 1)
                u_ = b * NT + i
                ge = ge_r.buf(u_)
                m1 = act.do(lambda e, i=i, bank=bank, ge=ge: e.activation(ge[:], bank[:], ACT.Exp, scale=st[:, 42 + i:43 + i]), after=[m, scales, *ge_r.free(u_)])
                m1 = dve.do(lambda e, ge=ge: e.tensor_scalar(ge[:], ge[:], 1.0, None, ALU.add), after=[m1])
                m1 = dve.do(lambda e, ge=ge: e.reciprocal(ge[:], ge[:]), after=[m1])
                mg = dve.do(lambda e, i=i, bank=bank, ge=ge: e.scalar_tensor_tensor(sg[:, i, :], bank[:], st[:, 30 + 2 * JG + i:31 + 2 * JG + i], ge[:], ALU.mult, ALU.mult),
                            after=[m1, m, scales, *sg_r.free(b)])
                ge_r.release(u_, mg)
                work.release(n, mg)
            n, bank, free = take()
            for i in range(NT):
                m = pe.do(lambda e, i=i, bank=bank: e.transpose(bank[0:R, i * P:(i + 1) * P], zw[:, i, :], ident[:]), after=[m_zw, *free], signal=i == NT - 1)
            z_r.release(b, m_zw)
            zw_r.release(b, m)
            mc = act.do(lambda e, bank=bank: e.activation(zT[:], bank[0:R, 0:L], ACT.Copy), after=[m, *zT_r.free(b)])
            work.release(n, mc)
            n, bank, free = take()
            for c_ in range(DC):
                m = pe.do(lambda e, c_=c_, bank=bank: e.matmul(bank[:, c_ * L:(c_ + 1) * L], wgk2_int[:, c_ * P:(c_ + 1) * P], zT[:], start=True, stop=True),
                          after=[mc, *free], signal=c_ == DC - 1)
            zT_r.release(b, m)
            xT_r.release(b, m)
            gk = gk_r.buf(b)
            mgk = act.do(lambda e, bank=bank: e.activation(gk[:], bank[:].rearrange("p (c l) -> p c l", c=DC), ACT.Copy), after=[m, *gk_r.free(b)])
            work.release(n, mgk)
            S[b] = dict(q=mq, k=mk, v=mv, g=mg, gk=mgk, scales=scales)

        abs_r = ring("gabs", [P, DC, L], 1)
        gate_r = ring("gate", [P, DC, L], 2)
        Q_r = ring("Q", [P, DC, L])
        tot_r = ring("tot", [P, DC, L], 1)
        A_bufs = [carve("attention", [P, DC, 2, NT, P]) for _ in range(2)]
        A_r = Ring(A_bufs)
        Aoff_r = ring("Aoff", [P, DC, 2, P], 2, phase="attention")
        a_zero = []
        for a in A_bufs:
            a_zero.append(pool.do(lambda e, a=a: e.memset(a[:], 0.0)))
        level_banks = Ring([(banks[0], banks[1]), (banks[2], banks[3])])
        level_n = [0]

        def A2(b):
            q, k, gk, ga, gate, Q, tot = (r.buf(b) for r in (q_r, k_r, gk_r, abs_r, gate_r, Q_r, tot_r))
            A, Aoff = A_r.buf(b), Aoff_r.buf(b)
            for c in range(DC):
                m = act.do(lambda e, c=c: e.activation(ga[:, c, :], gk[:, c, :], ACT.Abs, bias=bgk2[:, c:c + 1]), after=[S[b]["gk"], loaded("attn"), *abs_r.free(b)])
                mm = dve.do(lambda e, c=c: e.tensor_scalar(gk[:, c, :], gk[:, c, :], bgk2[:, c:c + 1], 0.0, ALU.add, ALU.min), after=[m])
            m = act.do(lambda e: e.activation(ga[:], ga[:], ACT.Exp, scale=-1.0), after=[m])
            m = act.do(lambda e: e.activation(ga[:], ga[:], ACT.Ln, bias=1.0), after=[m])
            m = dve.do(lambda e: e.tensor_tensor(gk[:], gk[:], ga[:], ALU.subtract), after=[m, mm])
            abs_r.release(b, m)
            m_gate = act.do(lambda e: e.activation(gate[:], gk[:], ACT.Exp, scale=1.0 / 16.0), after=[m, *gate_r.free(b)])
            gk_r.release(b, m_gate)
            mQ = [dve.do(lambda e, c=c: e.tensor_tensor(Q[:, c, :], q[:, c, :], gate[:, c, :], ALU.mult), after=[m_gate, S[b]["q"], *Q_r.free(b)]) for c in range(DC)]
            mK = [S[b]["k"]] * DC
            mT = [m_gate] * DC
            A_free = [*A_r.free(b), a_zero[b % 2]]
            for lev, h in enumerate([0] + LEVELS):
                for c in range(DC):
                    n = level_n[0]
                    level_n[0] += 1
                    pair = level_banks.buf(n)
                    queries = q if h == 0 else Q
                    pe.wait(*level_banks.free(n), mQ[c], mK[c], S[b]["q"])
                    hs = h if h >= 32 else P
                    for i in range(NT):
                        for s0 in range(0, P, 2 * h if h >= 32 else P):
                            t0 = s0 + h if h >= 32 else 0
                            for hd in range(2):
                                r0 = hd * DK
                                m = pe.do(lambda e, r0=r0, hd=hd, i=i, s0=s0, t0=t0, c=c, hs=hs, pair=pair, queries=queries: e.matmul(
                                    pair[hd][s0:s0 + hs, i * P + t0:i * P + t0 + hs],
                                    k[r0:r0 + DK, c, i * P + s0:i * P + s0 + hs], queries[r0:r0 + DK, c, i * P + t0:i * P + t0 + hs],
                                    start=True, stop=True), signal=False)
                    last = pe.queue.pop()
                    pe.count += 1
                    m_sc = (pe.sem, pe.count)
                    pe.queue.append(lambda e, last=last: last(e).then_inc(pe.sem, 1))
                    if h < 32:
                        for hd in range(2):
                            src = pair[hd][:, 0:NT * P].rearrange("p (i t) -> p i t", i=NT)
                            mc = dve.do(lambda e, c=c, hd=hd, src=src, lev=lev: e.copy_predicated(
                                A[:, c, hd], bcast(level_mask[:, lev, :], NT), src), after=[m_sc, mask_ok, *A_free])
                    else:
                        for hd in range(2):
                            for s0 in range(0, P, 2 * h):
                                t0 = s0 + h
                                src = pair[hd][s0:s0 + h, 0:NT * P].rearrange("p (i t) -> p i t", i=NT)[:, :, t0:t0 + h]
                                mc = act.do(lambda e, c=c, hd=hd, s0=s0, t0=t0, h=h, src=src: e.activation(
                                    A[s0:s0 + h, c, hd, :, t0:t0 + h], src, ACT.Copy), after=[m_sc, *A_free])
                    level_banks.release(n, mc)
                    if h == 0:
                        continue
                    v2 = lambda buf, w: buf[:, c, 0:2 * w * (L // (2 * w))].rearrange("p (n two w) -> p n two w", two=2, w=w)
                    nb = L // (2 * h)
                    at_h = L - 2 * L // h
                    T = gate[:, c, :] if h == 1 else tot[:, c, at_h:at_h + 2 * nb]
                    T = T.rearrange("p (n two) -> p n two", two=2)
                    Qv, Kv = v2(Q, h), v2(k, h)
                    if h < P:
                        mQ[c] = dve.do(lambda e, Qv=Qv, T=T, h=h, nb=nb: e.tensor_tensor(
                            Qv[:, :, 1], Qv[:, :, 1], T[:, :, 0:1].to_broadcast([P, nb, h]), ALU.mult), after=[m_sc, mT[c]])
                        mK[c] = pool.do(lambda e, Kv=Kv, T=T, h=h, nb=nb: e.tensor_tensor(
                            Kv[:, :, 0], Kv[:, :, 0], T[:, :, 1:2].to_broadcast([P, nb, h]), ALU.mult), after=[m_sc, mT[c]])
                        if h < 64:
                            mT[c] = dve.do(lambda e, T=T, c=c, nb=nb: e.tensor_tensor(tot[:, c, L - 2 * nb:L - nb], T[:, :, 0], T[:, :, 1], ALU.mult),
                                           after=[mT[c], *tot_r.free(b)])
            for c in range(DC):
                n = level_n[0]
                level_n[0] += 1
                pair = level_banks.buf(n)
                pe.wait(*level_banks.free(n), mQ[c], mK[c])
                for hd in range(2):
                    r0 = hd * DK
                    m = pe.do(lambda e, hd=hd, r0=r0, c=c, pair=pair: e.matmul(pair[hd][:, 0:P], k[r0:r0 + DK, c, 0:P], Q[r0:r0 + DK, c, P:2 * P], start=True, stop=True), signal=hd == 1)
                for hd in range(2):
                    m_off = act.do(lambda e, hd=hd, c=c, pair=pair: e.activation(Aoff[:, c, hd, :], pair[hd][:, 0:P], ACT.Copy), after=[m, *Aoff_r.free(b)])
                level_banks.release(n, m_off)
            q_r.release(b, m)
            k_r.release(b, m)
            Q_r.release(b, m)
            tot_r.release(b, mQ[1], mK[1])
            gate_r.release(b, mQ[1], mK[1])
            S[b].update(A=[dve.last(), act.last()], off=m_off)

        y_r = ring("y", [P, DV], 2, phase="attention")
        yw_r = ring("yw", [P, DV], 2, phase="attention")
        yi_r = ring("yi", [P, DV], 2, BF16)
        yT_r = ring("yT", [P, VC, P], 2, BF16)
        st3_r = ring("st3", [P, 32], 2)

        def layer_norm(dst, src, st, ready):
            m = dve.do(lambda e: e.bn_stats(st[:, 0:6], src), after=[ready])
            m = dve.do(lambda e: e.bn_aggr(st[:, 6:8], st[:, 0:6]), after=[m])
            m = dve.do(lambda e: e.tensor_scalar(st[:, 7:8], st[:, 7:8], 1e-5, None, ALU.add), after=[m])
            m = rsqrt(st[:, 7:8], st[:, 8:9], st[:, 9:10], m)
            return dve.do(lambda e: e.tensor_scalar(dst, src, st[:, 6:7], st[:, 9:10], ALU.subtract, ALU.mult), after=[m])

        def A3(b):
            st1, v, sg, A, Aoff = (r.buf(b) for r in (st_r, v_r, sg_r, A_r, Aoff_r))
            for i in range(NT):
                u = b * NT + i
                y, yw, yi, yT, st = (r.buf(u) for r in (y_r, yw_r, yi_r, yT_r, st3_r))
                n, bank, free = take()
                pe.wait(*free, *S[b]["A"], S[b]["off"], S[b]["v"])
                for c in range(DC):
                    for hd in range(2):
                        cols = slice((2 * c + hd) * DVH, (2 * c + hd + 1) * DVH)
                        m = pe.do(lambda e, c=c, hd=hd, i=i, cols=cols, bank=bank: e.matmul(bank[:, cols], A[:, c, hd, i, :], v[:, i, cols], start=True, stop=i == 0), signal=i == 0 and c * hd == 1)
                        if i == 1:
                            m = pe.do(lambda e, c=c, hd=hd, cols=cols, bank=bank: e.matmul(bank[:, cols], Aoff[:, c, hd, :], v[:, 0, cols], start=False, stop=True), signal=c * hd == 1)
                if i == NT - 1:
                    v_r.release(b, m)
                    A_r.release(b, m)
                    Aoff_r.release(b, m)
                my = dve.do(lambda e, i=i, y=y, bank=bank: e.scalar_tensor_tensor(y[:], bank[:], st1[:, 30 + 2 * JQ + i:31 + 2 * JQ + i], sg[:, i, :], ALU.mult, ALU.mult),
                            after=[m, S[b]["g"], *y_r.free(u)])
                work.release(n, my)
                m_w = pool.do(lambda e, yw=yw, y=y: e.tensor_tensor(yw[:], y[:], no_w[:], ALU.mult), after=[my, loaded("attn"), *yw_r.free(u)])
                m_s = act.do(lambda e, i=i, y=y, st=st: e.activation(sg[:, i, :], y[:], ACT.Square, accum_out=st[:, 0:1]), after=[my, *st3_r.free(u)])
                y_r.release(u, m_w, m_s)
                m = dve.do(lambda e, st=st: e.tensor_scalar(st[:, 0:1], st[:, 0:1], 1.0 / DV, 1e-8, ALU.mult, ALU.add), after=[m_s])
                m_r = rsqrt(st[:, 0:1], st[:, 1:2], st[:, 2:3], m)
                m = dve.do(lambda e, st=st, yw=yw: e.tensor_reduce(st[:, 3:4], yw[:], AX.X, ALU.max, apply_absolute_value=True), after=[m_w])
                m = dve.do(lambda e, st=st: e.tensor_scalar(st[:, 3:4], st[:, 3:4], st[:, 2:3], 1e-5, ALU.mult, ALU.max), after=[m, m_r])
                m = dve.do(lambda e, st=st: e.reciprocal(st[:, 4:5], st[:, 3:4]), after=[m])
                m = dve.do(lambda e, st=st: e.tensor_scalar(st[:, 4:5], st[:, 4:5], st[:, 2:3], 127.0, ALU.mult, ALU.mult), after=[m])
                dve.do(lambda e, st=st: e.tensor_scalar(st[:, 5:6], st[:, 3:4], w_unit[:, 5:6], None, ALU.mult))
                m = dve.do(lambda e, st=st, yw=yw: e.tensor_scalar(yw[:], yw[:], st[:, 4:5], ROUND, ALU.mult, ALU.add), after=[m])
                m_yi = dve.do(lambda e, yi=yi, yw=yw: e.tensor_scalar(yi[:], yw[:], ROUND, None, ALU.subtract), after=[m, *yi_r.free(u)])
                yw_r.release(u, m_yi)
                n, bank, free = take()
                tb = bank[:].bitcast(BF16)
                for c in range(VC):
                    m = pe.do(lambda e, c=c, tb=tb, yi=yi: e.transpose(tb[:, c * P:(c + 1) * P], yi[:, c * P:(c + 1) * P], ident_bf[:]), after=[m_yi, *free], signal=c == VC - 1)
                yi_r.release(u, m)
                mc = act.do(lambda e, tb=tb, yT=yT: e.activation(yT[:], tb[:, 0:VC * P].rearrange("p (c t) -> p c t", c=VC), ACT.Copy), after=[m, *yT_r.free(u)])
                work.release(n, mc)
                n, bank, free = take()
                for c in range(VC):
                    m = pe.do(lambda e, c=c, bank=bank, yT=yT: e.matmul(bank[:, 0:D], yT[:, c, :], w_chunk("woT", c, 0, D), start=c == 0, stop=c == VC - 1), after=[mc, *free], signal=c == VC - 1)
                yT_r.release(u, m)
                m = dve.do(lambda e, u=u, bank=bank, st=st: e.scalar_tensor_tensor(x[:, u, :], bank[:, 0:D], st[:, 5:6], x[:, u, :], ALU.mult, ALU.add), after=[m])
                work.release(n, m)
                m = layer_norm(x[:, u, :], x[:, u, :], st[:, 8:20], m)
                st3_r.release(u, m)
            sg_r.release(b, m_s)
            st_r.release(b, m)
            S[b]["x1"] = m

        xk = sb("xk", [P, DC, B * S2])
        xkb_r = ring("xkb", [P, DC, XH // DC, S2], 1)
        xv_r = ring("xv", [S2, XH, XD + 1])
        x1T_r = ring("x1T", [P, DC, L], 1)
        xq_r = ring("xq", [P, DC, L])
        sc_r = ring("sc", [P, XH, S2], 2, phase="cross")
        mx_r = ring("mx", [P, XH])
        pT_r = ring("pT", [S2, XH, P], 1, phase="cross")
        co_r = ring("co", [P, D])
        coT_r = ring("coT", [P, DC, P], 1)
        xr_r = ring("xr", [P, D])
        stx_r = ring("stx", [P, 12])

        xv_one = [dve.do(lambda e, a=a: e.memset(a[:], 1.0)) for a in xv_r.bufs]
        dve.do(lambda e: e.tensor_copy(keep[:], mask_raw[:]), after=[loaded("cross")])
        m = dve.do(lambda e: e.tensor_scalar(keep[:], keep[:], 0.0, None, ALU.is_equal), after=[dve.last()])
        m = dve.do(lambda e: e.tensor_scalar(drop[:], keep[:], -1e9, None, ALU.mult), after=[m])
        m_mask = dve.do(lambda e: e.tensor_scalar(keep[:], keep[:], -1.0, 1.0, ALU.mult, ALU.add), after=[m])
        half = B * S2 // 2
        for c in range(DC):
            for hf in range(2):
                n, bank, free = take()
                for d in range(DC):
                    m = pe.do(lambda e, c=c, d=d, hf=hf, bank=bank: e.matmul(bank[:, 0:half], xw_T["xWkT"][:, d, c * P:(c + 1) * P], ctxT[:, d, hf * half:(hf + 1) * half],
                                                                            start=d == 0, stop=d == DC - 1), after=[loaded("cross"), *free], signal=d == DC - 1)
                m_xk = act.do(lambda e, c=c, hf=hf, bank=bank: e.activation(xk[:, c, hf * half:(hf + 1) * half], bank[:, 0:half], ACT.Identity, bias=xbk[:, c:c + 1]), after=[m, loaded("cross")])
                work.release(n, m_xk)

        def X(b):
            xkb, xv, x1T, xq = (r.buf(b) for r in (xkb_r, xv_r, x1T_r, xq_r))
            NHC = XH // DC
            for c in range(DC):
                m_kb = pool.do(lambda e, c=c: e.tensor_tensor(xkb[:, c], bcast(xk[:, c, b * S2:(b + 1) * S2], NHC),
                                                              head_mask[:].unsqueeze(2).to_broadcast([P, NHC, S2]), ALU.mult), after=[m_xk, loaded("cross"), *xkb_r.free(b)])
            n, bank, free = take()
            for d in range(DC):
                m = pe.do(lambda e, d=d, bank=bank: e.matmul(bank[0:S2, 0:D], ctxT[:, d, b * S2:(b + 1) * S2], xw_T["xWvT"][:, d, :], start=d == 0, stop=d == DC - 1), after=[loaded("cross"), *free], signal=d == DC - 1)
            m_xv = dve.do(lambda e, bank=bank: e.tensor_tensor(xv[:, :, 0:XD], bank[0:S2, 0:D].rearrange("p (h d) -> p h d", h=XH), xbv[0:S2, :].rearrange("p (h d) -> p h d", h=XH), ALU.add),
                          after=[m, loaded("cross"), *xv_r.free(b), xv_one[b % 2]])
            work.release(n, m_xv)
            n, bank, free = take()
            for c in range(DC):
                for i in range(NT):
                    m = pe.do(lambda e, c=c, i=i, bank=bank: e.transpose(bank[:, c * L + i * P:c * L + (i + 1) * P], x[:, b * NT + i, c * P:(c + 1) * P], ident[:]),
                              after=[S[b]["x1"], *free, loaded("const")], signal=c * i == 1)
            mc = act.do(lambda e, bank=bank: e.activation(x1T[:], bank[:].rearrange("p (c l) -> p c l", c=DC), ACT.Copy), after=[m, *x1T_r.free(b)])
            work.release(n, mc)
            n, bank, free = take()
            for c in range(DC):
                for d in range(DC):
                    m = pe.do(lambda e, c=c, d=d, bank=bank: e.matmul(bank[:, c * L:(c + 1) * L], xw_T["xWqT"][:, d, c * P:(c + 1) * P], x1T[:, d, :], start=d == 0, stop=d == DC - 1),
                              after=[mc, *free], signal=c * d == 1)
            x1T_r.release(b, m)
            for c in range(DC):
                m_q = dve.do(lambda e, c=c, bank=bank: e.tensor_scalar(xq[:, c, :], bank[:, c * L:(c + 1) * L], xbq[:, c:c + 1], float(XD) ** -0.5, ALU.add, ALU.mult), after=[m, *xq_r.free(b)])
            work.release(n, m_q)
            for i in range(NT):
                u = b * NT + i
                sc, mx, pT, co, coT, xr, st = (r.buf(u) for r in (sc_r, mx_r, pT_r, co_r, coT_r, xr_r, stx_r))
                for c in range(DC):
                    for g_ in range(XH // DC // HB):
                        h0 = g_ * HB
                        hh = c * (XH // DC) + h0
                        n, bank, free = take()
                        m = pe.do(lambda e, c=c, i=i, h0=h0, bank=bank: e.matmul(bank[:, 0:HB * S2], xq[:, c, i * P:(i + 1) * P], xkb[:, c, h0:h0 + HB, :].rearrange("p h k -> p (h k)"), start=True, stop=True),
                                  after=[m_q, m_kb, *free])
                        m_k = dve.do(lambda e, i=i, hh=hh, bank=bank, sc=sc: e.tensor_tensor(sc[:, hh:hh + HB, :], bank[:, 0:HB * S2].rearrange("p (h k) -> p h k", h=HB), bcast(keep[:, i, :], HB), ALU.mult),
                                     after=[m, m_mask, *sc_r.free(u)])
                        work.release(n, m_k)
                m_scores = m
                m = pool.do(lambda e, i=i, sc=sc: e.tensor_tensor(sc[:], sc[:], bcast(drop[:, i, :], XH), ALU.add), after=[m_k, m_mask])
                m = dve.do(lambda e, mx=mx, sc=sc: e.tensor_reduce(mx[:], sc[:], AX.X, ALU.max), after=[m, *mx_r.free(u)])
                m = pool.do(lambda e, sc=sc, mx=mx: e.tensor_tensor(sc[:], sc[:], mx[:].unsqueeze(2).to_broadcast([P, XH, S2]), ALU.subtract), after=[m])
                m_e = act.do(lambda e, sc=sc: e.activation(sc[:], sc[:], ACT.Exp), after=[m])
                act.wait(*pT_r.free(u))
                for g_ in range(4):
                    n, bank, free = take()
                    for h in range(4):
                        m = pe.do(lambda e, h=h, g_=g_, bank=bank, sc=sc: e.transpose(bank[0:S2, h * P:(h + 1) * P], sc[:, 4 * g_ + h, :], ident[:]), after=[m_e, *free], signal=h == 3)
                    m_p = act.do(lambda e, g_=g_, bank=bank, pT=pT: e.activation(pT[:, 4 * g_:4 * g_ + 4, :], bank[0:S2, :].rearrange("p (h t) -> p h t", h=4), ACT.Copy), after=[m])
                    work.release(n, m_p)
                sc_r.release(u, m)
                n, bank, free = take()
                for h in range(XH):
                    m = pe.do(lambda e, h=h, bank=bank, pT=pT: e.matmul(bank[:, h * (XD + 1):(h + 1) * (XD + 1)], pT[:, h, :], xv[:, h, :], start=True, stop=True), after=[m_p, m_xv, *free], signal=h == XH - 1)
                pT_r.release(u, m)
                m_av = m
                ov = bank[:, 0:XH * (XD + 1)].rearrange("p (h d) -> p h d", h=XH)
                m = dve.do(lambda e, mx=mx, ov=ov: e.reciprocal(mx[:], ov[:, :, XD]), after=[m])
                m_co = dve.do(lambda e, mx=mx, ov=ov, co=co: e.tensor_tensor(co[:].rearrange("p (h d) -> p h d", h=XH), ov[:, :, 0:XD], mx[:].unsqueeze(2).to_broadcast([P, XH, XD]), ALU.mult),
                              after=[m, *co_r.free(u)])
                mx_r.release(u, m_co)
                work.release(n, m_co)
                n, bank, free = take()
                for c in range(DC):
                    m = pe.do(lambda e, c=c, bank=bank, co=co: e.transpose(bank[:, c * P:(c + 1) * P], co[:, c * P:(c + 1) * P], ident[:]), after=[m_co, *free], signal=c == DC - 1)
                co_r.release(u, m)
                mc = act.do(lambda e, bank=bank, coT=coT: e.activation(coT[:], bank[:, 0:DC * P].rearrange("p (c t) -> p c t", c=DC), ACT.Copy), after=[m, *coT_r.free(u)])
                work.release(n, mc)
                n, bank, free = take()
                for c in range(DC):
                    m = pe.do(lambda e, c=c, bank=bank, coT=coT: e.matmul(bank[:, 0:D], coT[:, c, :], xw_T["xWoT"][:, c, :], start=c == 0, stop=c == DC - 1), after=[mc, *free], signal=c == DC - 1)
                coT_r.release(u, m)
                m_xr = pool.do(lambda e, u=u, xr=xr: e.tensor_tensor(xr[:], x[:, u, :], xbo[:], ALU.add), after=[S[b]["x1"], loaded("cross"), *xr_r.free(u)])
                m = dve.do(lambda e, xr=xr, bank=bank: e.tensor_tensor(xr[:], bank[:, 0:D], xr[:], ALU.add), after=[m, m_xr])
                work.release(n, m)
                m = layer_norm(x[:, u, :], xr[:], st[:, 0:12], m)
                xr_r.release(u, m)
                stx_r.release(u, m)
            xkb_r.release(b, m_scores)
            xv_r.release(b, m_av)
            xq_r.release(b, m_scores)
            S[b]["x2"] = m

        for step in range(B + 3):
            if step < B:
                A1(step)
            if 0 <= step - 1 < B:
                A2(step - 1)
            if 0 <= step - 2 < B:
                A3(step - 2)
                attention_over = [lane.last() for lane in (pe, act, dve, pool)]
            if 0 <= step - 3 < B:
                X(step - 3)

        gateT = sb("gateT", [P, DC, E])
        gate_b = sb("gate_b", [P, E])
        lower = sb("lower", [P, E, E])
        load(gateT[:], t["gateT"].rearrange("(c p) e -> p c e", p=P), "router")
        load(gate_b[:], t["gate_bias"].partition_broadcast(P), "router")
        load(lower[:], t["lower"].rearrange("a b -> (a b)").partition_broadcast(P).rearrange("p (a b) -> p a b", a=E), "router")
        xhi = carve("experts", [P, DC, TILES * P], BF16)
        xlo = carve("experts", [P, DC, TILES * P], BF16)
        lg = sb("lg", [P, TILES, E])
        bi = sb("bi", [P, TILES, E])
        cm = carve("experts", [P, TILES, E, E])
        cm2 = carve("experts", [P, TILES, E, E])
        rt = sb("rt", [P, TILES])
        comb = sb("comb", [P, TILES, E])
        x2T_r = ring("x2T", [P, DC, L], 2, phase="experts")
        for lane in (act, dve, pool, sp):
            lane.wait(*attention_over)
        for b in range(B):
            x2T = x2T_r.buf(b)
            n, bank, free = take()
            for c in range(DC):
                for i in range(NT):
                    m = pe.do(lambda e, c=c, i=i, b=b, bank=bank: e.transpose(bank[:, c * L + i * P:c * L + (i + 1) * P], x[:, b * NT + i, c * P:(c + 1) * P], ident[:]),
                              after=[S[b]["x2"], *free], signal=c * i == 1)
            bv = bank[:].rearrange("p (c l) -> p c l", c=DC)
            act.do(lambda e, b=b, bv=bv: e.activation(xhi[:, :, b * L:(b + 1) * L], bv, ACT.Copy), after=[m])
            mc = act.do(lambda e, bv=bv, x2T=x2T: e.activation(x2T[:], bv, ACT.Copy), after=[*x2T_r.free(b)])
            m_split = dve.do(lambda e, b=b, x2T=x2T: e.tensor_tensor(xlo[:, :, b * L:(b + 1) * L], x2T[:], xhi[:, :, b * L:(b + 1) * L], ALU.subtract), after=[mc])
            work.release(n, mc)
            n, bank, free = take()
            for i in range(NT):
                for d in range(DC):
                    m = pe.do(lambda e, i=i, d=d, x2T=x2T, bank=bank: e.matmul(bank[:, i * E:(i + 1) * E], x2T[:, d, i * P:(i + 1) * P], gateT[:, d, :], start=d == 0, stop=d == DC - 1),
                              after=[mc, loaded("router"), *free], signal=i * d == 1)
            x2T_r.release(b, m, m_split)
            m_lg = act.do(lambda e, b=b, bank=bank: e.activation(lg[:, b * NT:(b + 1) * NT, :], bank[:, 0:NT * E].rearrange("p (i n) -> p i n", i=NT), ACT.Copy), after=[m])
            work.release(n, m_lg)
        rb = rt[:].unsqueeze(2).to_broadcast([P, TILES, E])
        m = dve.do(lambda e: e.tensor_reduce(rt[:], lg[:], AX.X, ALU.max), after=[m_lg])
        m = dve.do(lambda e: e.tensor_tensor(lg[:], lg[:], rb, ALU.subtract), after=[m])
        m = act.do(lambda e: e.activation(lg[:], lg[:], ACT.Exp), after=[m])
        m = dve.do(lambda e: e.tensor_reduce(rt[:], lg[:], AX.X, ALU.add), after=[m])
        m = dve.do(lambda e: e.reciprocal(rt[:], rt[:]), after=[m])
        m = dve.do(lambda e: e.tensor_tensor(lg[:], lg[:], rb, ALU.mult), after=[m])
        m = dve.do(lambda e: e.tensor_tensor(bi[:], lg[:], bcast(gate_b[:], TILES), ALU.add), after=[m, loaded("router")])
        mine = bi[:].unsqueeze(3).to_broadcast([P, TILES, E, E])
        other = bi[:].unsqueeze(2).to_broadcast([P, TILES, E, E])
        m = dve.do(lambda e: e.tensor_tensor(cm[:], other, mine, ALU.is_equal), after=[m])
        dve.do(lambda e: e.tensor_tensor(cm2[:], other, mine, ALU.is_gt))
        m = dve.do(lambda e: e.tensor_tensor(cm[:], cm[:], bcast(lower[:], TILES), ALU.mult), after=[m])
        m = dve.do(lambda e: e.tensor_tensor(cm[:], cm[:], cm2[:], ALU.add), after=[m])
        m = dve.do(lambda e: e.tensor_reduce(comb[:], cm[:], AX.X, ALU.add), after=[m])
        m = dve.do(lambda e: e.tensor_scalar(comb[:], comb[:], 1.5, None, ALU.is_lt), after=[m])
        m_comb = dve.do(lambda e: e.tensor_tensor(comb[:], comb[:], lg[:], ALU.mult), after=[m])

        CH = 512
        raw_r = ring("eraw", [P, 3, DC * F], 1, phase="experts")
        hi_r = ring("ehi", [P, 3, DC * F], 1, BF16, phase="experts")
        lo_r = ring("elo", [P, 3, DC * F], 1, BF16, phase="experts")
        sil_r = ring("sil", [P, CH], phase="experts")
        h_r = ring("h", [P, CH], phase="experts")
        hh_r = ring("hh", [P, FC, CH], 2, BF16, phase="experts")
        hl_r = ring("hl", [P, FC, CH], 2, BF16, phase="experts")
        hb = Ring(banks[0:4])
        m_lv = level_banks.marks[0] + level_banks.marks[1]
        hbn = 0
        job = 0
        fj = 0
        for ex in range(E + 1):
            raw_w, hi, lo = raw_r.buf(ex), hi_r.buf(ex), lo_r.buf(ex)
            srcs = [t["sw1T"], t["sw3T"], t["sw2T"]] if ex == E else [t["w1T"][ex], t["w3T"][ex], t["w2T"][ex]]
            sp.wait(*raw_r.free(ex))
            for k, s in enumerate(srcs):
                load(raw_w[:, k, :].rearrange("p (c n) -> p c n", c=s.shape[0] // P), s.rearrange("(c p) n -> p c n", p=P), f"expert{ex}")
            m_hi = act.do(lambda e, hi=hi, raw_w=raw_w: e.activation(hi[:], raw_w[:], ACT.Copy), after=[loaded(f"expert{ex}"), *hi_r.free(ex)])
            m_lo = pool.do(lambda e, hi=hi, lo=lo, raw_w=raw_w: e.tensor_tensor(lo[:], raw_w[:], hi[:], ALU.subtract), after=[m_hi, *lo_r.free(ex)])
            raw_r.release(ex, m_lo)
            for ch in range(TILES * P // CH):
                hh, hl = hh_r.buf(job), hl_r.buf(job)
                for f in range(FC):
                    sil, h = sil_r.buf(fj), h_r.buf(fj)
                    bk = []
                    for k in range(2):
                        bank = hb.buf(hbn)
                        pe.wait(*hb.free(hbn), *m_lv, m_lo, m_split)
                        parts = [(hi, xhi), (hi, xlo), (lo, xhi)]
                        for pi, (w, xx) in enumerate(parts):
                            for d in range(DC):
                                m = pe.do(lambda e, bank=bank, w=w, xx=xx, d=d, f=f, k=k, ch=ch, pi=pi: e.matmul(
                                    bank[:], w[:, k, d * F + f * P:d * F + (f + 1) * P], xx[:, d, ch * CH:(ch + 1) * CH],
                                    start=pi == 0 and d == 0, stop=pi == 2 and d == DC - 1), signal=pi == 2 and d == DC - 1)
                        bk.append((hbn, bank, m))
                        hbn += 1
                    m = act.do(lambda e, sil=sil, bank=bk[0][1]: e.activation(sil[:], bank[:], ACT.Silu), after=[bk[0][2], *sil_r.free(fj)])
                    hb.release(bk[0][0], m)
                    m = dve.do(lambda e, sil=sil, h=h, bank=bk[1][1]: e.tensor_tensor(h[:], sil[:], bank[:], ALU.mult), after=[m, bk[1][2], *h_r.free(fj)])
                    hb.release(bk[1][0], m)
                    sil_r.release(fj, m)
                    m_h = act.do(lambda e, h=h, hh=hh, f=f: e.activation(hh[:, f, :], h[:], ACT.Copy), after=[m, *hh_r.free(job)])
                    m_l = pool.do(lambda e, h=h, hh=hh, hl=hl, f=f: e.tensor_tensor(hl[:, f, :], h[:], hh[:, f, :], ALU.subtract), after=[m_h, *hl_r.free(job)])
                    h_r.release(fj, m_l)
                    fj += 1
                for i in range(CH // P):
                    tile_ = ch * (CH // P) + i
                    n, bank, free = take()
                    parts = [(hh, hi), (hh, lo), (hl, hi)]
                    for pi, (hx, w) in enumerate(parts):
                        for f in range(FC):
                            m = pe.do(lambda e, bank=bank, hx=hx, w=w, f=f, i=i, pi=pi: e.matmul(bank[:, 0:D], hx[:, f, i * P:(i + 1) * P], w[:, 2, f * D:(f + 1) * D],
                                      start=pi == 0 and f == 0, stop=pi == 2 and f == FC - 1), after=[m_l, *free], signal=pi == 2 and f == FC - 1)
                    if ex < E:
                        my = dve.do(lambda e, bank=bank, tile_=tile_, ex=ex: e.scalar_tensor_tensor(x[:, tile_, :], bank[:, 0:D], comb[:, tile_, ex:ex + 1], x[:, tile_, :], ALU.mult, ALU.add), after=[m, m_comb])
                    else:
                        my = dve.do(lambda e, bank=bank, tile_=tile_: e.tensor_tensor(x[:, tile_, :], bank[:, 0:D], x[:, tile_, :], ALU.add), after=[m])
                    work.release(n, my)
                    if ex == E:
                        st = st3_r.buf(tile_)
                        m2 = layer_norm(x[:, tile_, :], x[:, tile_, :], st[:, 8:20], my)
                        stores = sem("stores") if tile_ == 0 else stores
                        sp.dma(lambda e, tile_=tile_: e.dma_start(out[tile_ * P:(tile_ + 1) * P, :], x[:, tile_, :]), stores, after=[m2])
                hh_r.release(job, m)
                hl_r.release(job, m)
                job += 1
            hi_r.release(ex, m_lo, m)
            lo_r.release(ex, m)
        sp.wait((stores, 16 * TILES))
        block = ctx.enter_context(nc.Block())
        for name, lane in (("tensor", pe), ("scalar", act), ("vector", dve), ("gpsimd", pool), ("sync", sp)):
            def emit(e, lane=lane):
                for make in lane.queue:
                    make(e)
            {"tensor": block.tensor, "scalar": block.scalar, "vector": block.vector, "gpsimd": block.gpsimd, "sync": block.sync}[name](emit)


def kernel(**inputs):
    import concourse.bacc as bacc
    from concourse import mybir as mb
    from concourse.bass_utils import run_bass_kernel_spmd

    a = {k: np.asarray(v) for k, v in inputs.items()}
    B, L, D = a["x"].shape
    DV = a["L0_attn_wv"].shape[0]
    R = a["L0_attn_wgk1"].shape[0]
    HEADS = 4
    f32 = np.float32
    T = lambda w: np.swapaxes(w, -1, -2)
    columns = lambda v: v.reshape(-1, P).T
    s_, t_ = np.arange(P)[:, None], np.arange(P)[None, :]
    masks = [s_ == t_] + [(s_ // (2 * h) == t_ // (2 * h)) & (s_ % (2 * h) < h) & (t_ % (2 * h) >= h) for h in LEVELS if h < 32]
    n_heads = 16
    pi = np.arange(P)
    laid = {
        "x": a["x"], "ctxT": a["ctx_1024"].reshape(-1, D).T, "mask": a["mask_1x1xSxS2_if1"],
        "wqT": T(a["L0_attn_wq"]), "wkT": T(a["L0_attn_wk"]), "wvT": T(a["L0_attn_wv"]), "wgT": T(a["L0_attn_wg"]),
        "wgk1T": T(a["L0_attn_wgk1"]), "wgk2T": T(a["L0_attn_wgk2"]), "woT": T(a["L0_attn_wo"]),
        "norm_w": np.stack([a["L0_attn_n" + n] for n in ("q", "k", "v", "gk1", "g")]),
        "no_w": a["L0_attn_no"], "ngk2": a["L0_attn_ngk2"], "bgk2": columns(a["L0_attn_bgk2"]),
        "xWqT": T(a["L0_xattn_W_q"]), "xWkT": T(a["L0_xattn_W_k"]), "xWvT": T(a["L0_xattn_W_v"]), "xWoT": T(a["L0_xattn_W_o"]),
        "xbq": columns(a["L0_xattn_b_q"]), "xbk": columns(a["L0_xattn_b_k"]), "xbv": a["L0_xattn_b_v"], "xbo": a["L0_xattn_b_o"],
        "gateT": T(a["L0_ffn_gate_w"]), "gate_bias": a["L0_ffn_gate_bias"],
        "w1T": T(a["L0_ffn_w1"]), "w2T": T(a["L0_ffn_w2"]), "w3T": T(a["L0_ffn_w3"]),
        "sw1T": T(a["L0_ffn_sw1"]), "sw2T": T(a["L0_ffn_sw2"]), "sw3T": T(a["L0_ffn_sw3"]),
        "ident": np.eye(P, dtype=f32),
        "level_mask": np.stack(masks, 1).astype(np.int32),
        "inv_count": np.array([1.0 / n for n in (D * D, D * D, D * DV, D * R, D * DV, D * DV, D * R)], f32),
        "unit": np.array([(D // HEADS) ** -0.5 / 127.0] + [1.0 / 127.0] * 6, f32),
        "head_mask": (pi[:, None] // (D // n_heads) == np.arange(n_heads // (D // P))[None, :]).astype(f32),
        "lower": (np.arange(8)[None, :] < np.arange(8)[:, None]).astype(f32),
    }
    nc = bacc.Bacc("TRN2", target_bir_lowering=False, num_devices=1)
    arrays, handles = {}, {}
    for name, v in laid.items():
        v = np.ascontiguousarray(v)
        arrays[f"in_{name}"] = v
        handles[name] = nc.dram_tensor(f"in_{name}", v.shape, mb.dt.from_np(v.dtype), kind="ExternalInput").ap()
    out = nc.dram_tensor("out", (B * L, D), mb.dt.float32, kind="ExternalOutput").ap()
    decoder_layer(nc, handles, out)
    r = run_bass_kernel_spmd(nc, [arrays], core_ids=[0])
    return r.results[0]["out"].reshape(B, L, D)
```

```python
import itertools
from contextlib import ExitStack

import numpy as np

import concourse.bass as bass
from concourse import mybir

F32 = mybir.dt.float32
BF16 = mybir.dt.bfloat16
I32 = mybir.dt.int32
ALU = mybir.AluOpType
ACT = mybir.ActivationFunctionType
AX = mybir.AxisListType

P = 128
ROUND = 12582912.0
LEVELS = [1, 2, 4, 8, 16, 32, 64]


class Lane:

    def __init__(self, sem):
        self.sem, self.count, self.queue, self.met = sem, 0, [], {}

    def wait(self, *marks):
        for m in marks:
            if m is None:
                continue
            sem, value = m
            if value > self.met.get(sem.num, 0):
                self.met[sem.num] = value
                self.queue.append(lambda e, sem=sem, value=value: e.wait_ge(sem, value))

    def do(self, make, after=(), signal=True):
        self.wait(*after)
        if not signal:
            self.queue.append(make)
            return None
        self.count += 1
        self.queue.append(lambda e: make(e).then_inc(self.sem, 1))
        return (self.sem, self.count)

    def dma(self, make, sem, after=()):
        self.wait(*after)
        self.queue.append(lambda e: make(e).then_inc(sem, 16))

    def last(self):
        return (self.sem, self.count) if self.count else None


class Ring:

    def __init__(self, bufs):
        self.bufs, self.marks, self.released = bufs, [()] * len(bufs), [-1] * len(bufs)

    def buf(self, i):
        return self.bufs[i % len(self.bufs)]

    def free(self, i):
        assert i < len(self.bufs) or self.released[i % len(self.bufs)] == i - len(self.bufs), "taken before its readers are known"
        return self.marks[i % len(self.bufs)]

    def release(self, i, *marks):
        self.marks[i % len(self.bufs)], self.released[i % len(self.bufs)] = marks, i


def decoder_layer(nc, t, out):
    B, L, D = t["x"].shape
    NT = L // P
    TILES = B * NT
    DC = D // P
    DV = t["wvT"].shape[1]
    VC = DV // P
    R = t["wgk1T"].shape[1]
    HEADS = 4
    DK = D // HEADS
    DVH = DV // HEADS
    S2 = t["ctxT"].shape[1] // B
    XH = 16
    XD = D // XH
    HB = XH // 4
    E, F = t["w1T"].shape[0], t["w1T"].shape[2]
    FC = F // P
    NORMS = 5
    JQ, JK, JV, JR, JG = range(NORMS)
    assert DK == 64 and NT == 2 and DC == 2 and HB * S2 <= 512

    with ExitStack() as ctx:
        def sb(name, shape, dt=F32):
            return ctx.enter_context(nc.sbuf_tensor(name, shape, dt))

        EARLY, LATE = 29696, 16256
        early = sb("early", [P, EARLY])
        late = sb("late", [P, LATE])
        place = {"attention": [early, 0], "weights": [early, 0], "prepare": [late, 0], "cross": [late, 0],
                 "experts": [late, 0], "final": [early, 0]}
        place["cross2"] = [late, 10432]
        place["masks"] = [early, EARLY - 8 * P]

        def carve(phase, shape, dt=F32):
            words = int(np.prod(shape[1:])) * {BF16: 2, mybir.dt.int8: 1}.get(dt, 4) // 4
            area, a = place[phase]
            place[phase][1] += words
            assert a + words <= area.shape[1] and phase, (phase, a + words)
            v = area[0:shape[0], a:a + words]
            v = v.bitcast(dt) if dt != F32 else v
            names = "abcd"[:len(shape) - 1]
            if len(shape) > 2:
                v = v.rearrange(f"p ({' '.join(names)}) -> p {' '.join(names)}", **dict(zip(names, shape[1:])))
            return v

        def sem(name):
            return ctx.enter_context(nc.semaphore(name))

        pe, act, dve, pool, sp = (Lane(sem(f"{n}_done")) for n in ("pe", "act", "dve", "pool", "sp"))
        loads = {}

        def load(dst, src, name, lane=None):
            if name not in loads:
                loads[name] = [sem(f"ld_{name}"), 0]
            loads[name][1] += 16
            (lane or sp).dma(lambda e: e.dma_start(dst, src), loads[name][0])

        def loaded(name):
            return tuple(loads[name])

        def bcast(ap, n):
            a = ap.unsqueeze(1)
            return a.to_broadcast([a.shape[0], n] + list(a.shape[2:]))

        banks = [ctx.enter_context(nc.psum_tensor(f"bank{i}", [P, 512], F32)) for i in range(8)]
        class Work:
            idle = [(n, ()) for n in range(4, 8)]

            def release(self, n, *marks):
                self.idle.append((n, marks))

        work = Work()

        def take():
            n, marks = work.idle.pop(0)
            return n, banks[n], marks

        def spare():
            return len(work.idle) > 1

        x = sb("x", [P, TILES, D])
        ident = sb("ident", [P, P])
        ident_bf = sb("ident_bf", [P, P], BF16)
        ones = sb("ones", [P, P])
        level_mask = carve("attention", [P, 6, P], mybir.dt.int8)
        level_mask_raw = carve("masks", [P, 6, P], I32)
        norm_w = carve("attention", [P, NORMS, D])
        no_w = carve("attention", [P, DV])
        ngk2_w = carve("attention", [P, R])
        bgk2 = carve("attention", [P, DC])
        w_raw = carve("prepare", [P, DC * (2 * D + R + 2 * DV) + VC * D])
        w_int = carve("attention", [P, DC * (2 * D + R + 2 * DV) + VC * D], BF16)
        wgk2_raw = carve("prepare", [R, D])
        wgk2_int = carve("attention", [R, D])
        inv_count = carve("attention", [P, 7])
        unit = carve("attention", [P, 7])
        w_sums = sb("w_sums", [P, 7])
        w_mean = sb("w_mean", [P, 7])
        w_scale = sb("w_scale", [P, 7])
        w_unit = sb("w_unit", [P, 7])

        load(ident[:], t["ident"], "const")
        load(inv_count[:], t["inv_count"].partition_broadcast(P), "const")
        load(unit[:], t["unit"].partition_broadcast(P), "const")
        col, at = {}, 0
        for name, chunks, width in (("wqT", DC, D), ("wkT", DC, D), ("wvT", DC, DV), ("wgk1T", DC, R), ("wgT", DC, DV), ("woT", VC, D)):
            col[name] = (at, chunks, width)
            load(w_raw[:, at:at + chunks * width].rearrange("p (c n) -> p c n", c=chunks),
                 t[name].rearrange("(c p) n -> p c n", p=P), "w_bit", act)
            at += chunks * width
        load(wgk2_raw[:], t["wgk2T"], "w_bit", act)
        load(norm_w[:], t["norm_w"].partition_broadcast(P), "norm")
        for b in range(B):
            load(x[:, b * NT:(b + 1) * NT, :], t["x"][b].rearrange("(i p) d -> p i d", p=P), f"x{b}")
            if b == 0:
                load(level_mask_raw, t["level_mask"], "masks")
                load(no_w[:], t["no_w"].partition_broadcast(P), "attn")
                load(ngk2_w[:], t["ngk2"].partition_broadcast(P), "attn")
                load(bgk2[:], t["bgk2"], "attn")

        xw_T = {n: carve("cross2", [P, DC, D]) for n in ("xWqT", "xWkT", "xWvT", "xWoT")}
        ctxT = carve("cross2", [P, DC, B * S2])
        xbq = carve("cross2", [P, DC])
        xbk = carve("cross2", [P, DC])
        xbv = carve("cross2", [P, D])
        xbo = carve("cross2", [P, D])
        head_mask = carve("cross2", [P, XH // DC])
        mask_raw = carve("cross2", [P, NT, S2], I32)
        keep = carve("masks", [P, NT, S2])
        drop = carve("cross2", [P, NT, HB, S2])
        row = carve("cross2", [P, NT])
        for n in xw_T:
            load(xw_T[n][:], t[n].rearrange("(c p) n -> p c n", p=P), "cross")
        load(ctxT[:], t["ctxT"].rearrange("(c p) n -> p c n", p=P), "cross")
        load(xbq[:], t["xbq"], "cross")
        load(xbk[:], t["xbk"], "cross")
        load(xbv[:], t["xbv"].partition_broadcast(P), "cross")
        load(xbo[:], t["xbo"].partition_broadcast(P), "cross")
        load(head_mask[:], t["head_mask"], "cross")
        load(mask_raw[:], t["mask"].rearrange("a c (i p) k -> p (a c i) k", p=P), "cross")

        NTT = (2 * TILES * P + (P - 1) * E) // P
        xs = nc.dram_tensor("x_slots", (NTT * P, D), F32, kind="Internal").ap()
        ys = nc.dram_tensor("y_slots", (NTT * P, D), F32, kind="Internal").ap()
        zeros = sb("zeros", [P, D])
        cleared = sem("cleared")
        zero_ok = pool.do(lambda e: e.memset(zeros[:], 0.0))
        sp.dma(lambda e: e.dma_start(xs.rearrange("(k p) d -> p k d", p=P), bcast(zeros[:], NTT)), cleared, after=[zero_ok])

        ones_ok = dve.do(lambda e: e.memset(ones[:], 1.0))
        dve.do(lambda e: e.memset(w_sums[:], 0.0))
        sums_zero = dve.last()
        mask_ok = dve.do(lambda e: e.tensor_copy(level_mask[:], level_mask_raw), after=[loaded("masks")])
        act.do(lambda e: e.preload_act_table_set("natural_log_exp_and_others"), signal=False)
        ident_ok = act.do(lambda e: e.activation(ident_bf[:], ident[:], ACT.Copy), after=[loaded("const")])
        order = ["wqT", "wkT", "wvT", "wgk1T", "wgT", "woT"]

        def raw(name, buf):
            a, c, w = col[name]
            return buf[:, a:a + c * w]

        for j, n in enumerate(order):
            dve.do(lambda e, j=j, n=n: e.tensor_reduce(w_sums[:, j:j + 1], raw(n, w_raw), AX.X, ALU.add,
                                                       apply_absolute_value=True),
                   after=[loaded("w_bit"), sums_zero])
        sums = dve.do(lambda e: e.tensor_reduce(w_sums[0:R, 6:7], wgk2_raw[:], AX.X, ALU.add, apply_absolute_value=True))
        i, bank, free = take()
        total = pe.do(lambda e, bank=bank: e.matmul(bank[:, 0:7], ones[:], w_sums[:], start=True, stop=True),
                      after=[*free, sums, ones_ok])
        m = dve.do(lambda e, bank=bank: e.tensor_tensor(w_mean[:], bank[:, 0:7], inv_count[:], ALU.mult), after=[total, loaded("const")])
        work.release(i, m)
        m = dve.do(lambda e: e.tensor_scalar(w_mean[:], w_mean[:], 1e-5, None, ALU.max), after=[m])
        dve.do(lambda e: e.reciprocal(w_scale[:], w_mean[:]), after=[m])
        w_unit_ok = m = dve.do(lambda e: e.tensor_tensor(w_unit[:], w_mean[:], unit[:], ALU.mult))
        for j, n in enumerate(order + ["wgk2"]):
            src = wgk2_raw[:] if n == "wgk2" else raw(n, w_raw)
            tmp = wgk2_raw[:] if n == "wgk2" else raw(n, w_raw)
            dst = wgk2_int[:] if n == "wgk2" else raw(n, w_int)
            rows = R if n == "wgk2" else P
            s = w_scale[0:rows, j:j + 1]
            m1 = dve.do(lambda e, a=(tmp, src, s): e.tensor_scalar(a[0], a[1], a[2], 1.0, ALU.mult, ALU.min), after=[m])
            m1 = dve.do(lambda e, a=tmp: e.tensor_scalar(a, a, -1.0, ROUND, ALU.max, ALU.add), after=[m1])
            w_int_ok = dve.do(lambda e, a=(dst, tmp): e.tensor_scalar(a[0], a[1], ROUND, None, ALU.subtract), after=[m1])

        def w_chunk(name, c, a, b):
            at, _, w = col[name]
            return w_int[:, at + c * w + a:at + c * w + b]

        def rsqrt(v, tmp, out, ready):
            m = act.do(lambda e: e.activation(tmp, v, ACT.Ln), after=[ready])
            m = act.do(lambda e: e.activation(out, tmp, ACT.Exp, scale=-0.5), after=[m])
            m = dve.do(lambda e: e.tensor_tensor(tmp, out, out, ALU.mult), after=[m])
            m = dve.do(lambda e: e.tensor_tensor(tmp, tmp, v, ALU.mult), after=[m])
            m = dve.do(lambda e: e.tensor_scalar(tmp, tmp, -0.5, 1.5, ALU.mult, ALU.add), after=[m])
            return dve.do(lambda e: e.tensor_tensor(out, out, tmp, ALU.mult), after=[m])

        def ring(name, shape, n=2, dt=F32, phase=None):
            if phase:
                return Ring([carve(phase, shape, dt) for _ in range(n)])
            return Ring([sb(f"{name}{i}", shape, dt) for i in range(n)])

        def abreast(gens):
            gens = list(gens)
            while gens:
                gens = [g for g in gens if next(g, "end") != "end"]
                yield

        xn_r = ring("xn", [P, NORMS, NT * D], 1, phase="attention")
        st_r = ring("st", [P, 64], 3)
        xi_r = ring("xi", [P, NORMS, NT * D], 1, BF16, phase="attention")
        xT_r = ring("xT", [P, NORMS, DC, L], 1, BF16, phase="attention")
        sq_r = ring("sq", [P, D], 2, BF16, phase="attention")
        q_r = ring("q", [P, DC, L], phase="attention")
        k_r = ring("k", [P, DC, L], phase="attention")
        gk_r = ring("gk", [P, DC, L], phase="attention")
        v_r = ring("v", [P, NT, DV], 3, phase="attention")
        sg_r = ring("sg", [P, NT, DV], 3, phase="attention")
        ge_r = ring("ge", [P, DV], 2, phase="attention")
        z_r = ring("z", [P, NT, R], phase="attention")
        zw_r = ring("zw", [P, NT, R], phase="attention")
        zT_r = ring("zT", [R, L], phase="attention")
        S = {}

        def A1(b):
            xb = x[:, b * NT:(b + 1) * NT, :].rearrange("p i d -> p (i d)")
            xn, st, xi, xT = xn_r.buf(b), st_r.buf(b), xi_r.buf(b), xT_r.buf(b)
            wv = norm_w[:].unsqueeze(2).to_broadcast([P, NORMS, NT, D])
            m_xn = pool.do(lambda e: e.tensor_tensor(xn[:].rearrange("p j (i d) -> p j i d", i=NT), bcast(x[:, b * NT:(b + 1) * NT, :], NORMS), wv, ALU.mult),
                           after=[loaded(f"x{b}"), loaded("norm"), *xn_r.free(b)])
            for i in range(NT):
                n = b * NT + i
                act.wait(*sq_r.free(n), *st_r.free(b))
                m = act.do(lambda e, i=i, n=n: e.activation(sq_r.buf(n)[:], x[:, n, :], ACT.Square, accum_out=st[:, i:i + 1]),
                           after=[loaded(f"x{b}")])
                sq_r.release(n, m)
            yield
            m = dve.do(lambda e: e.tensor_scalar(st[:, 0:2], st[:, 0:2], 1.0 / D, 1e-8, ALU.mult, ALU.add), after=[m])
            rms = rsqrt(st[:, 0:2], st[:, 4:6], st[:, 2:4], m)
            yield
            c = st[:, 10:20]
            cv = c.rearrange("p (j i) -> p j i", i=NT)
            m = dve.do(lambda e: e.tensor_reduce(c, xn[:].rearrange("p j (i d) -> p (j i) d", i=NT), AX.X, ALU.max,
                                                 apply_absolute_value=True), after=[m_xn])
            yield
            rb = bcast(st[:, 2:4], NORMS)
            m = dve.do(lambda e: e.tensor_tensor(cv, cv, rb, ALU.mult), after=[m, rms])
            m = dve.do(lambda e: e.tensor_scalar(c, c, 1e-5, None, ALU.max), after=[m])
            s = st[:, 20:30]
            sv = s.rearrange("p (j i) -> p j i", i=NT)
            m = dve.do(lambda e: e.reciprocal(s, c), after=[m])
            m = dve.do(lambda e: e.tensor_tensor(sv, sv, rb, ALU.mult), after=[m])
            m = dve.do(lambda e: e.tensor_scalar(s, s, 127.0, None, ALU.mult), after=[m])
            u = st[:, 30:40]
            m2 = dve.do(lambda e: e.tensor_tensor(u.rearrange("p (j i) -> p j i", i=NT), cv,
                                                  w_unit[:, 0:NORMS].unsqueeze(2).to_broadcast([P, NORMS, NT]), ALU.mult), after=[w_unit_ok])
            m2 = dve.do(lambda e: e.tensor_tensor(st[:, 40:42], st[:, 30 + 2 * JK:32 + 2 * JK], st[:, 30 + 2 * JV:32 + 2 * JV], ALU.mult), after=[m2])
            scales = dve.do(lambda e: e.tensor_scalar(st[:, 42:44], st[:, 30 + 2 * JG:32 + 2 * JG], -1.0, None, ALU.mult))
            yield
            for j in range(NORMS):
                for i in range(NT):
                    a = xn[:, j, i * D:(i + 1) * D]
                    m = dve.do(lambda e, a=a, k=20 + 2 * j + i: e.tensor_scalar(a, a, st[:, k:k + 1], ROUND, ALU.mult, ALU.add), after=[m] if i + j == 0 else [])
            m_xi = dve.do(lambda e: e.tensor_scalar(xi[:], xn[:], ROUND, None, ALU.subtract), after=[m, *xi_r.free(b)])
            xn_r.release(b, m_xi)
            yield
            copied = []
            for j in range(NORMS):
                if j % 2 == 0:
                    n, bank, free = take()
                    tb = bank[:].bitcast(BF16)
                    pe.wait(m_xi, ident_ok, *free)
                o = (j % 2) * DC * L
                for c_ in range(DC):
                    for i in range(NT):
                        m = pe.do(lambda e, j=j, c_=c_, i=i, tb=tb, o=o: e.transpose(
                            tb[:, o + c_ * L + i * P:o + c_ * L + (i + 1) * P], xi[:, j, i * D + c_ * P:i * D + (c_ + 1) * P], ident_bf[:]),
                            signal=(j % 2 == 1 or j == NORMS - 1) and c_ == DC - 1 and i == NT - 1)
                if j % 2 == 1 or j == NORMS - 1:
                    if spare():
                        yield
                    j0 = j - j % 2
                    k = j - j0 + 1
                    src = tb[:, 0:k * DC * L].rearrange("p (j c l) -> p j c l", j=k, c=DC)
                    mc = act.do(lambda e, src=src, j0=j0, k=k: e.activation(xT[:, j0:j0 + k], src, ACT.Copy), after=[m, *xT_r.free(b)])
                    work.release(n, mc)
                    copied.append(mc)
                    yield
            xi_r.release(b, m)
            v, sg, z, zw, zT = (r.buf(b) for r in (v_r, sg_r, z_r, zw_r, zT_r))
            n, bank, free = take()
            for i in range(NT):
                for c_ in range(DC):
                    m = pe.do(lambda e, i=i, c_=c_, bank=bank: e.matmul(bank[:, i * R:(i + 1) * R], xT[:, JR, c_, i * P:(i + 1) * P],
                                                                        w_chunk("wgk1T", c_, 0, R), start=c_ == 0, stop=c_ == DC - 1),
                              after=[*free, copied[1], w_int_ok], signal=i == NT - 1 and c_ == DC - 1)
            if spare():
                yield
            for i in range(NT):
                mz = dve.do(lambda e, i=i, bank=bank: e.tensor_scalar(z[:, i, :], bank[:, i * R:(i + 1) * R], st[:, 30 + 2 * JR + i:31 + 2 * JR + i], None, ALU.mult),
                            after=[m, scales, *z_r.free(b)])
            work.release(n, mz)
            def project(name, j, m_in):
                n, bank, free = take()
                for e_ in range(DC):
                    for c_ in range(DC):
                        m = pe.do(lambda e, e_=e_, c_=c_, bank=bank: e.matmul(bank[:, e_ * L:(e_ + 1) * L], w_chunk(name, c_, e_ * P, (e_ + 1) * P),
                                                                              xT[:, j, c_, :], start=c_ == 0, stop=c_ == DC - 1),
                                  after=[*free, m_in], signal=e_ == DC - 1 and c_ == DC - 1)
                return n, bank[:].rearrange("p (c l) -> p c l", c=DC), m
            n, qps, m = project("wqT", JQ, copied[0])
            if spare():
                yield
            mq = act.do(lambda e: e.activation(q_r.buf(b)[:], qps, ACT.Copy), after=[m, *q_r.free(b)])
            work.release(n, mq)
            n, kps, m = project("wkT", JK, copied[0])
            if spare():
                yield
            mk = act.do(lambda e: e.activation(k_r.buf(b)[:], kps, ACT.Copy), after=[m, *k_r.free(b)])
            work.release(n, mk)
            yield
            ms, rr, tt, cc, uu = (st[:, 44 + 2 * k:46 + 2 * k] for k in range(5))
            m = dve.do(lambda e: e.tensor_tensor(zw[:], z[:], z[:], ALU.mult), after=[mz, *zw_r.free(b)])
            m = dve.do(lambda e: e.tensor_reduce(ms, zw[:], AX.X, ALU.add), after=[m])
            m = dve.do(lambda e: e.tensor_scalar(ms, ms, 1.0 / R, 1e-8, ALU.mult, ALU.add), after=[m])
            mr = rsqrt(ms, tt, rr, m)
            yield
            m = dve.do(lambda e: e.tensor_tensor(zw[:], z[:], bcast(ngk2_w[:], NT), ALU.mult), after=[loaded("attn")])
            m = dve.do(lambda e: e.tensor_reduce(cc, zw[:], AX.X, ALU.max, apply_absolute_value=True), after=[m])
            m = dve.do(lambda e: e.tensor_tensor(cc, cc, rr, ALU.mult), after=[m, mr])
            m = dve.do(lambda e: e.tensor_scalar(cc, cc, 1e-5, None, ALU.max), after=[m])
            m = dve.do(lambda e: e.reciprocal(tt, cc), after=[m])
            m = dve.do(lambda e: e.tensor_tensor(tt, tt, rr, ALU.mult), after=[m])
            m = dve.do(lambda e: e.tensor_scalar(tt, tt, 127.0, None, ALU.mult), after=[m])
            m = dve.do(lambda e: e.tensor_scalar(uu, cc, w_unit[:, 6:7], None, ALU.mult), after=[m])
            for i in range(NT):
                m = dve.do(lambda e, i=i: e.tensor_scalar(zw[:, i, :], zw[:, i, :], tt[:, i:i + 1], ROUND, ALU.mult, ALU.add), after=[m])
            for i in range(NT):
                m = dve.do(lambda e, i=i: e.tensor_scalar(zw[:, i, :], zw[:, i, :], ROUND, uu[:, i:i + 1], ALU.subtract, ALU.mult), after=[m])
            m_zw = m
            yield
            for i in range(NT):
                n, bank, free = take()
                for c_ in range(DC):
                    m = pe.do(lambda e, i=i, c_=c_, bank=bank: e.matmul(bank[:], xT[:, JV, c_, i * P:(i + 1) * P], w_chunk("wvT", c_, 0, DV), start=c_ == 0, stop=c_ == DC - 1),
                              after=[*free, copied[1]], signal=c_ == DC - 1)
                if spare():
                    yield
                mv = act.do(lambda e, i=i, bank=bank: e.activation(v[:, i, :], bank[:], ACT.Copy, scale=st[:, 40 + i:41 + i]), after=[m, scales, *v_r.free(b)])
                work.release(n, mv)
                yield
            for i in range(NT):
                n, bank, free = take()
                for c_ in range(DC):
                    m = pe.do(lambda e, i=i, c_=c_, bank=bank: e.matmul(bank[:], xT[:, JG, c_, i * P:(i + 1) * P], w_chunk("wgT", c_, 0, DV), start=c_ == 0, stop=c_ == DC - 1),
                              after=[*free, copied[2]], signal=c_ == DC - 1)
                u_ = b * NT + i
                ge = ge_r.buf(u_)
                if spare():
                    yield
                m1 = act.do(lambda e, i=i, bank=bank, ge=ge: e.activation(ge[:], bank[:], ACT.Exp, scale=st[:, 42 + i:43 + i]), after=[m, scales, *ge_r.free(u_)])
                m1 = dve.do(lambda e, ge=ge: e.tensor_scalar(ge[:], ge[:], 1.0, None, ALU.add), after=[m1])
                m1 = dve.do(lambda e, ge=ge: e.reciprocal(ge[:], ge[:]), after=[m1])
                mg = dve.do(lambda e, i=i, bank=bank, ge=ge: e.scalar_tensor_tensor(sg[:, i, :], bank[:], st[:, 30 + 2 * JG + i:31 + 2 * JG + i], ge[:], ALU.mult, ALU.mult),
                            after=[m1, m, scales, *sg_r.free(b)])
                ge_r.release(u_, mg)
                work.release(n, mg)
                yield
            n, bank, free = take()
            for i in range(NT):
                m = pe.do(lambda e, i=i, bank=bank: e.transpose(bank[0:R, i * P:(i + 1) * P], zw[:, i, :], ident[:]), after=[m_zw, *free], signal=i == NT - 1)
            z_r.release(b, m_zw)
            zw_r.release(b, m)
            if spare():
                yield
            mc = act.do(lambda e, bank=bank: e.activation(zT[:], bank[0:R, 0:L], ACT.Copy), after=[m, *zT_r.free(b)])
            work.release(n, mc)
            yield
            n, bank, free = take()
            for c_ in range(DC):
                m = pe.do(lambda e, c_=c_, bank=bank: e.matmul(bank[:, c_ * L:(c_ + 1) * L], wgk2_int[:, c_ * P:(c_ + 1) * P], zT[:], start=True, stop=True),
                          after=[mc, *free], signal=c_ == DC - 1)
            zT_r.release(b, m)
            xT_r.release(b, m)
            gk = gk_r.buf(b)
            if spare():
                yield
            mgk = act.do(lambda e, bank=bank: e.activation(gk[:], bank[:].rearrange("p (c l) -> p c l", c=DC), ACT.Copy), after=[m, *gk_r.free(b)])
            work.release(n, mgk)
            S[b] = dict(q=mq, k=mk, v=mv, g=mg, gk=mgk, scales=scales)

        gate_r = ring("gate", [P, DC, L], 2, phase="attention")
        Q_r = ring("Q", [P, DC, L], phase="attention")
        tot_r = ring("tot", [P, DC, L], 1, phase="attention")
        A_bufs = [carve("attention", [P, DC, 2, NT, P]) for _ in range(2)]
        A_r = Ring(A_bufs)
        Aoff_r = ring("Aoff", [P, DC, 2, P], 2, phase="attention")
        a_zero = []
        for a in A_bufs:
            a_zero.append(pool.do(lambda e, a=a: e.memset(a[:], 0.0)))
        level_banks = Ring([(banks[0], banks[1]), (banks[2], banks[3])])
        level_n = [0]

        def A2(b):
            q, k, gk, gate, Q, tot = (r.buf(b) for r in (q_r, k_r, gk_r, gate_r, Q_r, tot_r))
            ga = Q
            A, Aoff = A_r.buf(b), Aoff_r.buf(b)
            for c in range(DC):
                m = act.do(lambda e, c=c: e.activation(ga[:, c, :], gk[:, c, :], ACT.Abs, bias=bgk2[:, c:c + 1]), after=[S[b]["gk"], loaded("attn"), *Q_r.free(b)])
                mm = dve.do(lambda e, c=c: e.tensor_scalar(gk[:, c, :], gk[:, c, :], bgk2[:, c:c + 1], 0.0, ALU.add, ALU.min), after=[m])
            yield
            m = act.do(lambda e: e.activation(ga[:], ga[:], ACT.Exp, scale=-1.0), after=[m])
            m = act.do(lambda e: e.activation(ga[:], ga[:], ACT.Ln, bias=1.0), after=[m])
            yield
            m = dve.do(lambda e: e.tensor_tensor(gk[:], gk[:], ga[:], ALU.subtract), after=[m, mm])
            m_ga = m
            m_gate = act.do(lambda e: e.activation(gate[:], gk[:], ACT.Exp, scale=1.0 / 16.0), after=[m, *gate_r.free(b)])
            gk_r.release(b, m_gate)
            yield
            mQ = [dve.do(lambda e, c=c: e.tensor_tensor(Q[:, c, :], q[:, c, :], gate[:, c, :], ALU.mult), after=[m_gate, m_ga, S[b]["q"]]) for c in range(DC)]
            mK = [S[b]["k"]] * DC
            mT = [m_gate] * DC
            A_free = [*A_r.free(b), a_zero[b % 2]]
            for lev, h in enumerate([0] + LEVELS):
                for c in range(DC):
                    n = level_n[0]
                    level_n[0] += 1
                    pair = level_banks.buf(n)
                    queries = q if h == 0 else Q
                    pe.wait(*level_banks.free(n), mQ[c], mK[c], S[b]["q"])
                    hs = h if h >= 32 else P
                    for i in range(NT):
                        for s0 in range(0, P, 2 * h if h >= 32 else P):
                            t0 = s0 + h if h >= 32 else 0
                            for hd in range(2):
                                r0 = hd * DK
                                m = pe.do(lambda e, r0=r0, hd=hd, i=i, s0=s0, t0=t0, c=c, hs=hs, pair=pair, queries=queries: e.matmul(
                                    pair[hd][s0:s0 + hs, i * P + t0:i * P + t0 + hs],
                                    k[r0:r0 + DK, c, i * P + s0:i * P + s0 + hs], queries[r0:r0 + DK, c, i * P + t0:i * P + t0 + hs],
                                    start=True, stop=True), signal=False)
                    last = pe.queue.pop()
                    pe.count += 1
                    m_sc = (pe.sem, pe.count)
                    pe.queue.append(lambda e, last=last: last(e).then_inc(pe.sem, 1))
                    yield
                    if h < 32:
                        for hd in range(2):
                            src = pair[hd][:, 0:NT * P].rearrange("p (i t) -> p i t", i=NT)
                            mc = dve.do(lambda e, c=c, hd=hd, src=src, lev=lev: e.copy_predicated(
                                A[:, c, hd], bcast(level_mask[:, lev, :], NT), src), after=[m_sc, mask_ok, *A_free])
                    else:
                        for hd in range(2):
                            for s0 in range(0, P, 2 * h):
                                t0 = s0 + h
                                src = pair[hd][s0:s0 + h, 0:NT * P].rearrange("p (i t) -> p i t", i=NT)[:, :, t0:t0 + h]
                                mc = act.do(lambda e, c=c, hd=hd, s0=s0, t0=t0, h=h, src=src: e.activation(
                                    A[s0:s0 + h, c, hd, :, t0:t0 + h], src, ACT.Copy), after=[m_sc, *A_free])
                    level_banks.release(n, mc)
                    if h == 0:
                        yield
                        continue
                    v2 = lambda buf, w: buf[:, c, 0:2 * w * (L // (2 * w))].rearrange("p (n two w) -> p n two w", two=2, w=w)
                    nb = L // (2 * h)
                    at_h = L - 2 * L // h
                    T = gate[:, c, :] if h == 1 else tot[:, c, at_h:at_h + 2 * nb]
                    T = T.rearrange("p (n two) -> p n two", two=2)
                    Qv, Kv = v2(Q, h), v2(k, h)
                    if h < P:
                        mQ[c] = dve.do(lambda e, Qv=Qv, T=T, h=h, nb=nb: e.tensor_tensor(
                            Qv[:, :, 1], Qv[:, :, 1], T[:, :, 0:1].to_broadcast([P, nb, h]), ALU.mult), after=[m_sc, mT[c]])
                        mK[c] = pool.do(lambda e, Kv=Kv, T=T, h=h, nb=nb: e.tensor_tensor(
                            Kv[:, :, 0], Kv[:, :, 0], T[:, :, 1:2].to_broadcast([P, nb, h]), ALU.mult), after=[m_sc, mT[c]])
                        if h < 64:
                            mT[c] = dve.do(lambda e, T=T, c=c, nb=nb: e.tensor_tensor(tot[:, c, L - 2 * nb:L - nb], T[:, :, 0], T[:, :, 1], ALU.mult),
                                           after=[mT[c], *tot_r.free(b)])
                    yield
            for c in range(DC):
                n = level_n[0]
                level_n[0] += 1
                pair = level_banks.buf(n)
                pe.wait(*level_banks.free(n), mQ[c], mK[c])
                for hd in range(2):
                    r0 = hd * DK
                    m = pe.do(lambda e, hd=hd, r0=r0, c=c, pair=pair: e.matmul(pair[hd][:, 0:P], k[r0:r0 + DK, c, 0:P], Q[r0:r0 + DK, c, P:2 * P], start=True, stop=True), signal=hd == 1)
                yield
                for hd in range(2):
                    m_off = act.do(lambda e, hd=hd, c=c, pair=pair: e.activation(Aoff[:, c, hd, :], pair[hd][:, 0:P], ACT.Copy), after=[m, *Aoff_r.free(b)])
                level_banks.release(n, m_off)
            q_r.release(b, m)
            k_r.release(b, m)
            Q_r.release(b, m)
            tot_r.release(b, mQ[1], mK[1])
            gate_r.release(b, mQ[1], mK[1])
            S[b].update(A=[dve.last(), act.last()], off=m_off)

        y_r = ring("y", [P, DV], 2, phase="attention")
        yw_r = ring("yw", [P, DV], 2, phase="attention")
        yi_r = ring("yi", [P, DV], 2, BF16, phase="attention")
        yT_r = ring("yT", [P, VC, P], 2, BF16, phase="attention")
        st3_r = ring("st3", [P, 32], 2)

        def layer_norm(dst, src, st, ready):
            m = dve.do(lambda e: e.bn_stats(st[:, 0:6], src), after=[ready])
            m = dve.do(lambda e: e.bn_aggr(st[:, 6:8], st[:, 0:6]), after=[m])
            m = dve.do(lambda e: e.tensor_scalar(st[:, 7:8], st[:, 7:8], 1e-5, None, ALU.add), after=[m])
            yield
            m = rsqrt(st[:, 7:8], st[:, 8:9], st[:, 9:10], m)
            yield
            return dve.do(lambda e: e.tensor_scalar(dst, src, st[:, 6:7], st[:, 9:10], ALU.subtract, ALU.mult), after=[m])

        def A3(b):
            readers = [None] * NT
            yield from abreast([A3_tile(b, i, readers) for i in range(NT)])
            for r, k in ((v_r, 0), (A_r, 0), (Aoff_r, 0), (sg_r, 1), (st_r, 2)):
                r.release(b, *[marks[k] for marks in readers])
            S[b]["x1"] = [marks[2] for marks in readers]

        def A3_tile(b, i, readers):
                st1, v, sg, A, Aoff = (r.buf(b) for r in (st_r, v_r, sg_r, A_r, Aoff_r))
                u = b * NT + i
                y, yw, yi, yT, st = (r.buf(u) for r in (y_r, yw_r, yi_r, yT_r, st3_r))
                n, bank, free = take()
                pe.wait(*free, *S[b]["A"], S[b]["off"], S[b]["v"])
                for c in range(DC):
                    for hd in range(2):
                        cols = slice((2 * c + hd) * DVH, (2 * c + hd + 1) * DVH)
                        m = pe.do(lambda e, c=c, hd=hd, i=i, cols=cols, bank=bank: e.matmul(bank[:, cols], A[:, c, hd, i, :], v[:, i, cols], start=True, stop=i == 0), signal=i == 0 and c * hd == 1)
                        if i == 1:
                            m = pe.do(lambda e, c=c, hd=hd, cols=cols, bank=bank: e.matmul(bank[:, cols], Aoff[:, c, hd, :], v[:, 0, cols], start=False, stop=True), signal=c * hd == 1)
                m_av = m
                if spare():
                    yield
                my = dve.do(lambda e, i=i, y=y, bank=bank: e.scalar_tensor_tensor(y[:], bank[:], st1[:, 30 + 2 * JQ + i:31 + 2 * JQ + i], sg[:, i, :], ALU.mult, ALU.mult),
                            after=[m, S[b]["g"], *y_r.free(u)])
                work.release(n, my)
                yield
                m_w = pool.do(lambda e, yw=yw, y=y: e.tensor_tensor(yw[:], y[:], no_w[:], ALU.mult), after=[my, loaded("attn"), *yw_r.free(u)])
                m_s = act.do(lambda e, i=i, y=y, st=st: e.activation(sg[:, i, :], y[:], ACT.Square, accum_out=st[:, 0:1]), after=[my, *st3_r.free(u)])
                y_r.release(u, m_w, m_s)
                yield
                m = dve.do(lambda e, st=st: e.tensor_scalar(st[:, 0:1], st[:, 0:1], 1.0 / DV, 1e-8, ALU.mult, ALU.add), after=[m_s])
                m_r = rsqrt(st[:, 0:1], st[:, 1:2], st[:, 2:3], m)
                yield
                m = dve.do(lambda e, st=st, yw=yw: e.tensor_reduce(st[:, 3:4], yw[:], AX.X, ALU.max, apply_absolute_value=True), after=[m_w])
                m = dve.do(lambda e, st=st: e.tensor_scalar(st[:, 3:4], st[:, 3:4], st[:, 2:3], 1e-5, ALU.mult, ALU.max), after=[m, m_r])
                m = dve.do(lambda e, st=st: e.reciprocal(st[:, 4:5], st[:, 3:4]), after=[m])
                m = dve.do(lambda e, st=st: e.tensor_scalar(st[:, 4:5], st[:, 4:5], st[:, 2:3], 127.0, ALU.mult, ALU.mult), after=[m])
                dve.do(lambda e, st=st: e.tensor_scalar(st[:, 5:6], st[:, 3:4], w_unit[:, 5:6], None, ALU.mult))
                m = dve.do(lambda e, st=st, yw=yw: e.tensor_scalar(yw[:], yw[:], st[:, 4:5], ROUND, ALU.mult, ALU.add), after=[m])
                m_yi = dve.do(lambda e, yi=yi, yw=yw: e.tensor_scalar(yi[:], yw[:], ROUND, None, ALU.subtract), after=[m, *yi_r.free(u)])
                yw_r.release(u, m_yi)
                yield
                n, bank, free = take()
                tb = bank[:].bitcast(BF16)
                for c in range(VC):
                    m = pe.do(lambda e, c=c, tb=tb, yi=yi: e.transpose(tb[:, c * P:(c + 1) * P], yi[:, c * P:(c + 1) * P], ident_bf[:]), after=[m_yi, *free], signal=c == VC - 1)
                yi_r.release(u, m)
                if spare():
                    yield
                mc = act.do(lambda e, tb=tb, yT=yT: e.activation(yT[:], tb[:, 0:VC * P].rearrange("p (c t) -> p c t", c=VC), ACT.Copy), after=[m, *yT_r.free(u)])
                work.release(n, mc)
                yield
                n, bank, free = take()
                for c in range(VC):
                    m = pe.do(lambda e, c=c, bank=bank, yT=yT: e.matmul(bank[:, 0:D], yT[:, c, :], w_chunk("woT", c, 0, D), start=c == 0, stop=c == VC - 1), after=[mc, *free], signal=c == VC - 1)
                yT_r.release(u, m)
                if spare():
                    yield
                m = dve.do(lambda e, u=u, bank=bank, st=st: e.scalar_tensor_tensor(x[:, u, :], bank[:, 0:D], st[:, 5:6], x[:, u, :], ALU.mult, ALU.add), after=[m])
                work.release(n, m)
                m = yield from layer_norm(x[:, u, :], x[:, u, :], st[:, 8:20], m)
                st3_r.release(u, m)
                readers[i] = (m_av, m_s, m)

        xk = carve("cross2", [P, DC, B * S2])
        xkb_r = ring("xkb", [P, DC, XH // DC, S2], 1, phase="cross")
        xv_r = ring("xv", [S2, XH, XD + 1], phase="cross")
        x1T_r = ring("x1T", [P, DC, L], 1, phase="cross")
        xq_r = ring("xq", [P, DC, L], phase="cross")
        sc_r = ring("sc", [P, XH, S2], 2, phase="cross")
        mx_r = ring("mx", [P, XH], phase="cross")
        pT_r = ring("pT", [S2, XH // 2, P], 3, phase="cross")
        co_r = ring("co", [P, D], phase="cross")
        coT_r = ring("coT", [P, DC, P], phase="cross")
        xr_r = ring("xr", [P, D], phase="cross")
        stx_r = ring("stx", [P, 12])

        xv_one = [dve.do(lambda e, a=a: e.memset(a[:], 1.0)) for a in xv_r.bufs]
        m = dve.do(lambda e: e.tensor_copy(keep[:], mask_raw[:]), after=[loaded("cross")])
        m = dve.do(lambda e: e.tensor_scalar(keep[:], keep[:], 0.0, None, ALU.is_equal), after=[m])
        m = dve.do(lambda e: e.tensor_reduce(row[:], keep[:], AX.X, ALU.min), after=[m])
        m = dve.do(lambda e: e.tensor_scalar(row[:], row[:], -1.0, 1.0, ALU.mult, ALU.add), after=[m])
        for i in range(NT):
            m_mask = dve.do(lambda e, i=i: e.tensor_scalar(drop[:, i], bcast(keep[:, i, :], HB), -1e9, None, ALU.mult), after=[m])
        half = B * S2 // 2
        for c in range(DC):
            for hf in range(2):
                n, bank, free = take()
                for d in range(DC):
                    m = pe.do(lambda e, c=c, d=d, hf=hf, bank=bank: e.matmul(bank[:, 0:half], xw_T["xWkT"][:, d, c * P:(c + 1) * P], ctxT[:, d, hf * half:(hf + 1) * half],
                                                                            start=d == 0, stop=d == DC - 1), after=[loaded("cross"), *free], signal=d == DC - 1)
                m_xk = act.do(lambda e, c=c, hf=hf, bank=bank: e.activation(xk[:, c, hf * half:(hf + 1) * half], bank[:, 0:half], ACT.Identity, bias=xbk[:, c:c + 1]), after=[m, loaded("cross")])
                work.release(n, m_xk)

        next_pT = [0]

        def X(b):
            xkb, xv, x1T, xq = (r.buf(b) for r in (xkb_r, xv_r, x1T_r, xq_r))
            NHC = XH // DC
            for c in range(DC):
                m_kb = pool.do(lambda e, c=c: e.tensor_tensor(xkb[:, c], bcast(xk[:, c, b * S2:(b + 1) * S2], NHC),
                                                              head_mask[:].unsqueeze(2).to_broadcast([P, NHC, S2]), ALU.mult), after=[m_xk, loaded("cross"), *xkb_r.free(b)])
            n, bank, free = take()
            for d in range(DC):
                m = pe.do(lambda e, d=d, bank=bank: e.matmul(bank[0:S2, 0:D], ctxT[:, d, b * S2:(b + 1) * S2], xw_T["xWvT"][:, d, :], start=d == 0, stop=d == DC - 1), after=[loaded("cross"), *free], signal=d == DC - 1)
            yield
            m_xv = dve.do(lambda e, bank=bank: e.tensor_tensor(xv[:, :, 0:XD], bank[0:S2, 0:D].rearrange("p (h d) -> p h d", h=XH), xbv[0:S2, :].rearrange("p (h d) -> p h d", h=XH), ALU.add),
                          after=[m, loaded("cross"), *xv_r.free(b), xv_one[b % 2]])
            work.release(n, m_xv)
            n, bank, free = take()
            for c in range(DC):
                for i in range(NT):
                    m = pe.do(lambda e, c=c, i=i, bank=bank: e.transpose(bank[:, c * L + i * P:c * L + (i + 1) * P], x[:, b * NT + i, c * P:(c + 1) * P], ident[:]),
                              after=[*S[b]["x1"], *free, loaded("const")], signal=c * i == 1)
            if spare():
                yield
            mc = act.do(lambda e, bank=bank: e.activation(x1T[:], bank[:].rearrange("p (c l) -> p c l", c=DC), ACT.Copy), after=[m, *x1T_r.free(b)])
            work.release(n, mc)
            yield
            n, bank, free = take()
            for c in range(DC):
                for d in range(DC):
                    m = pe.do(lambda e, c=c, d=d, bank=bank: e.matmul(bank[:, c * L:(c + 1) * L], xw_T["xWqT"][:, d, c * P:(c + 1) * P], x1T[:, d, :], start=d == 0, stop=d == DC - 1),
                              after=[mc, *free], signal=c * d == 1)
            x1T_r.release(b, m)
            if spare():
                yield
            for c in range(DC):
                m_q = dve.do(lambda e, c=c, bank=bank: e.tensor_scalar(xq[:, c, :], bank[:, c * L:(c + 1) * L], xbq[:, c:c + 1], float(XD) ** -0.5, ALU.add, ALU.mult), after=[m, *xq_r.free(b)])
            work.release(n, m_q)
            readers = [None] * NT
            yield from abreast([X_tile(b, i, readers, m_q, m_kb, m_xv) for i in range(NT)])
            for r, k in ((xkb_r, 0), (xq_r, 0), (xv_r, 1)):
                r.release(b, *[marks[k] for marks in readers])
            S[b]["x2"] = [marks[2] for marks in readers]

        def X_tile(b, i, readers, m_q, m_kb, m_xv):
                xkb, xv, xq = (r.buf(b) for r in (xkb_r, xv_r, xq_r))
                u = b * NT + i
                sc, mx, pT, co, coT, xr, st = (r.buf(u) for r in (sc_r, mx_r, pT_r, co_r, coT_r, xr_r, stx_r))
                for c in range(DC):
                    for g_ in range(XH // DC // HB):
                        h0 = g_ * HB
                        hh = c * (XH // DC) + h0
                        n, bank, free = take()
                        m = pe.do(lambda e, c=c, i=i, h0=h0, bank=bank: e.matmul(bank[:, 0:HB * S2], xq[:, c, i * P:(i + 1) * P], xkb[:, c, h0:h0 + HB, :].rearrange("p h k -> p (h k)"), start=True, stop=True),
                                  after=[m_q, m_kb, *free])
                        if spare():
                            yield
                        m_k = dve.do(lambda e, i=i, hh=hh, bank=bank, sc=sc: e.scalar_tensor_tensor(
                            sc[:, hh:hh + HB, :].rearrange("p h k -> p (h k)"), bank[:, 0:HB * S2], row[:, i:i + 1], drop[:, i].rearrange("p h k -> p (h k)"), ALU.mult, ALU.add),
                                     after=[m, m_mask, *sc_r.free(u)])
                        work.release(n, m_k)
                        yield
                m_scores = m
                yield
                m = m_k
                m = dve.do(lambda e, mx=mx, sc=sc: e.tensor_reduce(mx[:], sc[:], AX.X, ALU.max), after=[m, *mx_r.free(u)])
                m = pool.do(lambda e, sc=sc, mx=mx: e.tensor_tensor(sc[:], sc[:], mx[:].unsqueeze(2).to_broadcast([P, XH, S2]), ALU.subtract), after=[m])
                yield
                m_e = act.do(lambda e, sc=sc: e.activation(sc[:], sc[:], ACT.Exp), after=[m])
                for half_ in range(2):
                    n_pT = next_pT[0]
                    next_pT[0] += 1
                    pT = pT_r.buf(n_pT)
                    pT_free = pT_r.free(n_pT)
                    h0 = half_ * (XH // 2)
                    for g_ in range(2):
                        n, bank, free = take()
                        for h in range(4):
                            m = pe.do(lambda e, h=h, g_=g_, bank=bank, h0=h0: e.transpose(bank[0:S2, h * P:(h + 1) * P], sc[:, h0 + 4 * g_ + h, :], ident[:]), after=[m_e, *free], signal=h == 3)
                        m_p = act.do(lambda e, g_=g_, bank=bank, pT=pT: e.activation(pT[:, 4 * g_:4 * g_ + 4, :], bank[0:S2, :].rearrange("p (h t) -> p h t", h=4), ACT.Copy), after=[m, *pT_free])
                        work.release(n, m_p)
                    if half_:
                        sc_r.release(u, m)
                    n, bank, free = take()
                    for h in range(XH // 2):
                        m = pe.do(lambda e, h=h, bank=bank, pT=pT, h0=h0: e.matmul(bank[:, h * (XD + 1):(h + 1) * (XD + 1)], pT[:, h, :], xv[:, h0 + h, :], start=True, stop=True), after=[m_p, m_xv, *free], signal=h == XH // 2 - 1)
                    pT_r.release(n_pT, m)
                    m_av = m
                    if spare():
                        yield
                    ov = bank[:, 0:XH // 2 * (XD + 1)].rearrange("p (h d) -> p h d", h=XH // 2)
                    mxh = mx[:, h0:h0 + XH // 2]
                    m = dve.do(lambda e, mxh=mxh, ov=ov: e.reciprocal(mxh, ov[:, :, XD]), after=[m])
                    m_co = dve.do(lambda e, mxh=mxh, ov=ov, h0=h0: e.tensor_tensor(co[:, h0 * XD:(h0 + XH // 2) * XD].rearrange("p (h d) -> p h d", d=XD), ov[:, :, 0:XD],
                                                                                mxh.unsqueeze(2).to_broadcast([P, XH // 2, XD]), ALU.mult), after=[m, *co_r.free(u)])
                    work.release(n, m_co)
                    yield
                mx_r.release(u, m_co)
                n, bank, free = take()
                for c in range(DC):
                    m = pe.do(lambda e, c=c, bank=bank, co=co: e.transpose(bank[:, c * P:(c + 1) * P], co[:, c * P:(c + 1) * P], ident[:]), after=[m_co, *free], signal=c == DC - 1)
                co_r.release(u, m)
                if spare():
                    yield
                mc = act.do(lambda e, bank=bank, coT=coT: e.activation(coT[:], bank[:, 0:DC * P].rearrange("p (c t) -> p c t", c=DC), ACT.Copy), after=[m, *coT_r.free(u)])
                work.release(n, mc)
                yield
                n, bank, free = take()
                for c in range(DC):
                    m = pe.do(lambda e, c=c, bank=bank, coT=coT: e.matmul(bank[:, 0:D], coT[:, c, :], xw_T["xWoT"][:, c, :], start=c == 0, stop=c == DC - 1), after=[mc, *free], signal=c == DC - 1)
                coT_r.release(u, m)
                m_xr = pool.do(lambda e, u=u, xr=xr: e.tensor_tensor(xr[:], x[:, u, :], xbo[:], ALU.add), after=[*S[b]["x1"], loaded("cross"), *xr_r.free(u)])
                if spare():
                    yield
                m = dve.do(lambda e, xr=xr, bank=bank: e.tensor_tensor(xr[:], bank[:, 0:D], xr[:], ALU.add), after=[m, m_xr])
                work.release(n, m)
                m = yield from layer_norm(x[:, u, :], xr[:], st[:, 0:12], m)
                xr_r.release(u, m)
                stx_r.release(u, m)
                readers[i] = (m_scores, m_av, m)

        turns = {}

        def weave(stages):
            live = [[name, g, 0] for name, g in stages]
            while live:
                it = min(live, key=lambda v: (v[2] + 1) / turns.get(v[0], 40))
                it[2] += 1
                if next(it[1], "end") == "end":
                    turns[it[0]] = it[2]
                    live.remove(it)

        gateT = sb("gateT", [P, DC, E])
        gate_b = sb("gate_b", [P, E])
        load(gateT[:], t["gateT"].rearrange("(c p) e -> p c e", p=P), "router")
        load(gate_b[:], t["gate_bias"].partition_broadcast(P), "router")
        lg = sb("lg", [P, TILES, E])
        lg_max = sb("lg_max", [P, TILES])
        x2T_r = ring("x2T", [P, DC, L], 1)

        def Rt(b):
            x2T = x2T_r.buf(b)
            n, bank, free = take()
            for c in range(DC):
                for i in range(NT):
                    m = pe.do(lambda e, c=c, i=i, b=b, bank=bank: e.transpose(bank[:, c * L + i * P:c * L + (i + 1) * P], x[:, b * NT + i, c * P:(c + 1) * P], ident[:]),
                              after=[*S[b]["x2"], *free], signal=c * i == 1)
            if spare():
                yield
            bv = bank[:].rearrange("p (c l) -> p c l", c=DC)
            mc = act.do(lambda e, bv=bv, x2T=x2T: e.activation(x2T[:], bv, ACT.Copy), after=[m, *x2T_r.free(b)])
            work.release(n, mc)
            yield
            n, bank, free = take()
            for i in range(NT):
                for d in range(DC):
                    m = pe.do(lambda e, i=i, d=d, x2T=x2T, bank=bank: e.matmul(bank[:, i * E:(i + 1) * E], x2T[:, d, i * P:(i + 1) * P], gateT[:, d, :], start=d == 0, stop=d == DC - 1),
                              after=[mc, loaded("router"), *free], signal=i * d == 1)
            x2T_r.release(b, m)
            if spare():
                yield
            scores = bank[:, 0:NT * E].rearrange("p (i n) -> p i n", i=NT)
            lgb, mxb = lg[:, b * NT:(b + 1) * NT, :], lg_max[:, b * NT:(b + 1) * NT]
            m = dve.do(lambda e: e.tensor_reduce(mxb, scores, AX.X, ALU.max), after=[m])
            m = dve.do(lambda e: e.tensor_tensor(lgb, scores, mxb.unsqueeze(2).to_broadcast([P, NT, E]), ALU.subtract), after=[m])
            work.release(n, m)
            S["router"] = (act.do(lambda e: e.activation(lgb, lgb, ACT.Exp), after=[m]),)

        CW = DC * F
        WX = 3 * 2 * CW
        w_area = carve("weights", [P, (3 * (E + 1) + 2) * CW])
        w_bf = w_area.bitcast(BF16)
        HI, LO = 0, CW

        def w_part(number, k, part, a, n):
            return w_bf[:, bass.ds(number * WX + k * 2 * CW + part + a, n)]

        split = {}

        def W(_):
            sp.wait(*early_over)
            sources = [t["sw1T"], t["sw3T"], t["sw2T"]] + [t[w][ex] for ex in range(E) for w in ("w1T", "w3T", "w2T")]
            raw_w = [w_area[:, (q + 2) * CW:(q + 3) * CW] for q in range(len(sources))]
            for q, src in enumerate(sources):
                load(raw_w[q].rearrange("p (c n) -> p c n", c=src.shape[0] // P), src.rearrange("(c p) n -> p c n", p=P), f"weights{q}")
            done = []
            for q in range(len(sources)):
                hi, lo = (w_bf[:, q * 2 * CW + part:q * 2 * CW + part + CW] for part in (HI, LO))
                m = act.do(lambda e, q=q, hi=hi: e.activation(hi, raw_w[q], ACT.Copy), after=[loaded(f"weights{q}"), *early_over, *done[max(0, q - 2):q - 1]])
                m = (dve if q % 2 else pool).do(lambda e, q=q, hi=hi, lo=lo: e.tensor_tensor(lo, raw_w[q], hi, ALU.subtract), after=[m])
                done.append(m)
                split.setdefault(q // 3, []).append(m)
                yield

        for step in range(B + 3):
            stages = [(name, stage(step - late_by)) for name, stage, late_by in (("R", Rt, 4), ("X", X, 3), ("A3", A3, 2), ("A2", A2, 1), ("A1", A1, 0))
                      if 0 <= step - late_by < B]
            if step == B + 2:
                early_over = [lane.last() for lane in (pe, act, dve, pool)]
                stages.append(("W", W(0)))
            weave(stages)
        late_over = [lane.last() for lane in (pe, act, dve, pool)]
        for _ in Rt(B - 1):
            pass

        lower = carve("experts", [P, E, E])
        cm = carve("experts", [P, TILES, E, E])
        bi, first, second, sel, incl, incl2, pos = (carve("experts", [P, TILES, E]) for _ in range(7))
        rt = carve("experts", [P, TILES])
        nt8, nt8b, n8 = (carve("experts", [P, E]) for _ in range(3))
        before = carve("experts", [P, P])
        tile_no = carve("experts", [P, NTT])
        tile_cmp = carve("experts", [P, NTT, E])
        tile_e = carve("experts", [P, NTT])
        tile_ex = sb("tile_ex", [P, NTT], I32)
        posf = [carve("experts", [P, TILES]) for _ in range(2)]
        slot = [sb(f"slot{k}", [P, TILES], I32) for k in range(2)]
        weight = [sb(f"weight{k}", [P, TILES]) for k in range(2)]
        for lane in (act, dve, pool, sp):
            lane.wait(*late_over)
        load(lower, t["lower"].rearrange("a b -> (a b)").partition_broadcast(P).rearrange("p (a b) -> p a b", a=E), "routing")
        load(before, t["before"], "routing")
        load(tile_no, t["tile_no"].partition_broadcast(P), "routing")
        def running_sum(a, b, n, ready):
            m, d = ready, 1
            while d < n:
                dve.do(lambda e, a=a, b=b, d=d: e.tensor_copy(b[:, 0:d], a[:, 0:d]), after=[m])
                m = dve.do(lambda e, a=a, b=b, d=d: e.tensor_tensor(b[:, d:], a[:, d:], a[:, 0:n - d], ALU.add), after=[m])
                a, b, d = b, a, 2 * d
            return a, m

        scattered = sem("scattered")

        def route():
            rb = rt.unsqueeze(2).to_broadcast([P, TILES, E])
            m = dve.do(lambda e: e.tensor_reduce(rt, lg[:], AX.X, ALU.add), after=S["router"])
            yield
            m = dve.do(lambda e: e.reciprocal(rt, rt), after=[m])
            yield
            m = dve.do(lambda e: e.tensor_tensor(lg[:], lg[:], rb, ALU.mult), after=[m])
            yield
            m = dve.do(lambda e: e.tensor_tensor(bi, lg[:], bcast(gate_b[:], TILES), ALU.add), after=[m, loaded("router")])
            yield
            mine = bi.unsqueeze(3).to_broadcast([P, TILES, E, E])
            other = bi.unsqueeze(2).to_broadcast([P, TILES, E, E])
            m = dve.do(lambda e: e.tensor_tensor(cm, other, mine, ALU.is_gt), after=[m])
            yield
            m = dve.do(lambda e: e.tensor_reduce(incl, cm, AX.X, ALU.add), after=[m])
            yield
            m = dve.do(lambda e: e.tensor_tensor(cm, other, mine, ALU.is_equal), after=[m])
            yield
            m = dve.do(lambda e: e.tensor_tensor(cm, cm, bcast(lower, TILES), ALU.mult), after=[m, loaded("routing")])
            yield
            m = dve.do(lambda e: e.tensor_reduce(pos, cm, AX.X, ALU.add), after=[m])
            yield
            m = dve.do(lambda e: e.tensor_tensor(pos, pos, incl, ALU.add), after=[m])
            yield
            dve.do(lambda e: e.tensor_scalar(first, pos, 0.0, None, ALU.is_equal), after=[m])
            dve.do(lambda e: e.tensor_scalar(second, pos, 1.0, None, ALU.is_equal))
            m_sel = dve.do(lambda e: e.tensor_scalar(sel, pos, 1.5, None, ALU.is_lt))
            flat = lambda v: v.rearrange("p i n -> p (i n)")
            n, bank, free = take()
            pe.do(lambda e, bank=bank: e.matmul(bank[:, 0:P], before, flat(sel), start=True, stop=True), after=[m_sel, *free, loaded("routing")], signal=False)
            m_cnt = pe.do(lambda e, bank=bank: e.matmul(bank[:, P:2 * P], ones[:], flat(sel), start=True, stop=True))
            pre, tot_t = bank[:, 0:P].rearrange("p (i n) -> p i n", i=TILES), bank[:, P:2 * P].rearrange("p (i n) -> p i n", i=TILES)

            m = dve.do(lambda e: e.tensor_copy(incl, tot_t), after=[m_cnt])
            yield
            sums, m = running_sum(incl, incl2, TILES, m)
            counts = sums[:, TILES - 1, :]
            m1 = dve.do(lambda e: e.tensor_scalar(n8, counts, 1.0 / P, (P - 1.0) / P - 0.498, ALU.mult, ALU.add), after=[m])
            yield
            m1 = dve.do(lambda e: e.tensor_scalar(n8, n8, ROUND, None, ALU.add), after=[m1])
            yield
            m1 = dve.do(lambda e: e.tensor_scalar(n8, n8, ROUND, None, ALU.subtract), after=[m1])
            yield
            m1 = dve.do(lambda e: e.tensor_copy(nt8, n8), after=[m1])
            yield
            ends, m1 = running_sum(nt8, nt8b, E, m1)
            m2 = dve.do(lambda e: e.tensor_tensor(tile_cmp, tile_no.unsqueeze(2).to_broadcast([P, NTT, E]), bcast(ends, NTT), ALU.is_ge), after=[m1, loaded("routing")])
            yield
            m2 = dve.do(lambda e: e.tensor_reduce(tile_e, tile_cmp, AX.X, ALU.add), after=[m2])
            yield
            m2 = dve.do(lambda e: e.tensor_scalar(tile_e, tile_e, E - 1.0, None, ALU.min), after=[m2])
            yield
            m_ex = dve.do(lambda e: e.tensor_copy(tile_ex[:], tile_e), after=[m2])
            m = dve.do(lambda e: e.tensor_tensor(n8, ends, n8, ALU.subtract), after=[m1])
            yield
            m = dve.do(lambda e: e.tensor_scalar(n8, n8, float(P), None, ALU.mult), after=[m])
            yield
            m = dve.do(lambda e: e.tensor_tensor(pos, sums, tot_t, ALU.subtract), after=[m])
            yield
            m = dve.do(lambda e: e.tensor_tensor(pos, pos, pre, ALU.add), after=[m])
            yield
            work.release(n, m)
            m = dve.do(lambda e: e.tensor_tensor(pos, pos, bcast(n8, TILES), ALU.add), after=[m])
            yield
            for k, onehot in enumerate((first, second)):
                cmk = cm[:, :, k, :]
                ma = dve.do(lambda e, o=onehot, c=cmk: e.tensor_tensor(c, pos, o, ALU.mult), after=[m])
                ma = dve.do(lambda e, k=k, c=cmk: e.tensor_reduce(posf[k], c, AX.X, ALU.add), after=[ma])
                m_slot = dve.do(lambda e, k=k: e.tensor_copy(slot[k][:], posf[k]), after=[ma])
            m_wgt = []
            for k, onehot in enumerate((first, second)):
                cmk = cm[:, :, 2 + k, :]
                ma = dve.do(lambda e, o=onehot, c=cmk: e.tensor_tensor(c, lg[:], o, ALU.mult), after=[m])
                m_wgt = dve.do(lambda e, k=k, c=cmk: e.tensor_reduce(weight[k][:], c, AX.X, ALU.add), after=[ma])
            for i in range(TILES):
                for k in range(2):
                    pool.dma(lambda e, i=i, k=k: e.indirect_dma_start(xs, bass.IndirectOffsetOnAxis(slot[k][:, i:i + 1], 0), x[:, i, :], None), scattered,
                             after=[m_slot, (cleared, 16), *S[i // NT]["x2"]])
            S["scattered"] = m_ex, m_wgt

        CH = 256
        xch_r = ring("xch", [P, DC, CH], 2, BF16, phase="experts")
        xcl_r = ring("xcl", [P, DC, CH], 2, BF16, phase="experts")
        acc = carve("experts", [P, TILES, D])
        sil_r = ring("sil", [P, F], phase="experts")
        h_r = ring("h", [P, F], phase="experts")
        hh_r = ring("hh", [P, FC, CH], 2, BF16, phase="experts")
        hl_r = ring("hl", [P, FC, CH], 2, BF16, phase="experts")
        hb = Ring(banks[0:4])
        hb_before = level_banks.marks[0] + level_banks.marks[1]
        act.do(lambda e: e.preload_act_table_set("silu_and_others"), signal=False)

        def two_parts(n, bank, hi, lo, ready, hi_free, lo_free):
            bv = bank[:, 0:DC * hi.shape[2]].rearrange("p (c t) -> p c t", c=DC)
            mh = act.do(lambda e: e.activation(hi, bv, ACT.Copy), after=[ready, *hi_free])
            ml = dve.do(lambda e: e.tensor_tensor(lo, bv, hi, ALU.subtract), after=[mh, *lo_free])
            work.release(n, ml)
            return ml

        x_parts = {}

        def shared_x(job):
            n, bank, free = take()
            for c in range(DC):
                for i in range(CH // P):
                    m = pe.do(lambda e, c=c, i=i: e.transpose(bank[:, c * CH + i * P:c * CH + (i + 1) * P], x[:, job * (CH // P) + i, c * P:(c + 1) * P], ident[:]),
                              after=[*free], signal=c == DC - 1 and i == CH // P - 1)
            x_parts[job] = two_parts(n, bank, xch_r.buf(job), xcl_r.buf(job), m, xch_r.free(job), xcl_r.free(job))

        def shared_h(job, f):
            fj = job * FC + f
            sil, h, hh, hl = sil_r.buf(fj), h_r.buf(fj), hh_r.buf(job), hl_r.buf(job)
            got = []
            for k in range(2):
                n = 2 * fj + k
                bank = hb.buf(n)
                pe.wait(*hb.free(n), *hb_before, *split[0], x_parts[job])
                for pi, (part, xx) in enumerate([(HI, xch_r.buf(job)), (HI, xcl_r.buf(job)), (LO, xch_r.buf(job))]):
                    for d in range(DC):
                        m = pe.do(lambda e, bank=bank, part=part, xx=xx, d=d, k=k, pi=pi: e.matmul(
                            bank[:, 0:CH], w_part(0, k, part, d * F + f * P, P), xx[:, d, :], start=pi == 0 and d == 0, stop=pi == 2 and d == DC - 1),
                            signal=pi == 2 and d == DC - 1)
                got.append((n, bank, m))
            sil, h = sil[:, 0:CH], h[:, 0:CH]
            m = act.do(lambda e, bank=got[0][1]: e.activation(sil, bank[:, 0:CH], ACT.Silu), after=[got[0][2], *sil_r.free(fj)])
            hb.release(got[0][0], m)
            m = dve.do(lambda e, bank=got[1][1]: e.tensor_tensor(h, sil, bank[:, 0:CH], ALU.mult), after=[m, got[1][2], *h_r.free(fj)])
            hb.release(got[1][0], m)
            sil_r.release(fj, m)
            m_h = act.do(lambda e: e.activation(hh[:, f, :], h, ACT.Copy), after=[m, *hh_r.free(job)])
            m_l = dve.do(lambda e: e.tensor_tensor(hl[:, f, :], h, hh[:, f, :], ALU.subtract), after=[m_h, *hl_r.free(job)])
            h_r.release(fj, m_l)
            if f == FC - 1:
                xch_r.release(job, got[1][2])
                xcl_r.release(job, got[1][2])
            return m_l

        def shared_y(job, ready):
            hh, hl = hh_r.buf(job), hl_r.buf(job)
            for i in range(CH // P):
                u = job * (CH // P) + i
                n, bank, free = take()
                for pi, (hx, w) in enumerate([(hh, HI), (hh, LO), (hl, HI)]):
                    for f in range(FC):
                        m = pe.do(lambda e, bank=bank, hx=hx, w=w, f=f, i=i, pi=pi: e.matmul(bank[:, 0:D], hx[:, f, i * P:(i + 1) * P], w_part(0, 2, w, f * D, D),
                                  start=pi == 0 and f == 0, stop=pi == 2 and f == FC - 1), after=[ready, *free], signal=pi == 2 and f == FC - 1)
                my = dve.do(lambda e, bank=bank, u=u: e.tensor_tensor(acc[:, u, :], bank[:, 0:D], x[:, u, :], ALU.add), after=[m])
                work.release(n, my)
            hh_r.release(job, m)
            hl_r.release(job, m)
            return my

        JOBS = TILES * P // CH
        def shared():
            ready = None
            shared_x(0)
            for job in range(JOBS):
                if job + 1 < JOBS:
                    shared_x(job + 1)
                for f in range(FC):
                    m = shared_h(job, f)
                    yield
                    if f == 0 and job:
                        shared_y(job - 1, ready)
                        yield
                ready = m
            S["acc"] = shared_y(JOBS - 1, ready)

        turns["route"] = 5 * JOBS * FC
        turns["shared"] = JOBS * FC
        weave([("route", route()), ("shared", shared())])
        m_ex, m_wgt = S["scattered"]
        m_acc = S["acc"]

        XTN = 4
        xt_r = ring("xt", [P, D], XTN, phase="experts")
        xt_sem = [sem(f"xt{k}") for k in range(XTN)]
        xth_r = ring("xth", [P, DC, P], 2, BF16, phase="experts")
        xtl_r = ring("xtl", [P, DC, P], 2, BF16, phase="experts")
        th_r = ring("th", [P, F], 2, BF16, phase="experts")
        tl_r = ring("tl", [P, F], 2, BF16, phase="experts")
        hT_r = ring("hT", [P, 2, FC, P], 2, BF16, phase="experts")
        yt_r = ring("yt", [P, D], 2, phase="experts")
        yt_sem = [sem(f"yt{k}") for k in range(2)]
        marks = {}

        def tile_load(k):
            sp.dma(lambda e: e.dma_start(xt_r.buf(k), xs[k * P:(k + 1) * P, :]), xt_sem[k % XTN], after=[(scattered, 16 * 2 * TILES), *xt_r.free(k)])

        def tile_x(k):
            xt, xh, xl = xt_r.buf(k), xth_r.buf(k), xtl_r.buf(k)
            n, bank, free = take()
            for c in range(DC):
                m = pe.do(lambda e, c=c: e.transpose(bank[:, c * P:(c + 1) * P], xt[:, c * P:(c + 1) * P], ident[:]), after=[(xt_sem[k % XTN], 16 * (k // XTN + 1)), *free], signal=c == DC - 1)
            xt_r.release(k, m)
            ml = two_parts(n, bank, xh, xl, m, xth_r.free(k), xtl_r.free(k))
            marks[k] = {"x": ml}

        def tile_h(k):
            xh, xl, th, tl, sil, h = (*(r.buf(k) for r in (xth_r, xtl_r, th_r, tl_r)), *(r.buf(JOBS * FC + k) for r in (sil_r, h_r)))
            got = []
            pe.wait(m_ex, marks[k]["x"], *[m for p in split.values() for m in p])
            value = {}
            pe.queue.append(lambda e, k=k: value.__setitem__("e", e.value_load(tile_ex[0:1, k:k + 1], min_val=0, max_val=E - 1)))
            marks[k]["e"] = value
            for q in range(2):
                n = 2 * (JOBS * FC + k) + q
                bank = hb.buf(n)
                for pi, (xx, w) in enumerate([(xh, HI), (xh, LO), (xl, HI)]):
                    for d in range(DC):
                        m = pe.do(lambda e, bank=bank, w=w, xx=xx, d=d, q=q, pi=pi: e.matmul(
                            bank[:], xx[:, d, :], w_part(value["e"] + 1, q, w, d * F, F), start=pi == 0 and d == 0, stop=pi == 2 and d == DC - 1),
                            after=[*hb.free(n)], signal=pi == 2 and d == DC - 1)
                got.append((n, bank, m))
            xth_r.release(k, m)
            xtl_r.release(k, m)
            m = act.do(lambda e, bank=got[0][1]: e.activation(sil, bank[:], ACT.Silu), after=[got[0][2], *sil_r.free(JOBS * FC + k)])
            hb.release(got[0][0], m)
            m = dve.do(lambda e, bank=got[1][1]: e.tensor_tensor(h, sil, bank[:], ALU.mult), after=[m, got[1][2], *h_r.free(JOBS * FC + k)])
            hb.release(got[1][0], m)
            sil_r.release(JOBS * FC + k, m)
            m_h = act.do(lambda e: e.activation(th, h, ACT.Copy), after=[m, *th_r.free(k)])
            m_l = pool.do(lambda e: e.tensor_tensor(tl, h, th, ALU.subtract), after=[m_h, *tl_r.free(k)])
            h_r.release(JOBS * FC + k, m_l)
            marks[k]["h"] = m_l

        def tile_turn(k):
            th, tl, hT = th_r.buf(k), tl_r.buf(k), hT_r.buf(k)
            n, bank, free = take()
            tb = bank[:].bitcast(BF16)
            for q, part in enumerate((th, tl)):
                for f in range(FC):
                    m = pe.do(lambda e, q=q, f=f, part=part: e.transpose(tb[:, (q * FC + f) * P:(q * FC + f + 1) * P], part[:, f * P:(f + 1) * P], ident_bf[:]),
                              after=[marks[k]["h"], *free], signal=q * FC + f == 2 * FC - 1)
            th_r.release(k, m)
            tl_r.release(k, m)
            tv = tb.rearrange("p (q f t) -> p q f t", q=2, f=FC)
            m = dve.do(lambda e: e.tensor_copy(hT, tv), after=[m, *hT_r.free(k)])
            work.release(n, m)
            marks[k]["hT"] = m

        def tile_y(k):
            hT, yt, value = hT_r.buf(k), yt_r.buf(k), marks[k]["e"]
            n, bank, free = take()
            for pi, (q, w) in enumerate([(0, HI), (0, LO), (1, HI)]):
                for f in range(FC):
                    m = pe.do(lambda e, q=q, w=w, f=f, pi=pi: e.matmul(bank[:, 0:D], hT[:, q, f, :], w_part(value["e"] + 1, 2, w, f * D, D),
                              start=pi == 0 and f == 0, stop=pi == 2 and f == FC - 1), after=[marks[k]["hT"], *free], signal=pi == 2 and f == FC - 1)
            hT_r.release(k, m)
            m = act.do(lambda e: e.activation(yt, bank[:, 0:D], ACT.Copy), after=[m, *yt_r.free(k)])
            work.release(n, m)
            sp.dma(lambda e: e.dma_start(ys[k * P:(k + 1) * P, :], yt), yt_sem[k % 2], after=[m])
            yt_r.release(k, (yt_sem[k % 2], 16 * (k // 2 + 1)))

        for k in range(XTN - 1):
            tile_load(k)
        for k in range(NTT + 3):
            if k + XTN - 1 < NTT:
                tile_load(k + XTN - 1)
            if k < NTT:
                tile_x(k)
            if 0 <= k - 1 < NTT:
                tile_h(k - 1)
            if 0 <= k - 2 < NTT:
                tile_turn(k - 2)
            if 0 <= k - 3 < NTT:
                tile_y(k - 3)

        act.do(lambda e: e.preload_act_table_set("natural_log_exp_and_others"), signal=False)
        YAN = 8
        ya_r = ring("ya", [P, 2, D], YAN, phase="final")
        ya_sem = [sem(f"ya{k}") for k in range(YAN)]
        pool.wait(pe.last())
        y_stored = [(yt_sem[k], 16 * ((NTT - k + 1) // 2)) for k in range(2)]
        stores = sem("stores")
        stf_r = ring("stf", [P, 12], 4)

        def finish(u):
            ya, st = ya_r.buf(u), stf_r.buf(u)
            for k in range(2):
                pool.dma(lambda e, k=k: e.indirect_dma_start(ya[:, k, :], None, ys, bass.IndirectOffsetOnAxis(slot[k][:, u:u + 1], 0)), ya_sem[u % YAN],
                         after=[*y_stored, *ya_r.free(u)])
            yield
            m = dve.do(lambda e: e.scalar_tensor_tensor(acc[:, u, :], ya[:, 0, :], weight[0][:, u:u + 1], acc[:, u, :], ALU.mult, ALU.add), after=[(ya_sem[u % YAN], 32 * (u // YAN + 1)), m_acc])
            m = dve.do(lambda e: e.scalar_tensor_tensor(acc[:, u, :], ya[:, 1, :], weight[1][:, u:u + 1], acc[:, u, :], ALU.mult, ALU.add), after=[m])
            ya_r.release(u, m)
            yield
            m = yield from layer_norm(acc[:, u, :], acc[:, u, :], st[:], m)
            sp.dma(lambda e: e.dma_start(out[u * P:(u + 1) * P, :], acc[:, u, :]), stores, after=[m])
            stf_r.release(u, m)

        for u in range(0, TILES, 4):
            for _ in abreast([finish(u + v) for v in range(4)]):
                pass
        sp.wait((stores, 16 * TILES))
        block = ctx.enter_context(nc.Block())
        for name, lane in (("tensor", pe), ("scalar", act), ("vector", dve), ("gpsimd", pool), ("sync", sp)):
            def emit(e, lane=lane):
                for make in lane.queue:
                    make(e)
            {"tensor": block.tensor, "scalar": block.scalar, "vector": block.vector, "gpsimd": block.gpsimd, "sync": block.sync}[name](emit)


def kernel(**inputs):
    import concourse.bacc as bacc
    from concourse import mybir as mb
    from concourse.bass_utils import run_bass_kernel_spmd

    a = {k: np.asarray(v) for k, v in inputs.items()}
    B, L, D = a["x"].shape
    DV = a["L0_attn_wv"].shape[0]
    R = a["L0_attn_wgk1"].shape[0]
    HEADS = 4
    f32 = np.float32
    T = lambda w: np.swapaxes(w, -1, -2)
    columns = lambda v: v.reshape(-1, P).T
    s_, t_ = np.arange(P)[:, None], np.arange(P)[None, :]
    masks = [s_ == t_] + [(s_ // (2 * h) == t_ // (2 * h)) & (s_ % (2 * h) < h) & (t_ % (2 * h) >= h) for h in LEVELS if h < 32]
    n_heads = 16
    pi = np.arange(P)
    laid = {
        "x": a["x"], "ctxT": a["ctx_1024"].reshape(-1, D).T, "mask": a["mask_1x1xSxS2_if1"],
        "wqT": T(a["L0_attn_wq"]), "wkT": T(a["L0_attn_wk"]), "wvT": T(a["L0_attn_wv"]), "wgT": T(a["L0_attn_wg"]),
        "wgk1T": T(a["L0_attn_wgk1"]), "wgk2T": T(a["L0_attn_wgk2"]), "woT": T(a["L0_attn_wo"]),
        "norm_w": np.stack([a["L0_attn_n" + n] for n in ("q", "k", "v", "gk1", "g")]),
        "no_w": a["L0_attn_no"], "ngk2": a["L0_attn_ngk2"], "bgk2": columns(a["L0_attn_bgk2"]),
        "xWqT": T(a["L0_xattn_W_q"]), "xWkT": T(a["L0_xattn_W_k"]), "xWvT": T(a["L0_xattn_W_v"]), "xWoT": T(a["L0_xattn_W_o"]),
        "xbq": columns(a["L0_xattn_b_q"]), "xbk": columns(a["L0_xattn_b_k"]), "xbv": a["L0_xattn_b_v"], "xbo": a["L0_xattn_b_o"],
        "gateT": T(a["L0_ffn_gate_w"]), "gate_bias": a["L0_ffn_gate_bias"],
        "w1T": T(a["L0_ffn_w1"]), "w2T": T(a["L0_ffn_w2"]), "w3T": T(a["L0_ffn_w3"]),
        "sw1T": T(a["L0_ffn_sw1"]), "sw2T": T(a["L0_ffn_sw2"]), "sw3T": T(a["L0_ffn_sw3"]),
        "ident": np.eye(P, dtype=f32),
        "level_mask": np.stack(masks, 1).astype(np.int32),
        "inv_count": np.array([1.0 / n for n in (D * D, D * D, D * DV, D * R, D * DV, D * DV, D * R)], f32),
        "unit": np.array([(D // HEADS) ** -0.5 / 127.0] + [1.0 / 127.0] * 6, f32),
        "head_mask": (pi[:, None] // (D // n_heads) == np.arange(n_heads // (D // P))[None, :]).astype(f32),
        "before": (s_ < t_).astype(f32),
        "tile_no": np.arange((2 * B * L + (P - 1) * 8) // P).astype(f32),
        "lower": (np.arange(8)[None, :] < np.arange(8)[:, None]).astype(f32),
    }
    nc = bacc.Bacc("TRN2", target_bir_lowering=False, num_devices=1)
    arrays, handles = {}, {}
    for name, v in laid.items():
        v = np.ascontiguousarray(v)
        arrays[f"in_{name}"] = v
        handles[name] = nc.dram_tensor(f"in_{name}", v.shape, mb.dt.from_np(v.dtype), kind="ExternalInput").ap()
    out = nc.dram_tensor("out", (B * L, D), mb.dt.float32, kind="ExternalOutput").ap()
    decoder_layer(nc, handles, out)
    r = run_bass_kernel_spmd(nc, [arrays], core_ids=[0])
    return r.results[0]["out"].reshape(B, L, D)
```

```python
import itertools
from contextlib import ExitStack

import numpy as np

import concourse.bass as bass
from concourse import mybir

F32 = mybir.dt.float32
BF16 = mybir.dt.bfloat16
I32 = mybir.dt.int32
ALU = mybir.AluOpType
ACT = mybir.ActivationFunctionType
AX = mybir.AxisListType

P = 128
ROUND = 12582912.0
DMA_BYTES_US = 180e3
HOP_US = 0.1
NEXT = "next"
LEVELS = [1, 2, 4, 8, 16, 32, 64]


class Lane:
    ends = {}
    latest = dma_end = 0.0

    def __init__(self, sem, us):
        self.sem, self.count, self.queue, self.met = sem, 0, [], {}
        self.us, self.clock = us, 0.0

    def wait(self, *marks):
        for m in marks:
            if m is None:
                continue
            sem, value = m
            self.clock = max(self.clock, Lane.ends.get((sem.num, value), 0.0))
            if value > self.met.get(sem.num, 0):
                self.met[sem.num] = value
                self.queue.append(lambda e, sem=sem, value=value: e.wait_ge(sem, value))

    def do(self, make, after=(), signal=True, us=None):
        self.wait(*after)
        self.clock += us or self.us
        if not signal:
            self.queue.append(make)
            return None
        self.count += 1
        self.queue.append(lambda e: make(e).then_inc(self.sem, 1))
        Lane.ends[self.sem.num, self.count] = Lane.latest = self.clock + HOP_US
        return (self.sem, self.count)

    def dma(self, make, sem, after=()):
        self.wait(*after)
        self.queue.append(lambda e: make(e).then_inc(sem, 16))

    def last(self):
        return (self.sem, self.count) if self.count else None


class Ring:

    def __init__(self, bufs):
        self.bufs, self.marks, self.released = bufs, [()] * len(bufs), [-1] * len(bufs)

    def buf(self, i):
        return self.bufs[i % len(self.bufs)]

    def free(self, i):
        assert i < len(self.bufs) or self.released[i % len(self.bufs)] == i - len(self.bufs), "taken before its readers are known"
        return self.marks[i % len(self.bufs)]

    def release(self, i, *marks):
        self.marks[i % len(self.bufs)], self.released[i % len(self.bufs)] = marks, i


def decoder_layer(nc, t, out):
    B, L, D = t["x"].shape
    NT = L // P
    TILES = B * NT
    DC = D // P
    DV = t["wvT"].shape[1]
    VC = DV // P
    R = t["wgk1T"].shape[1]
    HEADS = 4
    DK = D // HEADS
    DVH = DV // HEADS
    S2 = t["ctxT"].shape[1] // B
    XH = 16
    XD = D // XH
    HB = XH // 4
    E, F = t["w1T"].shape[0], t["w1T"].shape[2]
    FC = F // P
    NORMS = 5
    JQ, JK, JV, JR, JG = range(NORMS)
    assert DK == 64 and NT == 2 and DC == 2 and HB * S2 <= 512

    with ExitStack() as ctx:
        def sb(name, shape, dt=F32):
            return ctx.enter_context(nc.sbuf_tensor(name, shape, dt))

        EARLY, LATE = 29696, 16256
        early = sb("early", [P, EARLY])
        late = sb("late", [P, LATE])
        place = {"attention": [early, 0], "weights": [early, 0], "prepare": [late, 0], "cross": [late, 0],
                 "experts": [late, 0], "final": [early, 0]}
        place["cross2"] = [late, 10432]
        place["masks"] = [early, EARLY - 8 * P]

        def carve(phase, shape, dt=F32):
            words = int(np.prod(shape[1:])) * {BF16: 2, mybir.dt.int8: 1}.get(dt, 4) // 4
            area, a = place[phase]
            place[phase][1] += words
            assert a + words <= area.shape[1] and phase, (phase, a + words)
            v = area[0:shape[0], a:a + words]
            v = v.bitcast(dt) if dt != F32 else v
            names = "abcd"[:len(shape) - 1]
            if len(shape) > 2:
                v = v.rearrange(f"p ({' '.join(names)}) -> p {' '.join(names)}", **dict(zip(names, shape[1:])))
            return v

        def sem(name):
            return ctx.enter_context(nc.semaphore(name))

        pe, act, dve, pool, sp = (Lane(sem(f"{n}_done"), us) for n, us in (("pe", 0.2), ("act", 0.35), ("dve", 0.25), ("pool", 1.2), ("sp", 0.1)))
        Lane.ends.clear()
        Lane.latest = Lane.dma_end = 0.0
        loads = {}

        def load(dst, src, name, lane=None):
            if name not in loads:
                loads[name] = [sem(f"ld_{name}"), 0]
            loads[name][1] += 16
            lane = lane or sp
            Lane.dma_end = max(Lane.dma_end, lane.clock) + int(np.prod(dst.shape)) * 4 / DMA_BYTES_US
            Lane.ends[loads[name][0].num, loads[name][1]] = Lane.dma_end + 2
            lane.dma(lambda e: e.dma_start(dst, src), loads[name][0])

        def loaded(name):
            return tuple(loads[name])

        def bcast(ap, n):
            a = ap.unsqueeze(1)
            return a.to_broadcast([a.shape[0], n] + list(a.shape[2:]))

        banks = [ctx.enter_context(nc.psum_tensor(f"bank{i}", [P, 512], F32)) for i in range(8)]
        class Work:
            idle = [(n, ()) for n in range(4, 8)]

            def release(self, n, *marks):
                self.idle.append((n, marks))

        work = Work()

        def take():
            n, marks = work.idle.pop(0)
            return n, banks[n], marks

        def spare():
            return len(work.idle) > 1

        x = sb("x", [P, TILES, D])
        ident = sb("ident", [P, P])
        ident_bf = sb("ident_bf", [P, P], BF16)
        ones = sb("ones", [P, P])
        level_mask = carve("attention", [P, 6, P], mybir.dt.int8)
        level_mask_raw = carve("masks", [P, 6, P], I32)
        norm_w = carve("attention", [P, NORMS, D])
        no_w = carve("attention", [P, DV])
        ngk2_w = carve("attention", [P, R])
        bgk2 = carve("attention", [P, DC])
        w_raw = carve("prepare", [P, DC * (2 * D + R + 2 * DV) + VC * D])
        w_int = carve("attention", [P, DC * (2 * D + R + 2 * DV) + VC * D], BF16)
        wgk2_raw = carve("prepare", [R, D])
        wgk2_int = carve("attention", [R, D])
        inv_count = carve("attention", [P, 7])
        unit = carve("attention", [P, 7])
        w_sums = sb("w_sums", [P, 7])
        round_c = sb("round_c", [P, 1])
        w_mean = sb("w_mean", [P, 7])
        w_scale = sb("w_scale", [P, 7])
        w_unit = sb("w_unit", [P, 7])

        load(ident[:], t["ident"], "const")
        load(inv_count[:], t["inv_count"].partition_broadcast(P), "const")
        load(unit[:], t["unit"].partition_broadcast(P), "const")
        col, at = {}, 0
        for name, chunks, width in (("wqT", DC, D), ("wkT", DC, D), ("wvT", DC, DV), ("wgk1T", DC, R), ("wgT", DC, DV), ("woT", VC, D)):
            col[name] = (at, chunks, width)
            load(w_raw[:, at:at + chunks * width].rearrange("p (c n) -> p c n", c=chunks),
                 t[name].rearrange("(c p) n -> p c n", p=P), "w_bit", act)
            at += chunks * width
        load(wgk2_raw[:], t["wgk2T"], "w_bit", act)
        load(norm_w[:], t["norm_w"].partition_broadcast(P), "norm")
        for b in range(B):
            load(x[:, b * NT:(b + 1) * NT, :], t["x"][b].rearrange("(i p) d -> p i d", p=P), f"x{b}")
            if b == 0:
                load(level_mask_raw, t["level_mask"], "masks")
                load(no_w[:], t["no_w"].partition_broadcast(P), "attn")
                load(ngk2_w[:], t["ngk2"].partition_broadcast(P), "attn")
                load(bgk2[:], t["bgk2"], "attn")

        xw_T = {n: carve("cross2", [P, DC, D]) for n in ("xWqT", "xWkT", "xWvT", "xWoT")}
        ctxT = carve("cross2", [P, DC, B * S2])
        xbq = carve("cross2", [P, DC])
        xbk = carve("cross2", [P, DC])
        xbv = carve("cross2", [P, D])
        xbo = carve("cross2", [P, D])
        head_mask = carve("cross2", [P, XH // DC])
        mask_raw = carve("cross2", [P, NT, S2], I32)
        keep = carve("masks", [P, NT, S2])
        drop = carve("cross2", [P, NT, HB, S2])
        row = carve("cross2", [P, NT])
        for n in xw_T:
            load(xw_T[n][:], t[n].rearrange("(c p) n -> p c n", p=P), "cross")
        load(ctxT[:], t["ctxT"].rearrange("(c p) n -> p c n", p=P), "cross")
        load(xbq[:], t["xbq"], "cross")
        load(xbk[:], t["xbk"], "cross")
        load(xbv[:], t["xbv"].partition_broadcast(P), "cross")
        load(xbo[:], t["xbo"].partition_broadcast(P), "cross")
        load(head_mask[:], t["head_mask"], "cross")
        load(mask_raw[:], t["mask"].rearrange("a c (i p) k -> p (a c i) k", p=P), "cross")

        NTT = (2 * TILES * P + (P - 1) * E) // P
        xs = nc.dram_tensor("x_slots", (NTT * P, D), F32, kind="Internal").ap()
        ys = nc.dram_tensor("y_slots", (NTT * P, D), F32, kind="Internal").ap()
        zeros = sb("zeros", [P, D])
        cleared = sem("cleared")
        zero_ok = pool.do(lambda e: e.memset(zeros[:], 0.0))
        sp.dma(lambda e: e.dma_start(xs.rearrange("(k p) d -> p k d", p=P), bcast(zeros[:], NTT)), cleared, after=[zero_ok])

        ones_ok = dve.do(lambda e: e.memset(ones[:], 1.0))
        round_ok = dve.do(lambda e: e.memset(round_c[:], ROUND))
        dve.do(lambda e: e.memset(w_sums[:], 0.0))
        sums_zero = dve.last()
        mask_ok = dve.do(lambda e: e.tensor_copy(level_mask[:], level_mask_raw), after=[loaded("masks")])
        act.do(lambda e: e.preload_act_table_set("natural_log_exp_and_others"), signal=False)
        ident_ok = act.do(lambda e: e.activation(ident_bf[:], ident[:], ACT.Copy), after=[loaded("const")])
        order = ["wqT", "wkT", "wvT", "wgk1T", "wgT", "woT"]

        def raw(name, buf):
            a, c, w = col[name]
            return buf[:, a:a + c * w]

        def w_chunk(name, c, a, b):
            at, _, w = col[name]
            return w_int[:, at + c * w + a:at + c * w + b]

        def rsqrt(v, tmp, out, ready):
            m = act.do(lambda e: e.activation(tmp, v, ACT.Ln), after=[ready])
            m = act.do(lambda e: e.activation(out, tmp, ACT.Exp, scale=-0.5), after=[m])
            yield
            m = dve.do(lambda e: e.tensor_tensor(tmp, out, out, ALU.mult), after=[m])
            m = dve.do(lambda e: e.tensor_tensor(tmp, tmp, v, ALU.mult), after=[m])
            m = dve.do(lambda e: e.tensor_scalar(tmp, tmp, -0.5, 1.5, ALU.mult, ALU.add), after=[m])
            return dve.do(lambda e: e.tensor_tensor(out, out, tmp, ALU.mult), after=[m])

        def ring(name, shape, n=2, dt=F32, phase=None):
            if phase:
                return Ring([carve(phase, shape, dt) for _ in range(n)])
            return Ring([sb(f"{name}{i}", shape, dt) for i in range(n)])

        def abreast(gens):
            gens = list(gens)
            while gens:
                gens = [g for g in gens if next(g, "end") != "end"]
                yield

        S = {}

        def ternary(b):
            if b:
                return
            for j, n in enumerate(order):
                dve.do(lambda e, j=j, n=n: e.tensor_reduce(w_sums[:, j:j + 1], raw(n, w_raw), AX.X, ALU.add,
                                                           apply_absolute_value=True),
                       after=[loaded("w_bit"), sums_zero])
                yield
            sums = dve.do(lambda e: e.tensor_reduce(w_sums[0:R, 6:7], wgk2_raw[:], AX.X, ALU.add, apply_absolute_value=True))
            i, bank, free = take()
            total = pe.do(lambda e, bank=bank: e.matmul(bank[:, 0:7], ones[:], w_sums[:], start=True, stop=True),
                          after=[*free, sums, ones_ok])
            m = dve.do(lambda e, bank=bank: e.tensor_tensor(w_mean[:], bank[:, 0:7], inv_count[:], ALU.mult), after=[total, loaded("const")])
            work.release(i, m)
            m = dve.do(lambda e: e.tensor_scalar(w_mean[:], w_mean[:], 1e-5, None, ALU.max), after=[m])
            dve.do(lambda e: e.reciprocal(w_scale[:], w_mean[:]), after=[m])
            S["w_unit"] = m = dve.do(lambda e: e.tensor_tensor(w_unit[:], w_mean[:], unit[:], ALU.mult))
            for j, n in enumerate(order + ["wgk2"]):
                src = wgk2_raw[:] if n == "wgk2" else raw(n, w_raw)
                tmp = wgk2_raw[:] if n == "wgk2" else raw(n, w_raw)
                dst = wgk2_int[:] if n == "wgk2" else raw(n, w_int)
                rows = R if n == "wgk2" else P
                s = w_scale[0:rows, j:j + 1]
                m1 = dve.do(lambda e, a=(tmp, src, s): e.tensor_scalar(a[0], a[1], a[2], 1.0, ALU.mult, ALU.min), after=[m])
                yield
                m1 = dve.do(lambda e, a=tmp: e.tensor_scalar(a, a, -1.0, ROUND, ALU.max, ALU.add), after=[m1])
                yield
                S["w_int"] = dve.do(lambda e, a=(dst, tmp): e.tensor_scalar(a[0], a[1], ROUND, None, ALU.subtract), after=[m1])

        xn_r = ring("xn", [P, NORMS, NT * D], 1, phase="attention")
        st_r = ring("st", [P, 64], 3)
        xi_r = ring("xi", [P, NORMS, NT * D], 1, BF16, phase="attention")
        xT_r = ring("xT", [P, NORMS, DC, L], 1, BF16, phase="attention")
        sq_r = ring("sq", [P, D], 2, BF16, phase="attention")
        q_r = ring("q", [P, DC, L], phase="attention")
        k_r = ring("k", [P, DC, L], phase="attention")
        gk_r = ring("gk", [P, DC, L], phase="attention")
        v_r = ring("v", [P, NT, DV], 3, phase="attention")
        sg_r = ring("sg", [P, NT, DV], 3, phase="attention")
        ge_r = ring("ge", [P, DV], 2, phase="attention")
        z_r = ring("z", [P, NT, R], phase="attention")
        zw_r = ring("zw", [P, NT, R], phase="attention")
        zT_r = ring("zT", [R, L], phase="attention")

        def A1(b):
            xb = x[:, b * NT:(b + 1) * NT, :].rearrange("p i d -> p (i d)")
            xn, st, xi, xT = xn_r.buf(b), st_r.buf(b), xi_r.buf(b), xT_r.buf(b)
            m_xn = []
            for j in range(NORMS):
                m_xn.append(pool.do(lambda e, j=j: e.tensor_tensor(xn[:, j].rearrange("p (i d) -> p i d", i=NT), x[:, b * NT:(b + 1) * NT, :], bcast(norm_w[:, j], NT), ALU.mult),
                                    after=[loaded(f"x{b}"), loaded("norm"), *xn_r.free(b)], us=1.1))
                yield
            for i in range(NT):
                n = b * NT + i
                act.wait(*sq_r.free(n), *st_r.free(b))
                m = act.do(lambda e, i=i, n=n: e.activation(sq_r.buf(n)[:], x[:, n, :], ACT.Square, accum_out=st[:, i:i + 1]),
                           after=[loaded(f"x{b}")])
                sq_r.release(n, m)
            yield
            m = dve.do(lambda e: e.tensor_scalar(st[:, 0:2], st[:, 0:2], 1.0 / D, 1e-8, ALU.mult, ALU.add), after=[m])
            rms = yield from rsqrt(st[:, 0:2], st[:, 4:6], st[:, 2:4], m)
            yield
            c = st[:, 10:20]
            cv = c.rearrange("p (j i) -> p j i", i=NT)
            for j in range(NORMS):
                m = dve.do(lambda e, j=j: e.tensor_reduce(cv[:, j, :], xn[:, j, :].rearrange("p (i d) -> p i d", i=NT), AX.X, ALU.max,
                                                          apply_absolute_value=True), after=[m_xn[j]], us=0.6)
                yield
            rb = bcast(st[:, 2:4], NORMS)
            m = dve.do(lambda e: e.tensor_tensor(cv, cv, rb, ALU.mult), after=[m, rms])
            m = dve.do(lambda e: e.tensor_scalar(c, c, 1e-5, None, ALU.max), after=[m])
            s = st[:, 20:30]
            sv = s.rearrange("p (j i) -> p j i", i=NT)
            m = dve.do(lambda e: e.reciprocal(s, c), after=[m])
            m = dve.do(lambda e: e.tensor_tensor(sv, sv, rb, ALU.mult), after=[m])
            m = dve.do(lambda e: e.tensor_scalar(s, s, 127.0, None, ALU.mult), after=[m])
            u = st[:, 30:40]
            m2 = dve.do(lambda e: e.tensor_tensor(u.rearrange("p (j i) -> p j i", i=NT), cv,
                                                  w_unit[:, 0:NORMS].unsqueeze(2).to_broadcast([P, NORMS, NT]), ALU.mult), after=[S["w_unit"]])
            m2 = dve.do(lambda e: e.tensor_tensor(st[:, 40:42], st[:, 30 + 2 * JK:32 + 2 * JK], st[:, 30 + 2 * JV:32 + 2 * JV], ALU.mult), after=[m2])
            scales = dve.do(lambda e: e.tensor_scalar(st[:, 42:44], st[:, 30 + 2 * JG:32 + 2 * JG], -1.0, None, ALU.mult))
            yield
            for j in range(NORMS):
                for i in range(NT):
                    a = xn[:, j, i * D:(i + 1) * D]
                    mr = act.do(lambda e, a=a, k=20 + 2 * j + i: e.activation(a, a, ACT.Identity, bias=round_c[:, 0:1], scale=st[:, k:k + 1]), after=[m, round_ok], us=0.4)
                yield
                m_xi = dve.do(lambda e, j=j: e.tensor_scalar(xi[:, j, :], xn[:, j, :], ROUND, None, ALU.subtract), after=[mr, *xi_r.free(b)])
                yield
            xn_r.release(b, m_xi)
            yield NEXT
            copied = []
            for j in range(NORMS):
                if j % 2 == 0:
                    n, bank, free = take()
                    tb = bank[:].bitcast(BF16)
                    pe.wait(m_xi, ident_ok, *free)
                o = (j % 2) * DC * L
                for c_ in range(DC):
                    for i in range(NT):
                        m = pe.do(lambda e, j=j, c_=c_, i=i, tb=tb, o=o: e.transpose(
                            tb[:, o + c_ * L + i * P:o + c_ * L + (i + 1) * P], xi[:, j, i * D + c_ * P:i * D + (c_ + 1) * P], ident_bf[:]),
                            signal=(j % 2 == 1 or j == NORMS - 1) and c_ == DC - 1 and i == NT - 1)
                if j % 2 == 1 or j == NORMS - 1:
                    if spare():
                        yield
                    j0 = j - j % 2
                    k = j - j0 + 1
                    src = tb[:, 0:k * DC * L].rearrange("p (j c l) -> p j c l", j=k, c=DC)
                    mc = act.do(lambda e, src=src, j0=j0, k=k: e.activation(xT[:, j0:j0 + k], src, ACT.Copy), after=[m, *xT_r.free(b)])
                    work.release(n, mc)
                    copied.append(mc)
                    yield
            xi_r.release(b, m)
            yield NEXT
            v, sg, z, zw, zT = (r.buf(b) for r in (v_r, sg_r, z_r, zw_r, zT_r))
            n, bank, free = take()
            for i in range(NT):
                for c_ in range(DC):
                    m = pe.do(lambda e, i=i, c_=c_, bank=bank: e.matmul(bank[:, i * R:(i + 1) * R], xT[:, JR, c_, i * P:(i + 1) * P],
                                                                        w_chunk("wgk1T", c_, 0, R), start=c_ == 0, stop=c_ == DC - 1),
                              after=[*free, copied[1], S["w_int"]], signal=i == NT - 1 and c_ == DC - 1)
            if spare():
                yield
            for i in range(NT):
                mz = dve.do(lambda e, i=i, bank=bank: e.tensor_scalar(z[:, i, :], bank[:, i * R:(i + 1) * R], st[:, 30 + 2 * JR + i:31 + 2 * JR + i], None, ALU.mult),
                            after=[m, scales, *z_r.free(b)])
            work.release(n, mz)
            def project(name, j, m_in):
                n, bank, free = take()
                for e_ in range(DC):
                    for c_ in range(DC):
                        m = pe.do(lambda e, e_=e_, c_=c_, bank=bank: e.matmul(bank[:, e_ * L:(e_ + 1) * L], w_chunk(name, c_, e_ * P, (e_ + 1) * P),
                                                                              xT[:, j, c_, :], start=c_ == 0, stop=c_ == DC - 1),
                                  after=[*free, m_in], signal=e_ == DC - 1 and c_ == DC - 1)
                return n, bank[:].rearrange("p (c l) -> p c l", c=DC), m
            n, qps, m = project("wqT", JQ, copied[0])
            if spare():
                yield
            mq = act.do(lambda e: e.activation(q_r.buf(b)[:], qps, ACT.Copy), after=[m, *q_r.free(b)])
            work.release(n, mq)
            n, kps, m = project("wkT", JK, copied[0])
            if spare():
                yield
            mk = act.do(lambda e: e.activation(k_r.buf(b)[:], kps, ACT.Copy), after=[m, *k_r.free(b)])
            work.release(n, mk)
            yield
            ms, rr, tt, cc, uu = (st[:, 44 + 2 * k:46 + 2 * k] for k in range(5))
            m = dve.do(lambda e: e.tensor_tensor(zw[:], z[:], z[:], ALU.mult), after=[mz, *zw_r.free(b)])
            m = dve.do(lambda e: e.tensor_reduce(ms, zw[:], AX.X, ALU.add), after=[m])
            m = dve.do(lambda e: e.tensor_scalar(ms, ms, 1.0 / R, 1e-8, ALU.mult, ALU.add), after=[m])
            mr = yield from rsqrt(ms, tt, rr, m)
            yield
            m = dve.do(lambda e: e.tensor_tensor(zw[:], z[:], bcast(ngk2_w[:], NT), ALU.mult), after=[loaded("attn")])
            m = dve.do(lambda e: e.tensor_reduce(cc, zw[:], AX.X, ALU.max, apply_absolute_value=True), after=[m])
            m = dve.do(lambda e: e.tensor_tensor(cc, cc, rr, ALU.mult), after=[m, mr])
            m = dve.do(lambda e: e.tensor_scalar(cc, cc, 1e-5, None, ALU.max), after=[m])
            m = dve.do(lambda e: e.reciprocal(tt, cc), after=[m])
            m = dve.do(lambda e: e.tensor_tensor(tt, tt, rr, ALU.mult), after=[m])
            m = dve.do(lambda e: e.tensor_scalar(tt, tt, 127.0, None, ALU.mult), after=[m])
            m = dve.do(lambda e: e.tensor_scalar(uu, cc, w_unit[:, 6:7], None, ALU.mult), after=[m])
            for i in range(NT):
                m = dve.do(lambda e, i=i: e.tensor_scalar(zw[:, i, :], zw[:, i, :], tt[:, i:i + 1], ROUND, ALU.mult, ALU.add), after=[m])
            for i in range(NT):
                m = dve.do(lambda e, i=i: e.tensor_scalar(zw[:, i, :], zw[:, i, :], ROUND, uu[:, i:i + 1], ALU.subtract, ALU.mult), after=[m])
            m_zw = m
            yield
            for i in range(NT):
                n, bank, free = take()
                for c_ in range(DC):
                    m = pe.do(lambda e, i=i, c_=c_, bank=bank: e.matmul(bank[:], xT[:, JV, c_, i * P:(i + 1) * P], w_chunk("wvT", c_, 0, DV), start=c_ == 0, stop=c_ == DC - 1),
                              after=[*free, copied[1]], signal=c_ == DC - 1)
                if spare():
                    yield
                mv = act.do(lambda e, i=i, bank=bank: e.activation(v[:, i, :], bank[:], ACT.Copy, scale=st[:, 40 + i:41 + i]), after=[m, scales, *v_r.free(b)])
                work.release(n, mv)
                yield
            for i in range(NT):
                n, bank, free = take()
                for c_ in range(DC):
                    m = pe.do(lambda e, i=i, c_=c_, bank=bank: e.matmul(bank[:], xT[:, JG, c_, i * P:(i + 1) * P], w_chunk("wgT", c_, 0, DV), start=c_ == 0, stop=c_ == DC - 1),
                              after=[*free, copied[2]], signal=c_ == DC - 1)
                u_ = b * NT + i
                ge = ge_r.buf(u_)
                if spare():
                    yield
                m1 = act.do(lambda e, i=i, bank=bank, ge=ge: e.activation(ge[:], bank[:], ACT.Exp, scale=st[:, 42 + i:43 + i]), after=[m, scales, *ge_r.free(u_)])
                m1 = act.do(lambda e, ge=ge: e.activation(ge[:], ge[:], ACT.Ln, bias=1.0), after=[m1])
                m1 = act.do(lambda e, ge=ge: e.activation(ge[:], ge[:], ACT.Exp, scale=-1.0), after=[m1])
                if spare():
                    yield
                mg = dve.do(lambda e, i=i, bank=bank, ge=ge: e.scalar_tensor_tensor(sg[:, i, :], bank[:], st[:, 30 + 2 * JG + i:31 + 2 * JG + i], ge[:], ALU.mult, ALU.mult),
                            after=[m1, m, scales, *sg_r.free(b)])
                ge_r.release(u_, mg)
                work.release(n, mg)
                yield
            n, bank, free = take()
            for i in range(NT):
                m = pe.do(lambda e, i=i, bank=bank: e.transpose(bank[0:R, i * P:(i + 1) * P], zw[:, i, :], ident[:]), after=[m_zw, *free], signal=i == NT - 1)
            z_r.release(b, m_zw)
            zw_r.release(b, m)
            if spare():
                yield
            mc = act.do(lambda e, bank=bank: e.activation(zT[:], bank[0:R, 0:L], ACT.Copy), after=[m, *zT_r.free(b)])
            work.release(n, mc)
            yield
            n, bank, free = take()
            for c_ in range(DC):
                m = pe.do(lambda e, c_=c_, bank=bank: e.matmul(bank[:, c_ * L:(c_ + 1) * L], wgk2_int[:, c_ * P:(c_ + 1) * P], zT[:], start=True, stop=True),
                          after=[mc, *free], signal=c_ == DC - 1)
            zT_r.release(b, m)
            xT_r.release(b, m)
            gk = gk_r.buf(b)
            if spare():
                yield
            mgk = act.do(lambda e, bank=bank: e.activation(gk[:], bank[:].rearrange("p (c l) -> p c l", c=DC), ACT.Copy), after=[m, *gk_r.free(b)])
            work.release(n, mgk)
            S[b] = dict(q=mq, k=mk, v=mv, g=mg, gk=mgk, scales=scales)

        gate_r = ring("gate", [P, DC, L], 2, phase="attention")
        Q_r = ring("Q", [P, DC, L], phase="attention")
        tot_r = ring("tot", [P, DC, L], 1, phase="attention")
        A_bufs = [carve("attention", [P, 2, DC, NT, P]) for _ in range(2)]
        A_r = Ring(A_bufs)
        Aoff_r = ring("Aoff", [P, 2, DC, P], 2, phase="attention")
        a_zero = []
        for a in A_bufs:
            a_zero.append(pool.do(lambda e, a=a: e.memset(a[:], 0.0)))
        level_banks = Ring([(banks[0], banks[1]), (banks[2], banks[3])])
        level_n = [0]

        def A2(b):
            q, k, gk, gate, Q, tot = (r.buf(b) for r in (q_r, k_r, gk_r, gate_r, Q_r, tot_r))
            ga = Q
            for c in range(DC):
                m = act.do(lambda e, c=c: e.activation(ga[:, c, :], gk[:, c, :], ACT.Abs, bias=bgk2[:, c:c + 1]), after=[S[b]["gk"], loaded("attn"), *Q_r.free(b)])
                yield
                mm = dve.do(lambda e, c=c: e.tensor_scalar(gk[:, c, :], gk[:, c, :], bgk2[:, c:c + 1], 0.0, ALU.add, ALU.min), after=[m])
            yield
            m = act.do(lambda e: e.activation(ga[:], ga[:], ACT.Exp, scale=-1.0), after=[m])
            m = act.do(lambda e: e.activation(ga[:], ga[:], ACT.Ln, bias=1.0), after=[m])
            yield
            m = dve.do(lambda e: e.tensor_tensor(gk[:], gk[:], ga[:], ALU.subtract), after=[m, mm])
            m_ga = m
            yield
            m_gate = act.do(lambda e: e.activation(gate[:], gk[:], ACT.Exp, scale=1.0 / 16.0), after=[m, *gate_r.free(b)])
            gk_r.release(b, m_gate)
            yield
            mQ = [dve.do(lambda e, c=c: e.tensor_tensor(Q[:, c, :], q[:, c, :], gate[:, c, :], ALU.mult), after=[m_gate, m_ga, S[b]["q"]]) for c in range(DC)]
            mK = [S[b]["k"]] * DC
            mT = [m_gate] * DC
            yield NEXT
            A, Aoff = A_r.buf(b), Aoff_r.buf(b)
            A_free = [*A_r.free(b), a_zero[b % 2]]
            m_A = [[], []]
            for lev, h in enumerate([0] + LEVELS):
                n = level_n[0]
                level_n[0] += 1
                pair = level_banks.buf(n)
                heads = [bank[:].rearrange("p (c i t) -> p c i t", c=DC, i=NT) for bank in pair]
                queries = q if h == 0 else Q
                hs = h if h >= 32 else P
                blocks = [(s0, s0 + h) for s0 in range(0, P, 2 * h)] if h >= 32 else [(0, 0)]
                m_sc = []

                def products(c):
                    pe.wait(*level_banks.free(n), mQ[c], mK[c], S[b]["q"])
                    for i, (s0, t0), hd in itertools.product(range(NT), blocks, range(2)):
                        r0 = hd * DK
                        m = pe.do(lambda e, r0=r0, hd=hd, i=i, s0=s0, t0=t0, hs=hs, heads=heads, queries=queries: e.matmul(
                            heads[hd][s0:s0 + hs, c, i, t0:t0 + hs],
                            k[r0:r0 + DK, c, i * P + s0:i * P + s0 + hs], queries[r0:r0 + DK, c, i * P + t0:i * P + t0 + hs],
                            start=True, stop=True), signal=(i, s0, hd) == (NT - 1, blocks[-1][0], 1), us=0.22 * hs / P)
                    m_sc.append(m)

                def double(c):
                    if not h:
                        return
                    v2 = lambda buf: buf[:, c, :].rearrange("p (n two w) -> p n two w", two=2, w=h)
                    nb = L // (2 * h)
                    at_h = L - 2 * L // h
                    T = gate[:, c, :] if h == 1 else tot[:, c, at_h:at_h + 2 * nb]
                    T = T.rearrange("p (n two) -> p n two", two=2)
                    Qv, Kv = v2(Q), v2(k)
                    mK[c] = pool.do(lambda e, h=h: e.tensor_tensor(Kv[:, :, 0], Kv[:, :, 0], T[:, :, 1:2].to_broadcast([P, nb, h]), ALU.mult), after=[m_sc[c], mT[c]], us=0.38)
                    mQ[c] = dve.do(lambda e, h=h: e.tensor_tensor(Qv[:, :, 1], Qv[:, :, 1], T[:, :, 0:1].to_broadcast([P, nb, h]), ALU.mult), after=[m_sc[c], mT[c]], us=0.2)
                    if h < 64:
                        mT[c] = dve.do(lambda e: e.tensor_tensor(tot[:, c, L - 2 * nb:L - nb], T[:, :, 0], T[:, :, 1], ALU.mult),
                                       after=[mT[c], *tot_r.free(b)], us=0.12)

                products(0)
                yield
                double(0)
                products(1)
                yield
                double(1)
                for hd in range(2):
                    if h < 32:
                        mc = dve.do(lambda e, hd=hd, heads=heads, lev=lev: e.copy_predicated(
                            A[:, hd], bcast(bcast(level_mask[:, lev, :], NT), DC), heads[hd]), after=[*m_sc, mask_ok, *A_free, *m_A[hd]], us=0.6)
                        m_A[hd] = [mc]
                    else:
                        for s0, t0 in blocks:
                            mc = act.do(lambda e, hd=hd, s0=s0, t0=t0, h=h, heads=heads: e.activation(
                                A[s0:s0 + h, hd, :, :, t0:t0 + h], heads[hd][s0:s0 + h, :, :, t0:t0 + h], ACT.Copy), after=[*m_sc, *m_A[hd]], us=0.3)
                level_banks.release(n, mc)
                yield
            n = level_n[0]
            level_n[0] += 1
            pair = level_banks.buf(n)
            pe.wait(*level_banks.free(n), *mQ, *mK)
            for c in range(DC):
                for hd in range(2):
                    r0 = hd * DK
                    m = pe.do(lambda e, hd=hd, r0=r0, c=c, pair=pair: e.matmul(pair[hd][:, c * P:(c + 1) * P], k[r0:r0 + DK, c, 0:P], Q[r0:r0 + DK, c, P:2 * P], start=True, stop=True),
                              signal=hd * c == 1)
            yield
            for hd in range(2):
                m_off = act.do(lambda e, hd=hd, pair=pair: e.activation(Aoff[:, hd], pair[hd][:, 0:DC * P].rearrange("p (c t) -> p c t", c=DC), ACT.Copy), after=[m, *Aoff_r.free(b)])
            level_banks.release(n, m_off)
            q_r.release(b, m)
            k_r.release(b, m)
            Q_r.release(b, m)
            tot_r.release(b, mQ[1], mK[1])
            gate_r.release(b, mQ[1], mK[1])
            S[b].update(A=[dve.last(), act.last()], off=m_off)

        y_r = ring("y", [P, DV], 2, phase="attention")
        yw_r = ring("yw", [P, DV], 2, phase="attention")
        yi_r = ring("yi", [P, DV], 2, BF16, phase="attention")
        yT_r = ring("yT", [P, VC, P], 2, BF16, phase="attention")
        st3_r = ring("st3", [P, 32], 2)

        def layer_norm(dst, src, st, ready):
            m = dve.do(lambda e: e.bn_stats(st[:, 0:6], src), after=[ready])
            m = dve.do(lambda e: e.bn_aggr(st[:, 6:8], st[:, 0:6]), after=[m])
            m = dve.do(lambda e: e.tensor_scalar(st[:, 7:8], st[:, 7:8], 1e-5, None, ALU.add), after=[m])
            yield
            m = yield from rsqrt(st[:, 7:8], st[:, 8:9], st[:, 9:10], m)
            yield
            return dve.do(lambda e: e.tensor_scalar(dst, src, st[:, 6:7], st[:, 9:10], ALU.subtract, ALU.mult), after=[m])

        def A3(b):
            readers = [None] * NT
            yield from abreast([A3_tile(b, i, readers) for i in range(NT)])
            for r, k in ((v_r, 0), (A_r, 0), (Aoff_r, 0), (sg_r, 1), (st_r, 2)):
                r.release(b, *[marks[k] for marks in readers])
            S[b]["x1"] = [marks[2] for marks in readers]

        def A3_tile(b, i, readers):
                st1, v, sg, A, Aoff = (r.buf(b) for r in (st_r, v_r, sg_r, A_r, Aoff_r))
                u = b * NT + i
                y, yw, yi, yT, st = (r.buf(u) for r in (y_r, yw_r, yi_r, yT_r, st3_r))
                n, bank, free = take()
                pe.wait(*free, *S[b]["A"], S[b]["off"], S[b]["v"])
                for c in range(DC):
                    for hd in range(2):
                        cols = slice((2 * c + hd) * DVH, (2 * c + hd + 1) * DVH)
                        m = pe.do(lambda e, c=c, hd=hd, i=i, cols=cols, bank=bank: e.matmul(bank[:, cols], A[:, hd, c, i, :], v[:, i, cols], start=True, stop=i == 0), signal=i == 0 and c * hd == 1)
                        if i == 1:
                            m = pe.do(lambda e, c=c, hd=hd, cols=cols, bank=bank: e.matmul(bank[:, cols], Aoff[:, hd, c, :], v[:, 0, cols], start=False, stop=True), signal=c * hd == 1)
                m_av = m
                if spare():
                    yield
                my = dve.do(lambda e, i=i, y=y, bank=bank: e.scalar_tensor_tensor(y[:], bank[:], st1[:, 30 + 2 * JQ + i:31 + 2 * JQ + i], sg[:, i, :], ALU.mult, ALU.mult),
                            after=[m, S[b]["g"], *y_r.free(u)])
                work.release(n, my)
                yield
                m_w = pool.do(lambda e, yw=yw, y=y: e.tensor_tensor(yw[:], y[:], no_w[:], ALU.mult), after=[my, loaded("attn"), *yw_r.free(u)])
                m_s = act.do(lambda e, i=i, y=y, st=st: e.activation(sg[:, i, :], y[:], ACT.Square, accum_out=st[:, 0:1]), after=[my, *st3_r.free(u)])
                y_r.release(u, m_w, m_s)
                yield
                m = dve.do(lambda e, st=st: e.tensor_scalar(st[:, 0:1], st[:, 0:1], 1.0 / DV, 1e-8, ALU.mult, ALU.add), after=[m_s])
                m_r = yield from rsqrt(st[:, 0:1], st[:, 1:2], st[:, 2:3], m)
                yield
                m = dve.do(lambda e, st=st, yw=yw: e.tensor_reduce(st[:, 3:4], yw[:], AX.X, ALU.max, apply_absolute_value=True), after=[m_w])
                m = dve.do(lambda e, st=st: e.tensor_scalar(st[:, 3:4], st[:, 3:4], st[:, 2:3], 1e-5, ALU.mult, ALU.max), after=[m, m_r])
                m = dve.do(lambda e, st=st: e.reciprocal(st[:, 4:5], st[:, 3:4]), after=[m])
                m = dve.do(lambda e, st=st: e.tensor_scalar(st[:, 4:5], st[:, 4:5], st[:, 2:3], 127.0, ALU.mult, ALU.mult), after=[m])
                dve.do(lambda e, st=st: e.tensor_scalar(st[:, 5:6], st[:, 3:4], w_unit[:, 5:6], None, ALU.mult))
                m = dve.do(lambda e, st=st, yw=yw: e.tensor_scalar(yw[:], yw[:], st[:, 4:5], ROUND, ALU.mult, ALU.add), after=[m])
                m_yi = dve.do(lambda e, yi=yi, yw=yw: e.tensor_scalar(yi[:], yw[:], ROUND, None, ALU.subtract), after=[m, *yi_r.free(u)])
                yw_r.release(u, m_yi)
                yield
                n, bank, free = take()
                tb = bank[:].bitcast(BF16)
                for c in range(VC):
                    m = pe.do(lambda e, c=c, tb=tb, yi=yi: e.transpose(tb[:, c * P:(c + 1) * P], yi[:, c * P:(c + 1) * P], ident_bf[:]), after=[m_yi, *free], signal=c == VC - 1)
                yi_r.release(u, m)
                if spare():
                    yield
                mc = act.do(lambda e, tb=tb, yT=yT: e.activation(yT[:], tb[:, 0:VC * P].rearrange("p (c t) -> p c t", c=VC), ACT.Copy), after=[m, *yT_r.free(u)])
                work.release(n, mc)
                yield
                n, bank, free = take()
                for c in range(VC):
                    m = pe.do(lambda e, c=c, bank=bank, yT=yT: e.matmul(bank[:, 0:D], yT[:, c, :], w_chunk("woT", c, 0, D), start=c == 0, stop=c == VC - 1), after=[mc, *free], signal=c == VC - 1)
                yT_r.release(u, m)
                if spare():
                    yield
                m = dve.do(lambda e, u=u, bank=bank, st=st: e.scalar_tensor_tensor(x[:, u, :], bank[:, 0:D], st[:, 5:6], x[:, u, :], ALU.mult, ALU.add), after=[m])
                work.release(n, m)
                m = yield from layer_norm(x[:, u, :], x[:, u, :], st[:, 8:20], m)
                st3_r.release(u, m)
                readers[i] = (m_av, m_s, m)

        xk = carve("cross2", [P, DC, B * S2])
        xkb_r = ring("xkb", [P, DC, XH // DC, S2], 1, phase="cross")
        xv_r = ring("xv", [S2, (XH + 1) * P], 1, phase="cross")
        x1T_r = ring("x1T", [P, DC, L], 1, phase="cross")
        xq_r = ring("xq", [P, DC, L], phase="cross")
        sc_r = ring("sc", [P, XH, S2], 2, phase="cross")
        mx_r = ring("mx", [P, XH], phase="cross")
        sum_r = ring("sum", [P, XH], phase="cross")
        pT_r = ring("pT", [S2, XH // DC, L], 1, phase="cross")
        coT_r = ring("coT", [P, DC, L], 1, phase="cross")
        stx_r = ring("stx", [P, 12])

        def context(b):
            if b:
                return
            S["xv_zero"] = dve.do(lambda e: e.memset(xv_r.buf(0), 0.0))
            m = dve.do(lambda e: e.tensor_copy(keep[:], mask_raw[:]), after=[loaded("cross")])
            m = dve.do(lambda e: e.tensor_scalar(keep[:], keep[:], 0.0, None, ALU.is_equal), after=[m])
            m = dve.do(lambda e: e.tensor_reduce(row[:], keep[:], AX.X, ALU.min), after=[m])
            m = dve.do(lambda e: e.tensor_scalar(row[:], row[:], -1.0, 1.0, ALU.mult, ALU.add), after=[m])
            for i in range(NT):
                S["mask"] = dve.do(lambda e, i=i: e.tensor_scalar(drop[:, i], bcast(keep[:, i, :], HB), -1e9, None, ALU.mult), after=[m])
            half = B * S2 // 2
            for c in range(DC):
                for hf in range(2):
                    n, bank, free = take()
                    for d in range(DC):
                        m = pe.do(lambda e, c=c, d=d, hf=hf, bank=bank: e.matmul(bank[:, 0:half], xw_T["xWkT"][:, d, c * P:(c + 1) * P], ctxT[:, d, hf * half:(hf + 1) * half],
                                                                                start=d == 0, stop=d == DC - 1), after=[loaded("cross"), *free], signal=d == DC - 1)
                    m_xk = S["xk"] = act.do(lambda e, c=c, hf=hf, bank=bank: e.activation(xk[:, c, hf * half:(hf + 1) * half], bank[:, 0:half], ACT.Identity, bias=xbk[:, c:c + 1]), after=[m, loaded("cross")])
                    work.release(n, m_xk)
                    yield

        def X(b):
            xkb, xv, x1T, xq = (r.buf(b) for r in (xkb_r, xv_r, x1T_r, xq_r))
            NHC = XH // DC
            for c in range(DC):
                m_kb = pool.do(lambda e, c=c: e.tensor_tensor(xkb[:, c], bcast(xk[:, c, b * S2:(b + 1) * S2], NHC),
                                                              head_mask[:].unsqueeze(2).to_broadcast([P, NHC, S2]), ALU.mult), after=[S["xk"], loaded("cross"), *xkb_r.free(b)])
            n, bank, free = take()
            for c in range(DC):
                for i in range(NT):
                    m = pe.do(lambda e, c=c, i=i, bank=bank: e.transpose(bank[:, c * L + i * P:c * L + (i + 1) * P], x[:, b * NT + i, c * P:(c + 1) * P], ident[:]),
                              after=[*S[b]["x1"], *free, loaded("const")], signal=c * i == 1)
            if spare():
                yield
            mc = act.do(lambda e, bank=bank: e.activation(x1T[:], bank[:].rearrange("p (c l) -> p c l", c=DC), ACT.Copy), after=[m, *x1T_r.free(b)])
            work.release(n, mc)
            yield
            n, bank, free = take()
            for c in range(DC):
                for d in range(DC):
                    m = pe.do(lambda e, c=c, d=d, bank=bank: e.matmul(bank[:, c * L:(c + 1) * L], xw_T["xWqT"][:, d, c * P:(c + 1) * P], x1T[:, d, :], start=d == 0, stop=d == DC - 1),
                              after=[mc, *free], signal=c * d == 1)
            x1T_r.release(b, m)
            m_xbo = pool.do(lambda e: e.tensor_tensor(x[:, b * NT:(b + 1) * NT, :], x[:, b * NT:(b + 1) * NT, :], bcast(xbo[:], NT), ALU.add), after=[mc])
            if spare():
                yield
            for c in range(DC):
                m_q = dve.do(lambda e, c=c, bank=bank: e.tensor_scalar(xq[:, c, :], bank[:, c * L:(c + 1) * L], xbq[:, c:c + 1], float(XD) ** -0.5, ALU.add, ALU.mult), after=[m, *xq_r.free(b)])
            work.release(n, m_q)
            yield NEXT
            n, bank, free = take()
            for d in range(DC):
                m = pe.do(lambda e, d=d, bank=bank: e.matmul(bank[0:S2, 0:D], ctxT[:, d, b * S2:(b + 1) * S2], xw_T["xWvT"][:, d, :], start=d == 0, stop=d == DC - 1), after=[loaded("cross"), *free], signal=d == DC - 1)
            yield
            own = xv[:, P - XD:(XH + 1) * P - XD].rearrange("p (h w) -> p h w", w=P)[:, :, 0:XD]
            m_xv = dve.do(lambda e, bank=bank: e.tensor_tensor(own, bank[0:S2, 0:D].rearrange("p (h d) -> p h d", h=XH), xbv[0:S2, :].rearrange("p (h d) -> p h d", h=XH), ALU.add),
                          after=[m, loaded("cross"), *xv_r.free(b), S["xv_zero"]])
            work.release(n, m_xv)
            readers = [None] * NT
            yield from abreast([X_tile(b, i, readers, m_q, m_kb) for i in range(NT)])
            for r in (xkb_r, xq_r):
                r.release(b, *[marks[0] for marks in readers])
            yield NEXT
            coT = coT_r.buf(b)
            for c in range(DC):
                pT = pT_r.buf(b * DC + c)
                for g_ in range(NHC // 4):
                    for i in range(NT):
                        sc, m_e = readers[i][1:]
                        n, bank, free = take()
                        for h in range(4):
                            m = pe.do(lambda e, h=h, c=c, g_=g_, bank=bank, sc=sc: e.transpose(bank[0:S2, h * P:(h + 1) * P], sc[:, c * NHC + 4 * g_ + h, :], ident[:]), after=[m_e, *free], signal=h == 3)
                        if c == DC - 1 and g_ == NHC // 4 - 1:
                            sc_r.release(b * NT + i, m)
                        if spare():
                            yield
                        m_p = act.do(lambda e, g_=g_, i=i, bank=bank, pT=pT: e.activation(pT[:, 4 * g_:4 * g_ + 4, i * P:(i + 1) * P], bank[0:S2, :].rearrange("p (h t) -> p h t", h=4), ACT.Copy),
                                     after=[m, *pT_r.free(b * DC + c)])
                        work.release(n, m_p)
                        yield
                n, bank, free = take()
                for h in range(NHC):
                    m = pe.do(lambda e, h=h, c=c, bank=bank, pT=pT: e.matmul(bank[:, 0:L], xv[:, (c * NHC + h + 1) * P - (h + 1) * XD:(c * NHC + h + 2) * P - (h + 1) * XD], pT[:, h, :], start=h == 0, stop=h == NHC - 1),
                              after=[m_p, m_xv, *free], signal=h == NHC - 1)
                pT_r.release(b * DC + c, m)
                if spare():
                    yield
                mc = act.do(lambda e, c=c, bank=bank: e.activation(coT[:, c, :], bank[:, 0:L], ACT.Copy), after=[m, *coT_r.free(b)])
                work.release(n, mc)
                yield
            xv_r.release(b, m)
            yield NEXT
            n, bank, free = take()
            for i in range(NT):
                for c in range(DC):
                    m = pe.do(lambda e, i=i, c=c, bank=bank: e.matmul(bank[:, i * D:(i + 1) * D], coT[:, c, i * P:(i + 1) * P], xw_T["xWoT"][:, c, :], start=c == 0, stop=c == DC - 1),
                              after=[mc, *free], signal=i == NT - 1 and c == DC - 1)
            coT_r.release(b, m)
            if spare():
                yield
            xb = x[:, b * NT:(b + 1) * NT, :]
            m = dve.do(lambda e, bank=bank: e.tensor_tensor(xb, bank[:].rearrange("p (i d) -> p i d", i=NT), xb, ALU.add), after=[m, m_xbo])
            work.release(n, m)
            out_ = [None] * NT

            def norm(i):
                st = stx_r.buf(b * NT + i)
                out_[i] = yield from layer_norm(x[:, b * NT + i, :], x[:, b * NT + i, :], st[:, 0:12], m)
                stx_r.release(b * NT + i, out_[i])

            yield from abreast([norm(i) for i in range(NT)])
            S[b]["x2"] = out_

        def X_tile(b, i, readers, m_q, m_kb):
                xkb, xq = xkb_r.buf(b), xq_r.buf(b)
                u = b * NT + i
                sc, mx, total = (r.buf(u) for r in (sc_r, mx_r, sum_r))
                for c in range(DC):
                    for g_ in range(XH // DC // HB):
                        h0 = g_ * HB
                        hh = c * (XH // DC) + h0
                        n, bank, free = take()
                        m = pe.do(lambda e, c=c, i=i, h0=h0, bank=bank: e.matmul(bank[:, 0:HB * S2], xq[:, c, i * P:(i + 1) * P], xkb[:, c, h0:h0 + HB, :].rearrange("p h k -> p (h k)"), start=True, stop=True),
                                  after=[m_q, m_kb, *free])
                        if spare():
                            yield
                        m_k = dve.do(lambda e, i=i, hh=hh, bank=bank, sc=sc: e.scalar_tensor_tensor(
                            sc[:, hh:hh + HB, :].rearrange("p h k -> p (h k)"), bank[:, 0:HB * S2], row[:, i:i + 1], drop[:, i].rearrange("p h k -> p (h k)"), ALU.mult, ALU.add),
                                     after=[m, S["mask"], *sc_r.free(u)])
                        work.release(n, m_k)
                        yield
                m_scores = m
                yield
                m = m_k
                to_all = lambda v: v[:].unsqueeze(2).to_broadcast([P, XH, S2])
                m = dve.do(lambda e: e.tensor_reduce(mx[:], sc[:], AX.X, ALU.max), after=[m, *mx_r.free(u)], us=1.35)
                yield
                lane, us = (dve, 1.3) if b == B - 1 else (pool, 2.2)
                m = lane.do(lambda e: e.tensor_tensor(sc[:], sc[:], to_all(mx), ALU.subtract), after=[m], us=us)
                mx_r.release(u, m)
                yield
                m = act.do(lambda e: e.activation(sc[:], sc[:], ACT.Exp), after=[m], us=1.2)
                yield
                m = dve.do(lambda e: e.tensor_reduce(total[:], sc[:], AX.X, ALU.add), after=[m, *sum_r.free(u)], us=1.35)
                m = dve.do(lambda e: e.reciprocal(total[:], total[:]), after=[m], us=0.1)
                yield
                m = lane.do(lambda e: e.tensor_tensor(sc[:], sc[:], to_all(total), ALU.mult), after=[m], us=us)
                sum_r.release(u, m)
                yield
                readers[i] = (m_scores, sc, m)

        def weave(count, stages):
            done = {part: 0 for _, parts in stages for part in parts}
            end = dict.fromkeys(done, 0.0)
            live, waiting = [], []
            for stage, parts in stages:
                waiting += [[0.0, stage(b), b, list(parts.items())] for b in range(count)]
            while live or waiting:
                for it in list(waiting):
                    (part, needs), b = it[3][0], it[2]
                    if done[part] == b and part not in [v[3][0][0] for v in live] and all(done[n] >= c for n, c in needs(b).items()):
                        it[0] = max([it[0], end[part]] + [end[n] for n in needs(b)])
                        waiting.remove(it)
                        live.append(it)
                it = min(live, key=lambda v: v[0])
                said = next(it[1], "end")
                if said is None:
                    it[0] = Lane.latest
                    continue
                part = it[3].pop(0)[0]
                end[part] = it[0]
                done[part] += 1
                live.remove(it)
                if said == NEXT:
                    waiting.append(it)
                assert bool(it[3]) == (said == NEXT)

        gateT = sb("gateT", [P, DC, E])
        gate_b = sb("gate_b", [P, E])
        load(gateT[:], t["gateT"].rearrange("(c p) e -> p c e", p=P), "router")
        load(gate_b[:], t["gate_bias"].partition_broadcast(P), "router")
        lg = sb("lg", [P, TILES, E])
        lg_max = sb("lg_max", [P, TILES])
        x2T_r = ring("x2T", [P, DC, L], 1)

        def Rt(b):
            x2T = x2T_r.buf(b)
            n, bank, free = take()
            for c in range(DC):
                for i in range(NT):
                    m = pe.do(lambda e, c=c, i=i, b=b, bank=bank: e.transpose(bank[:, c * L + i * P:c * L + (i + 1) * P], x[:, b * NT + i, c * P:(c + 1) * P], ident[:]),
                              after=[*S[b]["x2"], *free], signal=c * i == 1)
            if spare():
                yield
            bv = bank[:].rearrange("p (c l) -> p c l", c=DC)
            mc = act.do(lambda e, bv=bv, x2T=x2T: e.activation(x2T[:], bv, ACT.Copy), after=[m, *x2T_r.free(b)])
            work.release(n, mc)
            yield
            n, bank, free = take()
            for i in range(NT):
                for d in range(DC):
                    m = pe.do(lambda e, i=i, d=d, x2T=x2T, bank=bank: e.matmul(bank[:, i * E:(i + 1) * E], x2T[:, d, i * P:(i + 1) * P], gateT[:, d, :], start=d == 0, stop=d == DC - 1),
                              after=[mc, loaded("router"), *free], signal=i * d == 1)
            x2T_r.release(b, m)
            if spare():
                yield
            scores = bank[:, 0:NT * E].rearrange("p (i n) -> p i n", i=NT)
            lgb, mxb = lg[:, b * NT:(b + 1) * NT, :], lg_max[:, b * NT:(b + 1) * NT]
            m = dve.do(lambda e: e.tensor_reduce(mxb, scores, AX.X, ALU.max), after=[m])
            m = dve.do(lambda e: e.tensor_tensor(lgb, scores, mxb.unsqueeze(2).to_broadcast([P, NT, E]), ALU.subtract), after=[m])
            work.release(n, m)
            S["router"] = (act.do(lambda e: e.activation(lgb, lgb, ACT.Exp), after=[m]),)

        CW = DC * F
        WX = 3 * 2 * CW
        w_area = carve("weights", [P, (3 * (E + 1) + 2) * CW])
        w_bf = w_area.bitcast(BF16)
        HI, LO = 0, CW

        def w_part(number, k, part, a, n):
            return w_bf[:, bass.ds(number * WX + k * 2 * CW + part + a, n)]

        split = {}

        def W(b):
            if b:
                return
            early_over = [lane.last() for lane in (pe, act, dve, pool)]
            sp.wait(*early_over)
            sources = [t["sw1T"], t["sw3T"], t["sw2T"]] + [t[w][ex] for ex in range(E) for w in ("w1T", "w3T", "w2T")]
            raw_w = [w_area[:, (q + 2) * CW:(q + 3) * CW] for q in range(len(sources))]
            for q, src in enumerate(sources):
                load(raw_w[q].rearrange("p (c n) -> p c n", c=src.shape[0] // P), src.rearrange("(c p) n -> p c n", p=P), f"weights{q}")
            done = []
            for q in range(len(sources)):
                hi, lo = (w_bf[:, q * 2 * CW + part:q * 2 * CW + part + CW] for part in (HI, LO))
                m = act.do(lambda e, q=q, hi=hi: e.activation(hi, raw_w[q], ACT.Copy), after=[loaded(f"weights{q}"), *early_over, *done[max(0, q - 2):q - 1]])
                m = (pool if q > 6 else dve).do(lambda e, q=q, hi=hi, lo=lo: e.tensor_tensor(lo, raw_w[q], hi, ALU.subtract), after=[m])
                done.append(m)
                split.setdefault(q // 3, []).append(m)
                yield

        lower = carve("experts", [P, E, E])
        cm = carve("experts", [P, TILES, E, E])
        bi, first, second, sel, incl, incl2, pos = (carve("experts", [P, TILES, E]) for _ in range(7))
        rt = carve("experts", [P, TILES])
        nt8, nt8b, n8 = (carve("experts", [P, E]) for _ in range(3))
        before = carve("experts", [P, P])
        tile_no = carve("experts", [P, NTT])
        tile_cmp = carve("experts", [P, NTT, E])
        tile_e = carve("experts", [P, NTT])
        tile_ex = sb("tile_ex", [P, NTT], I32)
        posf = [carve("experts", [P, TILES]) for _ in range(2)]
        slot = [sb(f"slot{k}", [P, TILES], I32) for k in range(2)]
        weight = [sb(f"weight{k}", [P, TILES]) for k in range(2)]

        def experts_start(b):
            if b:
                return
            late_over = [lane.last() for lane in (pe, act, dve, pool)]
            for lane in (act, dve, pool, sp):
                lane.wait(*late_over)
            load(lower, t["lower"].rearrange("a b -> (a b)").partition_broadcast(P).rearrange("p (a b) -> p a b", a=E), "routing")
            load(before, t["before"], "routing")
            load(tile_no, t["tile_no"].partition_broadcast(P), "routing")
            S["level banks over"] = level_banks.marks[0] + level_banks.marks[1]
            act.do(lambda e: e.preload_act_table_set("silu_and_others"), signal=False)
            yield

        def running_sum(a, b, n, ready):
            m, d = ready, 1
            while d < n:
                dve.do(lambda e, a=a, b=b, d=d: e.tensor_copy(b[:, 0:d], a[:, 0:d]), after=[m])
                m = dve.do(lambda e, a=a, b=b, d=d: e.tensor_tensor(b[:, d:], a[:, d:], a[:, 0:n - d], ALU.add), after=[m])
                a, b, d = b, a, 2 * d
            return a, m

        scattered = sem("scattered")

        def route(b):
            if b:
                return
            rb = rt.unsqueeze(2).to_broadcast([P, TILES, E])
            m = dve.do(lambda e: e.tensor_reduce(rt, lg[:], AX.X, ALU.add), after=S["router"])
            yield
            m = dve.do(lambda e: e.reciprocal(rt, rt), after=[m])
            yield
            m = dve.do(lambda e: e.tensor_tensor(lg[:], lg[:], rb, ALU.mult), after=[m])
            yield
            m = dve.do(lambda e: e.tensor_tensor(bi, lg[:], bcast(gate_b[:], TILES), ALU.add), after=[m, loaded("router")])
            yield
            mine = bi.unsqueeze(3).to_broadcast([P, TILES, E, E])
            other = bi.unsqueeze(2).to_broadcast([P, TILES, E, E])
            m = dve.do(lambda e: e.tensor_tensor(cm, other, mine, ALU.is_gt), after=[m])
            yield
            m = dve.do(lambda e: e.tensor_reduce(incl, cm, AX.X, ALU.add), after=[m])
            yield
            m = dve.do(lambda e: e.tensor_tensor(cm, other, mine, ALU.is_equal), after=[m])
            yield
            m = dve.do(lambda e: e.tensor_tensor(cm, cm, bcast(lower, TILES), ALU.mult), after=[m, loaded("routing")])
            yield
            m = dve.do(lambda e: e.tensor_reduce(pos, cm, AX.X, ALU.add), after=[m])
            yield
            m = dve.do(lambda e: e.tensor_tensor(pos, pos, incl, ALU.add), after=[m])
            yield
            dve.do(lambda e: e.tensor_scalar(first, pos, 0.0, None, ALU.is_equal), after=[m])
            dve.do(lambda e: e.tensor_scalar(second, pos, 1.0, None, ALU.is_equal))
            m_sel = dve.do(lambda e: e.tensor_scalar(sel, pos, 1.5, None, ALU.is_lt))
            flat = lambda v: v.rearrange("p i n -> p (i n)")
            n, bank, free = take()
            pe.do(lambda e, bank=bank: e.matmul(bank[:, 0:P], before, flat(sel), start=True, stop=True), after=[m_sel, *free, loaded("routing")], signal=False)
            m_cnt = pe.do(lambda e, bank=bank: e.matmul(bank[:, P:2 * P], ones[:], flat(sel), start=True, stop=True))
            pre, tot_t = bank[:, 0:P].rearrange("p (i n) -> p i n", i=TILES), bank[:, P:2 * P].rearrange("p (i n) -> p i n", i=TILES)

            m = dve.do(lambda e: e.tensor_copy(incl, tot_t), after=[m_cnt])
            yield
            sums, m = running_sum(incl, incl2, TILES, m)
            counts = sums[:, TILES - 1, :]
            m1 = dve.do(lambda e: e.tensor_scalar(n8, counts, 1.0 / P, (P - 1.0) / P - 0.498, ALU.mult, ALU.add), after=[m])
            yield
            m1 = dve.do(lambda e: e.tensor_scalar(n8, n8, ROUND, None, ALU.add), after=[m1])
            yield
            m1 = dve.do(lambda e: e.tensor_scalar(n8, n8, ROUND, None, ALU.subtract), after=[m1])
            yield
            m1 = dve.do(lambda e: e.tensor_copy(nt8, n8), after=[m1])
            yield
            ends, m1 = running_sum(nt8, nt8b, E, m1)
            m2 = dve.do(lambda e: e.tensor_tensor(tile_cmp, tile_no.unsqueeze(2).to_broadcast([P, NTT, E]), bcast(ends, NTT), ALU.is_ge), after=[m1, loaded("routing")])
            yield
            m2 = dve.do(lambda e: e.tensor_reduce(tile_e, tile_cmp, AX.X, ALU.add), after=[m2])
            yield
            m2 = dve.do(lambda e: e.tensor_scalar(tile_e, tile_e, E - 1.0, None, ALU.min), after=[m2])
            yield
            m_ex = dve.do(lambda e: e.tensor_copy(tile_ex[:], tile_e), after=[m2])
            m = dve.do(lambda e: e.tensor_tensor(n8, ends, n8, ALU.subtract), after=[m1])
            yield
            m = dve.do(lambda e: e.tensor_scalar(n8, n8, float(P), None, ALU.mult), after=[m])
            yield
            m = dve.do(lambda e: e.tensor_tensor(pos, sums, tot_t, ALU.subtract), after=[m])
            yield
            m = dve.do(lambda e: e.tensor_tensor(pos, pos, pre, ALU.add), after=[m])
            yield
            work.release(n, m)
            m = dve.do(lambda e: e.tensor_tensor(pos, pos, bcast(n8, TILES), ALU.add), after=[m])
            yield
            for k, onehot in enumerate((first, second)):
                cmk = cm[:, :, k, :]
                ma = dve.do(lambda e, o=onehot, c=cmk: e.tensor_tensor(c, pos, o, ALU.mult), after=[m])
                ma = dve.do(lambda e, k=k, c=cmk: e.tensor_reduce(posf[k], c, AX.X, ALU.add), after=[ma])
                m_slot = dve.do(lambda e, k=k: e.tensor_copy(slot[k][:], posf[k]), after=[ma])
            m_wgt = []
            for k, onehot in enumerate((first, second)):
                cmk = cm[:, :, 2 + k, :]
                ma = dve.do(lambda e, o=onehot, c=cmk: e.tensor_tensor(c, lg[:], o, ALU.mult), after=[m])
                m_wgt = dve.do(lambda e, k=k, c=cmk: e.tensor_reduce(weight[k][:], c, AX.X, ALU.add), after=[ma])
            for i in range(TILES):
                for k in range(2):
                    pool.dma(lambda e, i=i, k=k: e.indirect_dma_start(xs, bass.IndirectOffsetOnAxis(slot[k][:, i:i + 1], 0), x[:, i, :], None), scattered,
                             after=[m_slot, (cleared, 16), *S[i // NT]["x2"]])
            S["scattered"] = m_ex, m_wgt

        CH = 256
        xch_r = ring("xch", [P, DC, CH], 2, BF16, phase="experts")
        xcl_r = ring("xcl", [P, DC, CH], 2, BF16, phase="experts")
        acc = carve("experts", [P, TILES, D])
        sil_r = ring("sil", [P, F], phase="experts")
        h_r = ring("h", [P, F], phase="experts")
        hh_r = ring("hh", [P, FC, CH], 2, BF16, phase="experts")
        hl_r = ring("hl", [P, FC, CH], 2, BF16, phase="experts")
        hb = Ring(banks[0:4])

        def two_parts(n, bank, hi, lo, ready, hi_free, lo_free):
            bv = bank[:, 0:DC * hi.shape[2]].rearrange("p (c t) -> p c t", c=DC)
            mh = act.do(lambda e: e.activation(hi, bv, ACT.Copy), after=[ready, *hi_free])
            ml = dve.do(lambda e: e.tensor_tensor(lo, bv, hi, ALU.subtract), after=[mh, *lo_free])
            work.release(n, ml)
            return ml

        x_parts = {}

        def shared_x(job):
            n, bank, free = take()
            for c in range(DC):
                for i in range(CH // P):
                    m = pe.do(lambda e, c=c, i=i: e.transpose(bank[:, c * CH + i * P:c * CH + (i + 1) * P], x[:, job * (CH // P) + i, c * P:(c + 1) * P], ident[:]),
                              after=[*free], signal=c == DC - 1 and i == CH // P - 1)
            x_parts[job] = two_parts(n, bank, xch_r.buf(job), xcl_r.buf(job), m, xch_r.free(job), xcl_r.free(job))

        def shared_h(job, f):
            fj = job * FC + f
            sil, h, hh, hl = sil_r.buf(fj), h_r.buf(fj), hh_r.buf(job), hl_r.buf(job)
            got = []
            for k in range(2):
                n = 2 * fj + k
                bank = hb.buf(n)
                pe.wait(*hb.free(n), *S["level banks over"], *split[0], x_parts[job])
                for pi, (part, xx) in enumerate([(HI, xch_r.buf(job)), (HI, xcl_r.buf(job)), (LO, xch_r.buf(job))]):
                    for d in range(DC):
                        m = pe.do(lambda e, bank=bank, part=part, xx=xx, d=d, k=k, pi=pi: e.matmul(
                            bank[:, 0:CH], w_part(0, k, part, d * F + f * P, P), xx[:, d, :], start=pi == 0 and d == 0, stop=pi == 2 and d == DC - 1),
                            signal=pi == 2 and d == DC - 1)
                got.append((n, bank, m))
            sil, h = sil[:, 0:CH], h[:, 0:CH]
            m = act.do(lambda e, bank=got[0][1]: e.activation(sil, bank[:, 0:CH], ACT.Silu), after=[got[0][2], *sil_r.free(fj)])
            hb.release(got[0][0], m)
            m = dve.do(lambda e, bank=got[1][1]: e.tensor_tensor(h, sil, bank[:, 0:CH], ALU.mult), after=[m, got[1][2], *h_r.free(fj)])
            hb.release(got[1][0], m)
            sil_r.release(fj, m)
            m_h = act.do(lambda e: e.activation(hh[:, f, :], h, ACT.Copy), after=[m, *hh_r.free(job)])
            m_l = dve.do(lambda e: e.tensor_tensor(hl[:, f, :], h, hh[:, f, :], ALU.subtract), after=[m_h, *hl_r.free(job)])
            h_r.release(fj, m_l)
            if f == FC - 1:
                xch_r.release(job, got[1][2])
                xcl_r.release(job, got[1][2])
            return m_l

        def shared_y(job, ready):
            hh, hl = hh_r.buf(job), hl_r.buf(job)
            for i in range(CH // P):
                u = job * (CH // P) + i
                n, bank, free = take()
                for pi, (hx, w) in enumerate([(hh, HI), (hh, LO), (hl, HI)]):
                    for f in range(FC):
                        m = pe.do(lambda e, bank=bank, hx=hx, w=w, f=f, i=i, pi=pi: e.matmul(bank[:, 0:D], hx[:, f, i * P:(i + 1) * P], w_part(0, 2, w, f * D, D),
                                  start=pi == 0 and f == 0, stop=pi == 2 and f == FC - 1), after=[ready, *free], signal=pi == 2 and f == FC - 1)
                my = dve.do(lambda e, bank=bank, u=u: e.tensor_tensor(acc[:, u, :], bank[:, 0:D], x[:, u, :], ALU.add), after=[m])
                work.release(n, my)
            hh_r.release(job, m)
            hl_r.release(job, m)
            return my

        JOBS = TILES * P // CH
        def shared(b):
            if b:
                return
            ready = None
            shared_x(0)
            for job in range(JOBS):
                if job + 1 < JOBS:
                    shared_x(job + 1)
                for f in range(FC):
                    m = shared_h(job, f)
                    yield
                    if f == 0 and job:
                        shared_y(job - 1, ready)
                        yield
                ready = m
            S["acc"] = shared_y(JOBS - 1, ready)

        weave(B, [
            (Rt, {"router scores": lambda b: {"cross out": b + 1}}),
            (X, {"cross in": lambda b: {"gated out": b + 1, "cross scores": b, "context": 1},
                 "cross scores": lambda b: {"cross values": b},
                 "cross values": lambda b: {"cross out": b},
                 "cross out": lambda b: {}}),
            (A3, {"gated out": lambda b: {"gated scores": b + 1}}),
            (A2, {"gates": lambda b: {"project": b + 1, "gated scores": b - 1},
                  "gated scores": lambda b: {"gated out": b - 1}}),
            (ternary, {"ternary": lambda b: {}}),
            (context, {"context": lambda b: {"ternary": 1}}),
            (A1, {"quantise": lambda b: {"turn": b, "gated out": b - 2},
                  "turn": lambda b: {"project": b},
                  "project": lambda b: {"gated scores": b - 1, "ternary": 1}}),
            (W, {"weights": lambda b: {"gated out": B}}),
            (experts_start, {"experts start": lambda b: {"router scores": B}}),
            (route, {"route": lambda b: {"experts start": 1}}),
            (shared, {"shared": lambda b: {"experts start": 1}}),
        ])
        m_ex, m_wgt = S["scattered"]
        m_acc = S["acc"]

        XTN = 4
        xt_r = ring("xt", [P, D], XTN, phase="experts")
        xt_sem = [sem(f"xt{k}") for k in range(XTN)]
        xth_r = ring("xth", [P, DC, P], 2, BF16, phase="experts")
        xtl_r = ring("xtl", [P, DC, P], 2, BF16, phase="experts")
        th_r = ring("th", [P, F], 2, BF16, phase="experts")
        tl_r = ring("tl", [P, F], 2, BF16, phase="experts")
        hT_r = ring("hT", [P, 2, FC, P], 2, BF16, phase="experts")
        yt_r = ring("yt", [P, D], 2, phase="experts")
        yt_sem = [sem(f"yt{k}") for k in range(2)]
        marks = {}

        def tile_load(k):
            sp.dma(lambda e: e.dma_start(xt_r.buf(k), xs[k * P:(k + 1) * P, :]), xt_sem[k % XTN], after=[(scattered, 16 * 2 * TILES), *xt_r.free(k)])

        def tile_x(k):
            xt, xh, xl = xt_r.buf(k), xth_r.buf(k), xtl_r.buf(k)
            n, bank, free = take()
            for c in range(DC):
                m = pe.do(lambda e, c=c: e.transpose(bank[:, c * P:(c + 1) * P], xt[:, c * P:(c + 1) * P], ident[:]), after=[(xt_sem[k % XTN], 16 * (k // XTN + 1)), *free], signal=c == DC - 1)
            xt_r.release(k, m)
            ml = two_parts(n, bank, xh, xl, m, xth_r.free(k), xtl_r.free(k))
            marks[k] = {"x": ml}

        def tile_h(k):
            xh, xl, th, tl, sil, h = (*(r.buf(k) for r in (xth_r, xtl_r, th_r, tl_r)), *(r.buf(JOBS * FC + k) for r in (sil_r, h_r)))
            got = []
            pe.wait(m_ex, marks[k]["x"], *[m for p in split.values() for m in p])
            value = {}
            pe.queue.append(lambda e, k=k: value.__setitem__("e", e.value_load(tile_ex[0:1, k:k + 1], min_val=0, max_val=E - 1)))
            marks[k]["e"] = value
            for q in range(2):
                n = 2 * (JOBS * FC + k) + q
                bank = hb.buf(n)
                for pi, (xx, w) in enumerate([(xh, HI), (xh, LO), (xl, HI)]):
                    for d in range(DC):
                        m = pe.do(lambda e, bank=bank, w=w, xx=xx, d=d, q=q, pi=pi: e.matmul(
                            bank[:], xx[:, d, :], w_part(value["e"] + 1, q, w, d * F, F), start=pi == 0 and d == 0, stop=pi == 2 and d == DC - 1),
                            after=[*hb.free(n)], signal=pi == 2 and d == DC - 1)
                got.append((n, bank, m))
            xth_r.release(k, m)
            xtl_r.release(k, m)
            m = act.do(lambda e, bank=got[0][1]: e.activation(sil, bank[:], ACT.Silu), after=[got[0][2], *sil_r.free(JOBS * FC + k)])
            hb.release(got[0][0], m)
            m = dve.do(lambda e, bank=got[1][1]: e.tensor_tensor(h, sil, bank[:], ALU.mult), after=[m, got[1][2], *h_r.free(JOBS * FC + k)])
            hb.release(got[1][0], m)
            sil_r.release(JOBS * FC + k, m)
            m_h = act.do(lambda e: e.activation(th, h, ACT.Copy), after=[m, *th_r.free(k)])
            m_l = pool.do(lambda e: e.tensor_tensor(tl, h, th, ALU.subtract), after=[m_h, *tl_r.free(k)])
            h_r.release(JOBS * FC + k, m_l)
            marks[k]["h"] = m_l

        def tile_turn(k):
            th, tl, hT = th_r.buf(k), tl_r.buf(k), hT_r.buf(k)
            n, bank, free = take()
            tb = bank[:].bitcast(BF16)
            for q, part in enumerate((th, tl)):
                for f in range(FC):
                    m = pe.do(lambda e, q=q, f=f, part=part: e.transpose(tb[:, (q * FC + f) * P:(q * FC + f + 1) * P], part[:, f * P:(f + 1) * P], ident_bf[:]),
                              after=[marks[k]["h"], *free], signal=q * FC + f == 2 * FC - 1)
            th_r.release(k, m)
            tl_r.release(k, m)
            tv = tb.rearrange("p (q f t) -> p q f t", q=2, f=FC)
            m = dve.do(lambda e: e.tensor_copy(hT, tv), after=[m, *hT_r.free(k)])
            work.release(n, m)
            marks[k]["hT"] = m

        def tile_y(k):
            hT, yt, value = hT_r.buf(k), yt_r.buf(k), marks[k]["e"]
            n, bank, free = take()
            for pi, (q, w) in enumerate([(0, HI), (0, LO), (1, HI)]):
                for f in range(FC):
                    m = pe.do(lambda e, q=q, w=w, f=f, pi=pi: e.matmul(bank[:, 0:D], hT[:, q, f, :], w_part(value["e"] + 1, 2, w, f * D, D),
                              start=pi == 0 and f == 0, stop=pi == 2 and f == FC - 1), after=[marks[k]["hT"], *free], signal=pi == 2 and f == FC - 1)
            hT_r.release(k, m)
            m = act.do(lambda e: e.activation(yt, bank[:, 0:D], ACT.Copy), after=[m, *yt_r.free(k)])
            work.release(n, m)
            sp.dma(lambda e: e.dma_start(ys[k * P:(k + 1) * P, :], yt), yt_sem[k % 2], after=[m])
            yt_r.release(k, (yt_sem[k % 2], 16 * (k // 2 + 1)))

        for k in range(XTN - 1):
            tile_load(k)
        for k in range(NTT + 3):
            if k + XTN - 1 < NTT:
                tile_load(k + XTN - 1)
            if k < NTT:
                tile_x(k)
            if 0 <= k - 1 < NTT:
                tile_h(k - 1)
            if 0 <= k - 2 < NTT:
                tile_turn(k - 2)
            if 0 <= k - 3 < NTT:
                tile_y(k - 3)

        act.do(lambda e: e.preload_act_table_set("natural_log_exp_and_others"), signal=False)
        YAN = 8
        ya_r = ring("ya", [P, 2, D], YAN, phase="final")
        ya_sem = [sem(f"ya{k}") for k in range(YAN)]
        pool.wait(pe.last())
        y_stored = [(yt_sem[k], 16 * ((NTT - k + 1) // 2)) for k in range(2)]
        stores = sem("stores")
        stf_r = ring("stf", [P, 12], 4)

        def finish(u):
            ya, st = ya_r.buf(u), stf_r.buf(u)
            for k in range(2):
                pool.dma(lambda e, k=k: e.indirect_dma_start(ya[:, k, :], None, ys, bass.IndirectOffsetOnAxis(slot[k][:, u:u + 1], 0)), ya_sem[u % YAN],
                         after=[*y_stored, *ya_r.free(u)])
            yield
            m = dve.do(lambda e: e.scalar_tensor_tensor(acc[:, u, :], ya[:, 0, :], weight[0][:, u:u + 1], acc[:, u, :], ALU.mult, ALU.add), after=[(ya_sem[u % YAN], 32 * (u // YAN + 1)), m_acc])
            m = dve.do(lambda e: e.scalar_tensor_tensor(acc[:, u, :], ya[:, 1, :], weight[1][:, u:u + 1], acc[:, u, :], ALU.mult, ALU.add), after=[m])
            ya_r.release(u, m)
            yield
            m = yield from layer_norm(acc[:, u, :], acc[:, u, :], st[:], m)
            sp.dma(lambda e: e.dma_start(out[u * P:(u + 1) * P, :], acc[:, u, :]), stores, after=[m])
            stf_r.release(u, m)

        for u in range(0, TILES, 4):
            for _ in abreast([finish(u + v) for v in range(4)]):
                pass
        sp.wait((stores, 16 * TILES))
        block = ctx.enter_context(nc.Block())
        for name, lane in (("tensor", pe), ("scalar", act), ("vector", dve), ("gpsimd", pool), ("sync", sp)):
            def emit(e, lane=lane):
                for make in lane.queue:
                    make(e)
            {"tensor": block.tensor, "scalar": block.scalar, "vector": block.vector, "gpsimd": block.gpsimd, "sync": block.sync}[name](emit)


def kernel(**inputs):
    import concourse.bacc as bacc
    from concourse import mybir as mb
    from concourse.bass_utils import run_bass_kernel_spmd

    a = {k: np.asarray(v) for k, v in inputs.items()}
    B, L, D = a["x"].shape
    DV = a["L0_attn_wv"].shape[0]
    R = a["L0_attn_wgk1"].shape[0]
    HEADS = 4
    f32 = np.float32
    T = lambda w: np.swapaxes(w, -1, -2)
    columns = lambda v: v.reshape(-1, P).T
    s_, t_ = np.arange(P)[:, None], np.arange(P)[None, :]
    masks = [s_ == t_] + [(s_ // (2 * h) == t_ // (2 * h)) & (s_ % (2 * h) < h) & (t_ % (2 * h) >= h) for h in LEVELS if h < 32]
    n_heads = 16
    pi = np.arange(P)
    laid = {
        "x": a["x"], "ctxT": a["ctx_1024"].reshape(-1, D).T, "mask": a["mask_1x1xSxS2_if1"],
        "wqT": T(a["L0_attn_wq"]), "wkT": T(a["L0_attn_wk"]), "wvT": T(a["L0_attn_wv"]), "wgT": T(a["L0_attn_wg"]),
        "wgk1T": T(a["L0_attn_wgk1"]), "wgk2T": T(a["L0_attn_wgk2"]), "woT": T(a["L0_attn_wo"]),
        "norm_w": np.stack([a["L0_attn_n" + n] for n in ("q", "k", "v", "gk1", "g")]),
        "no_w": a["L0_attn_no"], "ngk2": a["L0_attn_ngk2"], "bgk2": columns(a["L0_attn_bgk2"]),
        "xWqT": T(a["L0_xattn_W_q"]), "xWkT": T(a["L0_xattn_W_k"]), "xWvT": T(a["L0_xattn_W_v"]), "xWoT": T(a["L0_xattn_W_o"]),
        "xbq": columns(a["L0_xattn_b_q"]), "xbk": columns(a["L0_xattn_b_k"]), "xbv": a["L0_xattn_b_v"], "xbo": a["L0_xattn_b_o"],
        "gateT": T(a["L0_ffn_gate_w"]), "gate_bias": a["L0_ffn_gate_bias"],
        "w1T": T(a["L0_ffn_w1"]), "w2T": T(a["L0_ffn_w2"]), "w3T": T(a["L0_ffn_w3"]),
        "sw1T": T(a["L0_ffn_sw1"]), "sw2T": T(a["L0_ffn_sw2"]), "sw3T": T(a["L0_ffn_sw3"]),
        "ident": np.eye(P, dtype=f32),
        "level_mask": np.stack(masks, 1).astype(np.int32),
        "inv_count": np.array([1.0 / n for n in (D * D, D * D, D * DV, D * R, D * DV, D * DV, D * R)], f32),
        "unit": np.array([(D // HEADS) ** -0.5 / 127.0] + [1.0 / 127.0] * 6, f32),
        "head_mask": (pi[:, None] // (D // n_heads) == np.arange(n_heads // (D // P))[None, :]).astype(f32),
        "before": (s_ < t_).astype(f32),
        "tile_no": np.arange((2 * B * L + (P - 1) * 8) // P).astype(f32),
        "lower": (np.arange(8)[None, :] < np.arange(8)[:, None]).astype(f32),
    }
    nc = bacc.Bacc("TRN2", target_bir_lowering=False, num_devices=1)
    arrays, handles = {}, {}
    for name, v in laid.items():
        v = np.ascontiguousarray(v)
        arrays[f"in_{name}"] = v
        handles[name] = nc.dram_tensor(f"in_{name}", v.shape, mb.dt.from_np(v.dtype), kind="ExternalInput").ap()
    out = nc.dram_tensor("out", (B * L, D), mb.dt.float32, kind="ExternalOutput").ap()
    decoder_layer(nc, handles, out)
    r = run_bass_kernel_spmd(nc, [arrays], core_ids=[0])
    return r.results[0]["out"].reshape(B, L, D)
```
